# Optimizing a Trainium2 kernel written in Bass

```python
import numpy as np
import jax
import jax.numpy as jnp

def _softmax(x, axis=-1):
    return jax.nn.softmax(x, axis=axis)

def _gelu(x):
    return jax.nn.gelu(x, approximate=True)

def _silu(x):
    return jax.nn.silu(x)

def _sigmoid(x):
    return jax.nn.sigmoid(x)

def _layernorm(x, axis=-1, eps=1e-05):
    m = jnp.mean(x, axis=axis, keepdims=True)
    v = jnp.var(x, axis=axis, keepdims=True)
    return (x - m) / jnp.sqrt(v + eps)

def _scatter_add(tgt, idx, src, axis=0):
    return tgt.at[idx].add(src)

def _segment_sum(src, seg, n):
    return jax.ops.segment_sum(src, seg, n)
kernel_name = 'mk_prb_d2_jaxref_r8_35783f'

def setup_inputs(seed: int=0):
    np.random.seed(seed)
    _w = jnp.asarray

    def _L0_attn_setup():
        import jax, jax.numpy as jnp
        import numpy as np
        D = 256
        H = 8
        QK = D // 2
        FF = 1024
        CAP = 15.0
        EPS = 1e-06

        def _rmsnorm(x, w, eps=EPS):
            xf = x.astype(jnp.float32)
            var = jnp.mean(xf * xf, axis=-1, keepdims=True)
            return (w * xf * jax.lax.rsqrt(var + eps)).astype(x.dtype)

        def _soft_cap(x, cap=CAP):
            return cap * jnp.tanh(x / cap)

        def _mlstm_parallel(q, k, v, i_pre, f_pre):
            B, Hn, S, dqk = q.shape
            logfg = jax.nn.log_sigmoid(f_pre)
            Fcum = jnp.cumsum(logfg, axis=-1)
            Dmat = Fcum[..., :, None] - Fcum[..., None, :] + i_pre[..., None, :]
            causal = jnp.tril(jnp.ones((S, S), dtype=bool))
            Dmat = jnp.where(causal, Dmat, -jnp.inf)
            m = jnp.max(Dmat, axis=-1, keepdims=True)
            Smat = jnp.exp(Dmat - m)
            qk = jnp.einsum('bhsd,bhtd->bhst', q, k) / jnp.sqrt(jnp.float32(dqk))
            C = qk * Smat
            n = jnp.maximum(jnp.abs(jnp.sum(C, axis=-1, keepdims=True)), jnp.exp(-m))
            h = jnp.einsum('bhst,bhtd->bhsd', C / n, v)
            return h
        key = jax.random.key(seed)
        ks = jax.random.split(key, 17)
        sc = 0.02
        inp = {'x': jax.random.normal(ks[0], (2, 256, D), jnp.float32), 'norm1_w': jnp.ones((D,), jnp.float32), 'wq': jax.random.normal(ks[1], (D, QK), jnp.float32) * sc, 'wk': jax.random.normal(ks[2], (D, QK), jnp.float32) * sc, 'wv': jax.random.normal(ks[3], (D, D), jnp.float32) * sc, 'w_ig': jax.random.normal(ks[4], (D, H), jnp.float32) * sc, 'b_ig': jnp.zeros((H,), jnp.float32), 'w_fg': jax.random.normal(ks[5], (D, H), jnp.float32) * sc, 'b_fg': jnp.linspace(3.0, 6.0, H).astype(jnp.float32), 'w_og': jax.random.normal(ks[6], (D, D), jnp.float32) * sc, 'mh_w': jnp.ones((D,), jnp.float32), 'w_out': jax.random.normal(ks[7], (D, D), jnp.float32) * sc, 'norm2_w': jnp.ones((D,), jnp.float32), 'w_gate': jax.random.normal(ks[8], (D, FF), jnp.float32) * sc, 'w_up': jax.random.normal(ks[9], (D, FF), jnp.float32) * sc, 'w_down': jax.random.normal(ks[10], (FF, D), jnp.float32) * sc}
        return inp
    _L0_attn_in = _L0_attn_setup()

    def _L0_ffn_setup():
        import jax, jax.numpy as jnp
        import numpy as np
        B, S, D = (4, 256, 256)
        DFF = 704
        E, K, R = (8, 2, 16)
        SCALING = 32.0 / 16.0
        key = jax.random.key(seed)
        ks = jax.random.split(key, 12)
        s = lambda k, shape, scale: jax.random.normal(k, shape, dtype=jnp.float32) * scale
        return {'x': s(ks[0], (B, S, D), 1.0), 'Wg': s(ks[1], (DFF, D), 0.02), 'Wu': s(ks[2], (DFF, D), 0.02), 'Wd': s(ks[3], (D, DFF), 0.02), 'Wr': s(ks[4], (E, D), 0.02), 'Ag': s(ks[5], (E, R, D), 0.02), 'Bg': s(ks[6], (E, DFF, R), 0.02), 'Au': s(ks[7], (E, R, D), 0.02), 'Bu': s(ks[8], (E, DFF, R), 0.02), 'Ad': s(ks[9], (E, R, DFF), 0.02), 'Bd': s(ks[10], (E, D, R), 0.02)}
    _L0_ffn_in = _L0_ffn_setup()

    def _L1_attn_setup():
        import jax, jax.numpy as jnp
        import numpy as np
        L, N, E, H = (256, 2, 256, 16)
        DH = E // H
        SCALE = DH ** (-0.5)
        key = jax.random.key(seed)
        k1, k2, k3 = jax.random.split(key, 3)
        x = jax.random.normal(k1, (L, N, E), dtype=jnp.float32)
        weight_qkv = jax.random.normal(k2, (3 * E, E), dtype=jnp.float32) * 0.02
        weight_out = jax.random.normal(k3, (E, E), dtype=jnp.float32) * 0.02
        return {'x': x, 'weight_qkv': weight_qkv, 'weight_out': weight_out}
    _L1_attn_in = _L1_attn_setup()

    def _L1_ffn_setup():
        import jax, jax.numpy as jnp
        import numpy as np

        def _sparsify_2to4(h):
            B, S, I = h.shape
            g = h.reshape(B, S, I // 4, 4)
            a = jnp.abs(g)
            _, idx = jax.lax.top_k(a, 2)
            pos = jnp.arange(4)
            mask = (pos == idx[..., 0:1]) | (pos == idx[..., 1:2])
            return (g * mask.astype(g.dtype)).reshape(B, S, I)
        key = jax.random.key(seed)
        k1, k2, k3, k4 = jax.random.split(key, 4)
        B, S, H, I = (4, 256, 256, 1024)
        x = jax.random.normal(k1, (B, S, H), dtype=jnp.float32)
        w_gate = jax.random.normal(k2, (H, I), dtype=jnp.float32) / np.sqrt(H)
        w_up = jax.random.normal(k3, (H, I), dtype=jnp.float32) / np.sqrt(H)
        w_down = jax.random.normal(k4, (I, H), dtype=jnp.float32) / np.sqrt(I)
        return {'x': x, 'w_gate': w_gate, 'w_up': w_up, 'w_down': w_down}
    _L1_ffn_in = _L1_ffn_setup()
    _d = {'L0_attn_x': _L0_attn_in['x'], 'L0_attn_norm1_w': _L0_attn_in['norm1_w'], 'L0_attn_wq': _L0_attn_in['wq'], 'L0_attn_wk': _L0_attn_in['wk'], 'L0_attn_wv': _L0_attn_in['wv'], 'L0_attn_w_ig': _L0_attn_in['w_ig'], 'L0_attn_b_ig': _L0_attn_in['b_ig'], 'L0_attn_w_fg': _L0_attn_in['w_fg'], 'L0_attn_b_fg': _L0_attn_in['b_fg'], 'L0_attn_w_og': _L0_attn_in['w_og'], 'L0_attn_mh_w': _L0_attn_in['mh_w'], 'L0_attn_w_out': _L0_attn_in['w_out'], 'L0_attn_norm2_w': _L0_attn_in['norm2_w'], 'L0_attn_w_gate': _L0_attn_in['w_gate'], 'L0_attn_w_up': _L0_attn_in['w_up'], 'L0_attn_w_down': _L0_attn_in['w_down'], 'L0_ffn_Wg': _L0_ffn_in['Wg'], 'L0_ffn_Wu': _L0_ffn_in['Wu'], 'L0_ffn_Wd': _L0_ffn_in['Wd'], 'L0_ffn_Wr': _L0_ffn_in['Wr'], 'L0_ffn_Ag': _L0_ffn_in['Ag'], 'L0_ffn_Bg': _L0_ffn_in['Bg'], 'L0_ffn_Au': _L0_ffn_in['Au'], 'L0_ffn_Bu': _L0_ffn_in['Bu'], 'L0_ffn_Ad': _L0_ffn_in['Ad'], 'L0_ffn_Bd': _L0_ffn_in['Bd'], 'L1_attn_weight_qkv': _L1_attn_in['weight_qkv'], 'L1_attn_weight_out': _L1_attn_in['weight_out'], 'L1_ffn_w_gate': _L1_ffn_in['w_gate'], 'L1_ffn_w_up': _L1_ffn_in['w_up'], 'L1_ffn_w_down': _L1_ffn_in['w_down']}
    _x0 = _d['L0_attn_x']
    _d['L0_attn_x'] = jax.random.normal(jax.random.fold_in(jax.random.key(seed), 1), (4, 512, 256), dtype=_x0.dtype)
    del _x0
    return _d

def reference(L0_attn_x, L0_attn_norm1_w, L0_attn_wq, L0_attn_wk, L0_attn_wv, L0_attn_w_ig, L0_attn_b_ig, L0_attn_w_fg, L0_attn_b_fg, L0_attn_w_og, L0_attn_mh_w, L0_attn_w_out, L0_attn_norm2_w, L0_attn_w_gate, L0_attn_w_up, L0_attn_w_down, L0_ffn_Wg, L0_ffn_Wu, L0_ffn_Wd, L0_ffn_Wr, L0_ffn_Ag, L0_ffn_Bg, L0_ffn_Au, L0_ffn_Bu, L0_ffn_Ad, L0_ffn_Bd, L1_attn_weight_qkv, L1_attn_weight_out, L1_ffn_w_gate, L1_ffn_w_up, L1_ffn_w_down):

    def _L0_attn_ref(x, norm1_w, wq, wk, wv, w_ig, b_ig, w_fg, b_fg, w_og, mh_w, w_out, norm2_w, w_gate, w_up, w_down):
        import jax, jax.numpy as jnp
        import numpy as np
        D = 256
        H = 8
        QK = D // 2
        FF = 1024
        CAP = 15.0
        EPS = 1e-06

        def _rmsnorm(x, w, eps=EPS):
            xf = x.astype(jnp.float32)
            var = jnp.mean(xf * xf, axis=-1, keepdims=True)
            return (w * xf * jax.lax.rsqrt(var + eps)).astype(x.dtype)

        def _soft_cap(x, cap=CAP):
            return cap * jnp.tanh(x / cap)

        def _mlstm_parallel(q, k, v, i_pre, f_pre):
            B, Hn, S, dqk = q.shape
            logfg = jax.nn.log_sigmoid(f_pre)
            Fcum = jnp.cumsum(logfg, axis=-1)
            Dmat = Fcum[..., :, None] - Fcum[..., None, :] + i_pre[..., None, :]
            causal = jnp.tril(jnp.ones((S, S), dtype=bool))
            Dmat = jnp.where(causal, Dmat, -jnp.inf)
            m = jnp.max(Dmat, axis=-1, keepdims=True)
            Smat = jnp.exp(Dmat - m)
            qk = jnp.einsum('bhsd,bhtd->bhst', q, k) / jnp.sqrt(jnp.float32(dqk))
            C = qk * Smat
            n = jnp.maximum(jnp.abs(jnp.sum(C, axis=-1, keepdims=True)), jnp.exp(-m))
            h = jnp.einsum('bhst,bhtd->bhsd', C / n, v)
            return h
        B, S, _ = x.shape
        dqk, dv = (QK // H, D // H)
        h_in = _rmsnorm(x, norm1_w)
        q = (h_in @ wq).reshape(B, S, H, dqk).transpose(0, 2, 1, 3)
        k = (h_in @ wk).reshape(B, S, H, dqk).transpose(0, 2, 1, 3)
        v = (h_in @ wv).reshape(B, S, H, dv).transpose(0, 2, 1, 3)
        o_pre = h_in @ w_og
        i_pre = _soft_cap(h_in @ w_ig + b_ig).transpose(0, 2, 1)
        f_pre = _soft_cap(h_in @ w_fg + b_fg).transpose(0, 2, 1)
        h = _mlstm_parallel(q, k, v, i_pre, f_pre)
        h = h.transpose(0, 2, 1, 3)
        hf = h.astype(jnp.float32)
        var = jnp.mean(hf * hf, axis=-1, keepdims=True)
        h_norm = hf * jax.lax.rsqrt(var + EPS) * mh_w.reshape(H, dv)
        h_norm = h_norm.reshape(B, S, D)
        h_out = jax.nn.sigmoid(o_pre) * h_norm
        x1 = x + h_out @ w_out
        h2 = _rmsnorm(x1, norm2_w)
        mlp = jax.nn.silu(h2 @ w_gate) * (h2 @ w_up) @ w_down
        return x1 + mlp

    def _L0_ffn_ref(x, Wg, Wu, Wd, Wr, Ag, Bg, Au, Bu, Ad, Bd):
        import jax, jax.numpy as jnp
        import numpy as np
        B, S, D = (4, 256, 256)
        DFF = 704
        E, K, R = (8, 2, 16)
        SCALING = 32.0 / 16.0
        b, s, d = x.shape
        xf = x.reshape(-1, d)
        gate_base = xf @ Wg.T
        up_base = xf @ Wu.T
        base_out = jax.nn.silu(gate_base) * up_base @ Wd.T
        router_logits = xf @ Wr.T
        probs = jax.nn.softmax(router_logits.astype(jnp.float32), axis=-1)
        topw, topi = jax.lax.top_k(probs, K)
        topw = topw.astype(x.dtype)
        expert_w = jnp.sum(jax.nn.one_hot(topi, E, dtype=x.dtype) * topw[..., None], axis=1)

        def expert_step(acc, params):
            Ag_e, Bg_e, Au_e, Bu_e, Ad_e, Bd_e, we = params
            g_lora = xf @ Ag_e.T @ Bg_e.T * SCALING
            u_lora = xf @ Au_e.T @ Bu_e.T * SCALING
            h = jax.nn.silu(gate_base + g_lora) * (up_base + u_lora)
            d_delta = h @ Ad_e.T @ Bd_e.T * SCALING
            return (acc + d_delta * we[:, None], None)
        acc0 = jnp.zeros_like(base_out)
        acc, _ = jax.lax.scan(expert_step, acc0, (Ag, Bg, Au, Bu, Ad, Bd, expert_w.T))
        return (base_out + acc).reshape(b, s, d)

    def _L1_attn_ref(x, weight_qkv, weight_out):
        import jax, jax.numpy as jnp
        import numpy as np
        L, N, E, H = (256, 2, 256, 16)
        DH = E // H
        SCALE = DH ** (-0.5)
        l, n, e = x.shape
        h, dh = (H, DH)
        qkv = jnp.einsum('lne,fe->lnf', x, weight_qkv)
        q, k, v = jnp.split(qkv, 3, axis=-1)
        q = q.reshape(l, n, h, dh) * jnp.asarray(SCALE, x.dtype)
        k = k.reshape(l, n, h, dh)
        v = v.reshape(l, n, h, dh)
        attn = jnp.einsum('lnhd,mnhd->nhlm', q, k)
        causal = jnp.tril(jnp.ones((l, l), dtype=bool))
        attn = jnp.where(causal, attn, jnp.asarray(-jnp.inf, attn.dtype))
        attn = jax.nn.softmax(attn, axis=-1)
        out = jnp.einsum('nhlm,mnhd->lnhd', attn, v).reshape(l, n, e)
        return jnp.einsum('lne,fe->lnf', out, weight_out)

    def _L1_ffn_ref(x, w_gate, w_up, w_down):
        import jax, jax.numpy as jnp
        import numpy as np

        def _sparsify_2to4(h):
            B, S, I = h.shape
            g = h.reshape(B, S, I // 4, 4)
            a = jnp.abs(g)
            _, idx = jax.lax.top_k(a, 2)
            pos = jnp.arange(4)
            mask = (pos == idx[..., 0:1]) | (pos == idx[..., 1:2])
            return (g * mask.astype(g.dtype)).reshape(B, S, I)
        h = jax.nn.silu(jnp.einsum('bsh,hi->bsi', x, w_gate)) * jnp.einsum('bsh,hi->bsi', x, w_up)
        h_sparse = _sparsify_2to4(h)
        return jnp.einsum('bsi,ih->bsh', h_sparse, w_down)
    x = L0_attn_x
    xn = _layernorm(x, axis=-1)
    x = x + _L0_attn_ref(xn, L0_attn_norm1_w, L0_attn_wq, L0_attn_wk, L0_attn_wv, L0_attn_w_ig, L0_attn_b_ig, L0_attn_w_fg, L0_attn_b_fg, L0_attn_w_og, L0_attn_mh_w, L0_attn_w_out, L0_attn_norm2_w, L0_attn_w_gate, L0_attn_w_up, L0_attn_w_down) + _L0_ffn_ref(xn, L0_ffn_Wg, L0_ffn_Wu, L0_ffn_Wd, L0_ffn_Wr, L0_ffn_Ag, L0_ffn_Bg, L0_ffn_Au, L0_ffn_Bu, L0_ffn_Ad, L0_ffn_Bd)
    xn = _layernorm(x, axis=-1)
    x = x + _L1_attn_ref(xn, L1_attn_weight_qkv, L1_attn_weight_out) + _L1_ffn_ref(xn, L1_ffn_w_gate, L1_ffn_w_up, L1_ffn_w_down)
    return x

_drawn_inputs = setup_inputs


def setup_inputs(seed=0):
    import zlib

    import numpy as np

    out = dict(_drawn_inputs(seed))
    spreads = {'L0_attn_norm1_w': (1.0, 0.6),
     'L0_attn_b_ig': (0.0, 2.0),
     'L0_attn_mh_w': (1.0, 0.6),
     'L0_attn_norm2_w': (1.0, 0.6)}
    factors = {'L0_attn_w_fg': 64.0,
     'L0_attn_w_og': 26.96,
     'L0_ffn_Wg': 3.04,
     'L0_ffn_Wu': 2.844,
     'L0_ffn_Wd': 9.102,
     'L0_ffn_Wr': 8.0,
     'L0_ffn_Ag': 8.0,
     'L0_ffn_Bg': 8.0,
     'L0_ffn_Au': 8.0,
     'L0_ffn_Bu': 8.0,
     'L0_ffn_Ad': 8.0,
     'L0_ffn_Bd': 8.0,
     'L0_attn_wq': 7.425,
     'L0_attn_wk': 7.439,
     'L0_attn_wv': 7.391,
     'L0_attn_w_ig': 8.0,
     'L0_attn_b_fg': 8.0,
     'L0_attn_w_out': 7.402,
     'L0_attn_w_gate': 8.0,
     'L0_attn_w_up': 8.0,
     'L0_attn_w_down': 8.0,
     'L1_attn_weight_qkv': 8.0,
     'L1_attn_weight_out': 8.0,
     'L1_ffn_w_gate': 3.197,
     'L1_ffn_w_up': 2.969,
     'L1_ffn_w_down': 2.966}
    for name, (base, spread) in spreads.items():
        noise = np.random.default_rng([zlib.crc32(name.encode()), seed]).standard_normal(out[name].shape)
        drawn = base * np.exp(spread * noise) if base else spread * noise
        out[name] = jnp.asarray(drawn.astype(out[name].dtype))
    for name, factor in factors.items():
        out[name] = (out[name] * factor).astype(out[name].dtype)
    return out
```

```python
import concourse.bass as bass
from concourse import mybir
from contextlib import ExitStack

fp32 = mybir.dt.float32
fp32r = mybir.dt.float32r
ALU = mybir.AluOpType
ACT = mybir.ActivationFunctionType
AX = mybir.AxisListType
ds = bass.ds

P = 128
B, S, D = 4, 512, 256
C = S // P
KD = D // P
F = 704
FB = -(-F // P)
FP = FB * P
FT = F - (FB - 1) * P
E, RK = 8, 16
ER = E * RK
H = 8
DQ, DV = P // H, D // H
V1 = DV + 1
FF = 1024
NF = FF // P
H1, DH1 = 16, D // 16
CAP = 15.0
QUADS = (0, 32, 64)
KB = 1024


class Signal:

    def __init__(self, sem, per):
        self.sem, self.per = sem, per

    def at(self, turn, k):
        return turn * self.per + k


class Steps:

    def __init__(self, sem, turn, per):
        self.sem, self.turn, self.per, self.n = sem, turn, per, 0

    def one(self):
        self.n += 1
        return 1

    def done(self):
        return self.turn * self.per + self.n

    def close(self, what):
        assert self.n == self.per, f"{what}: {self.n} steps a turn, not {self.per}"


class Turns:

    def __init__(self, sem):
        self.sem = sem

    def at(self, turn):
        return turn * 4 + 4


class Shared:
    pass


class Map:

    def __init__(self, nc, at):
        self.nc, self.at = nc, at

    def __call__(self, name, shape, dt=fp32):
        n = 4
        for x in shape[1:]:
            n *= x
        t = self.nc.alloc_sbuf_tensor_at(name, shape, dt, offset=self.at)
        self.at += -(-n // 32) * 32
        assert self.at <= self.nc.sbuf_top, name
        return t

    def pair(self, name, shape):
        return self(name + "_hi", shape, fp32r), self(name + "_lo", shape, fp32r)


def f32(ap):
    return ap.bitcast(fp32)


def product(nc, out, w, x, start, stop):
    nc.tensor.matmul(out, w[0], x[0], start=start, stop=False, skip_group_check=True)
    nc.tensor.matmul(out, w[0], x[1], start=False, stop=False, skip_group_check=True)
    return nc.tensor.matmul(out, w[1], x[0], start=False, stop=stop, skip_group_check=True)


def cut(pair, *index):
    return pair[0][index], pair[1][index]


class Piece:

    def __init__(self, hi, lo, raw=None, turned=None, rows=P):
        self.hi, self.lo, self.raw, self.turned, self.rows = hi, lo, raw, turned, rows


def prepare(nc, sems, tag, banks, ident, loads, zeros, pieces, more=None):
    loaded, turned, high, low, blank = (sems(f"{tag}_{x}") for x in ("loaded", "turned", "high", "low", "blank"))
    block = nc.Block()
    with block:
        turns = [n for n, p in enumerate(pieces) if p.turned]

        @block.sync
        def _(sp):
            for dst, src in loads:
                sp.dma_start(dst, src).then_inc(loaded, 16)
            sp.wait_ge(loaded, 16 * len(loads))

        @block.gpsimd
        def _(pool):
            for z in zeros:
                nc.gpsimd.memset(z, 0.0).then_inc(blank, 1)
            if more:
                more(pool)

        @block.tensor
        def _(pe):
            pe.wait_ge(loaded, 16 * len(loads))
            for k, n in enumerate(turns):
                if k >= len(banks):
                    pe.wait_ge(low, turns[k - len(banks)] + 1)
                at = 0
                for x in pieces[n].turned:
                    rows, cols = x.shape[0], x.shape[1]
                    last = nc.tensor.transpose(banks[k % len(banks)][0:cols, at:at + rows], x, ident[0:rows, 0:rows])
                    at += rows
                last.then_inc(turned, 1)

        def source(n):
            p = pieces[n]
            if p.raw is not None:
                return p.raw
            k = turns.index(n)
            width = sum(x.shape[0] for x in p.turned)
            return banks[k % len(banks)][0:p.rows, 0:width]

        def shaped(src, dst):
            s = list(dst.shape)
            if len(s) == 3 and len(src.shape) == 2:
                return src.rearrange("p (a b) -> p a b", a=s[1])
            return src

        @block.scalar
        def _(act):
            act.wait_ge(loaded, 16 * len(loads))
            act.wait_ge(blank, len(zeros)) if zeros else None
            for n, p in enumerate(pieces):
                if p.turned:
                    act.wait_ge(turned, turns.index(n) + 1)
                nc.scalar.activation(p.hi, shaped(source(n), p.hi), ACT.Copy).then_inc(high, 1)

        @block.vector
        def _(dve):
            dve.wait_ge(loaded, 16 * len(loads))
            for n, p in enumerate(pieces):
                dve.wait_ge(high, n + 1)
                nc.vector.tensor_tensor(out=p.lo, in0=shaped(source(n), p.hi), in1=f32(p.hi), op=ALU.subtract).then_inc(low, 1)


def program(nc, x_in, norm1_w, wq, wk, wv, w_ig, b_ig, w_fg, b_fg, w_og, mh_w, w_out, norm2_w, w_gate, w_up,
            w_down, Wg, Wu, Wd, Wr, Ag, Bg, Au, Bu, Ad, Bd, wqkv, wo1, w1_gate, w1_up, w1_down, out):
    ctx = ExitStack()
    with ctx:
        def sems(name):
            return ctx.enter_context(nc.semaphore(name))

        def counted(name, per):
            return Signal(sems(name), per)

        bank = [ctx.enter_context(nc.psum_tensor(f"bank{n}", [P, 512], fp32)) for n in range(8)]

        keep = Map(nc, -(-nc.sbuf_base // KB) * KB)
        ident = keep("ident", [P, P])
        minus_half = keep("minus_half", [P, 16])
        head_mask = keep("head_mask", [P, H])
        head_spread = keep("head_spread", [H, P])
        expert_rank = keep("expert_rank", [P, C * E])
        ones_row = keep("ones_row", [H, S])
        causal = keep("causal", [P, P])
        norm1_col = keep("norm1_col", [P, KD])
        norm2_col = keep("norm2_col", [P, KD])
        mh_col = keep("mh_col", [P, KD])
        gate_bias = keep("gate_bias", [H, 2])
        gate_bias15 = keep("gate_bias15", [H, 2])
        scale_y = keep("scale_y", [P, B * C])
        res = keep("res", [P, B * C, D])
        xn = keep("xn", [P, B * C, D])
        W0 = -(-keep.at // KB) * KB
        x_tiles = x_in.rearrange("b (c p) d -> p (b c) d", p=P)

        const_ready, x_loaded = sems("const_ready"), sems("x_loaded")
        block = nc.Block()
        with block:
            @block.sync
            def _(sp):
                for b in range(B):
                    sp.dma_start(res[:, b * C:(b + 1) * C, :], x_tiles[:, b * C:(b + 1) * C, :]).then_inc(x_loaded, 16)
                small = [(norm1_col[:, :], norm1_w.rearrange("(k p) -> p k", p=P)),
                         (norm2_col[:, :], norm2_w.rearrange("(k p) -> p k", p=P)),
                         (mh_col[:, :], mh_w.rearrange("(k p) -> p k", p=P)),
                         (gate_bias[:, 0:1], b_ig.rearrange("(h o) -> h o", o=1)),
                         (gate_bias[:, 1:2], b_fg.rearrange("(h o) -> h o", o=1))]
                with nc.allow_non_contiguous_dma(reason="a few hundred words"):
                    for dst, src in small:
                        sp.dma_start(dst, src).then_inc(x_loaded, 16)
                sp.wait_ge(x_loaded, 16 * (B + len(small)))

            @block.gpsimd
            def _(pool):
                steps = Steps(const_ready, 0, 0)
                nc.gpsimd.memset(ident[:, :], 0.0).then_inc(steps.sem, steps.one())
                nc.gpsimd.memset(head_mask[:, :], 1.0).then_inc(steps.sem, steps.one())
                nc.gpsimd.memset(head_spread[:, :], 1.0).then_inc(steps.sem, steps.one())
                nc.gpsimd.memset(minus_half[:, :], -0.5).then_inc(steps.sem, steps.one())
                nc.gpsimd.memset(causal[:, :], 0.0).then_inc(steps.sem, steps.one())
                nc.gpsimd.memset(ones_row[:, :], 1.0).then_inc(steps.sem, steps.one())
                for e in range(E):
                    nc.gpsimd.memset(expert_rank[:, e::E], float(E - e)).then_inc(steps.sem, steps.one())
                pool.wait_ge(steps.sem, steps.done())
                nc.gpsimd.affine_select(out=ident[:, :], in_=ident[:, :], compare_op=ALU.not_equal, fill=1.0,
                                              base=0, pattern=[[-1, P]], channel_multiplier=1).then_inc(steps.sem, steps.one())
                nc.gpsimd.affine_select(out=causal[:, :], in_=causal[:, :], compare_op=ALU.is_ge, fill=-1e30,
                                              base=0, pattern=[[1, P]], channel_multiplier=-1).then_inc(steps.sem, steps.one())
                nc.gpsimd.affine_select(out=head_mask[:, :], in_=head_mask[:, :], compare_op=ALU.is_ge, fill=0.0,
                                              base=0, pattern=[[-DQ, H]], channel_multiplier=1).then_inc(steps.sem, steps.one())
                nc.gpsimd.affine_select(out=head_spread[:, :], in_=head_spread[:, :], compare_op=ALU.is_ge,
                                              fill=0.0, base=0, pattern=[[1, P]], channel_multiplier=-DQ).then_inc(steps.sem, steps.one())
                pool.wait_ge(steps.sem, steps.done())
                nc.gpsimd.affine_select(out=head_mask[:, :], in_=head_mask[:, :], compare_op=ALU.is_ge, fill=0.0,
                                              base=DQ - 1, pattern=[[DQ, H]], channel_multiplier=-1).then_inc(steps.sem, steps.one())
                nc.gpsimd.affine_select(out=head_spread[:, :], in_=head_spread[:, :], compare_op=ALU.is_ge,
                                              fill=0.0, base=DQ - 1, pattern=[[-1, P]], channel_multiplier=DQ).then_inc(steps.sem, steps.one())

            @block.vector
            def _(dve):
                dve.wait_ge(x_loaded, 16 * (B + 5))
                nc.vector.tensor_scalar(out=gate_bias15[:, :], in0=gate_bias[:, :], scalar1=1.0 / CAP, scalar2=None,
                                        op0=ALU.mult)

        g = Shared()
        g.ident, g.causal, g.head_mask, g.head_spread = ident, causal, head_mask, head_spread
        g.minus_half, g.expert_rank, g.ones_row = minus_half, expert_rank, ones_row
        g.norm1_col, g.norm2_col, g.mh_col, g.gate_bias15 = norm1_col, norm2_col, mh_col, gate_bias15
        g.scale_y, g.bank, g.W0, g.sems, g.counted = scale_y, bank, W0, sems, counted
        g.res, g.xnf = res[:, :, :].rearrange("p t d -> p (t d)"), xn[:, :, :].rearrange("p t d -> p (t d)")
        ffn_phase(nc, g, Wg, Wu, Wd, Wr, Ag, Bg, Au, Bu, Ad, Bd)
        mlstm_phase(nc, g, wq, wk, wv, w_ig, w_fg, w_og, w_out)
        mlp_phase(nc, g, w_gate, w_up, w_down)
        layer1_phase(nc, g, wqkv, wo1, w1_gate, w1_up, w1_down, out)


def moments(nc, v, st, mv, t):
    nc.vector.tensor_tensor(out=t[0][:, :], in0=st[:, :, 1], in1=st[:, :, 4], op=ALU.add).then_inc(v.sem, v.one())
    nc.vector.tensor_tensor(out=t[1][:, :], in0=st[:, :, 1], in1=st[:, :, 4], op=ALU.subtract).then_inc(v.sem, v.one())
    nc.vector.tensor_tensor(out=t[2][:, :], in0=st[:, :, 2], in1=st[:, :, 5], op=ALU.add).then_inc(v.sem, v.one())
    nc.vector.wait_ge(v.sem, v.done())
    nc.vector.tensor_scalar(out=mv[:, :, 0], in0=t[0][:, :], scalar1=0.5, scalar2=None, op0=ALU.mult).then_inc(v.sem, v.one())
    nc.vector.scalar_tensor_tensor(out=t[3][:, :], in0=t[1][:, :], scalar=0.25, in1=t[1][:, :], op0=ALU.mult, op1=ALU.mult).then_inc(v.sem, v.one())
    nc.vector.wait_ge(v.sem, v.done())
    nc.vector.scalar_tensor_tensor(out=mv[:, :, 1], in0=t[2][:, :], scalar=1.0 / D, in1=t[3][:, :], op0=ALU.mult, op1=ALU.add).then_inc(v.sem, v.one())
    nc.vector.wait_ge(v.sem, v.done())


class Hidden:

    RING = 4

    def __init__(self, nc, g, name, units, m):
        self.nc, self.units = nc, units
        self.gate_up = g.counted(name + "_gate_up", units)
        self.silu = g.counted(name + "_silu", units)
        self.hidden = g.counted(name + "_hidden", units)
        self.hi = g.counted(name + "_hi", units)
        self.lo = g.counted(name + "_lo", units)
        self.down = g.counted(name + "_down", units)
        self.s = [m(f"{name}_s{n}", [P, S]) for n in range(2)]
        self.h = [m(f"{name}_h{n}", [P, S]) for n in range(2)]
        self.ring = [m.pair(f"{name}_ring{n}", [P, S]) for n in range(self.RING)]

    def unit(self, u):
        return self.ring[u % self.RING]

    def act_silu(self, act, i, u, gate):
        act.wait_ge(self.gate_up.sem, self.gate_up.at(i, u + 1))
        if u >= 2:
            act.wait_ge(self.hidden.sem, self.hidden.at(i, u - 1))
        self.nc.scalar.activation(self.s[u % 2][:, :], gate, ACT.Silu).then_inc(self.silu.sem, 1)

    def act_hi(self, act, i, u):
        act.wait_ge(self.hidden.sem, self.hidden.at(i, u + 1))
        if u >= self.RING:
            act.wait_ge(self.down.sem, self.down.at(i, u + 1 - self.RING))
        self.nc.scalar.activation(self.unit(u)[0][:, :], self.h[u % 2][:, :], ACT.Copy).then_inc(self.hi.sem, 1)

    def dve_hidden(self, dve, i, u, up):
        dve.wait_ge(self.silu.sem, self.silu.at(i, u + 1))
        if u >= 2:
            dve.wait_ge(self.hi.sem, self.hi.at(i, u - 1))
            dve.wait_ge(self.lo.sem, self.lo.at(i, u - 1))
        self.nc.vector.tensor_tensor(out=self.h[u % 2][:, :], in0=self.s[u % 2][:, :], in1=up, op=ALU.mult).then_inc(self.hidden.sem, 1)

    def dve_lo(self, dve, i, u):
        dve.wait_ge(self.hi.sem, self.hi.at(i, u + 1))
        self.nc.vector.tensor_tensor(out=self.unit(u)[1][:, :], in0=self.h[u % 2][:, :],
                                                in1=f32(self.unit(u)[0][:, :]), op=ALU.subtract).then_inc(self.lo.sem, 1)


def expand(ap, n):
    return ap.unsqueeze(len(ap.shape)).to_broadcast(list(ap.shape) + [n])


def ffn_phase(nc, g, Wg, Wu, Wd, Wr, Ag, Bg, Au, Bu, Ad, Bd):
    bank, ident = g.bank, g.ident
    m = Map(nc, g.W0)
    wgu = m.pair("wgu", [P, KD, 2, FP])
    wb = m.pair("wb", [P, 2, FP])
    wa = m.pair("wa", [P, KD, 2, ER])
    wad = m.pair("wad", [P, FB, ER])
    wbd = m.pair("wbd", [P, D])
    wd = m.pair("wd", [P, FB, D])
    wr = m.pair("wr", [P, KD, P])
    r = Map(nc, m.at)
    rg, ru = r("rg", [P, FB, D]), r("ru", [P, FB, D])
    rbg, rbu = r("rbg", [P, FB, ER]), r("rbu", [P, FB, ER])
    rag, rau, rad = r("rag", [P, D]), r("rau", [P, D]), r("rad", [P, F])
    rbd, rd, rr = r("rbd", [P, KD, ER]), r("rd", [P, KD, F]), r("rr", [E, D])
    loads, pieces = [], []
    whole = (FB - 1) * P
    for dst, src in ((rg, Wg), (ru, Wu)):
        loads += [(dst[:, 0:FB - 1, :], src[0:whole, :].rearrange("(b p) d -> p b d", p=P)), (dst[0:FT, FB - 1, :], src[whole:F, :])]
    for dst, src in ((rbg, Bg), (rbu, Bu)):
        for e in range(E):
            c0 = slice(e * RK, (e + 1) * RK)
            loads += [(dst[:, 0:FB - 1, c0], src[e, 0:whole, :].rearrange("(b p) r -> p b r", p=P)),
                      (dst[0:FT, FB - 1, c0], src[e, whole:F, :])]
    loads += [(rag[:, :], Ag.rearrange("e r d -> (e r) d")), (rau[:, :], Au.rearrange("e r d -> (e r) d")),
              (rad[:, :], Ad.rearrange("e r f -> (e r) f")), (rd[:, :, :], Wd.rearrange("(k p) f -> p k f", p=P)),
              (rr[:, :], Wr)]
    loads += [(rbd[:, k, e * RK:(e + 1) * RK], Bd[e, k * P:(k + 1) * P, :]) for k in range(KD) for e in range(E)]

    def blocks(raw, b0, b1, cols):
        return [raw[0:min(P, F - b * P), b, cols] for b in range(b0, b1)]

    def both(pair, *index):
        return {"hi": pair[0][index], "lo": pair[1][index]}

    a = slice(None)
    for n, raw in ((0, rg), (1, ru)):
        for k in range(KD):
            cols = slice(k * P, (k + 1) * P)
            pieces.append(Piece(**both(wgu, a, k, n, slice(0, 4 * P)), turned=blocks(raw, 0, 4, cols)))
            pieces.append(Piece(**both(wgu, a, k, n, slice(4 * P, F)), turned=blocks(raw, 4, FB, cols)))
    for n, raw in ((0, rbg), (1, rbu)):
        pieces.append(Piece(**both(wb, a, n, slice(0, 4 * P)), turned=blocks(raw, 0, 4, a)))
        pieces.append(Piece(**both(wb, a, n, slice(4 * P, F)), turned=blocks(raw, 4, FB, a)))
    for k in range(KD):
        pieces.append(Piece(**both(wa, a, k), turned=[x[:, k * P:(k + 1) * P] for x in (rag, rau)]))
    pieces.append(Piece(**both(wad, a, slice(0, 4)), turned=[rad[:, b * P:(b + 1) * P] for b in range(4)]))
    pieces.append(Piece(**both(wad, a, 4), turned=[rad[:, 4 * P:5 * P]]))
    pieces.append(Piece(**both(wad, slice(0, FT), 5), turned=[rad[:, 5 * P:F]], rows=FT))
    pieces.append(Piece(**both(wbd, a, a), turned=[rbd[:, k, :] for k in range(KD)]))
    for b in range(FB):
        n = min(P, F - b * P)
        pieces.append(Piece(**both(wd, slice(0, n), b), turned=[rd[:, k, b * P:b * P + n] for k in range(KD)], rows=n))
    for k in range(KD):
        pieces.append(Piece(**both(wr, a, k, slice(0, E)), turned=[rr[:, k * P:(k + 1) * P]]))
    zeros = []
    for t in (0, 1):
        zeros += [f32(wgu[t][:, :, :, F:FP]), f32(wb[t][:, :, F:FP]), f32(wad[t][:, FB - 1, :]), f32(wd[t][:, FB - 1, :]), f32(wr[t][:, :, :])]
    prepare(nc, g.sems, "ffn_w", bank, ident, loads, zeros, pieces)

    xs = m("f_xs", [P, C, D])
    st, mv = m("f_st", [P, C, 6]), m("f_mv", [P, C, 2])
    vv, rstd, msq = m("f_vv", [P, C]), m("f_rstd", [P, C]), m("f_msq", [P, C])
    xT = m.pair("f_xT", [P, KD, S])
    lg = m("f_lg", [P, S])
    small = [m(f"f_small{n}", [P, C * E]) for n in range(7)]
    tiny = [m(f"f_tiny{n}", [P, C]) for n in range(7)]
    sel = m("f_sel", [P, 4, C * E])
    selx = m("f_selx", [P, 4, C * E * RK])
    mask = m("f_mask", [P, 4, S])
    low = [m.pair(f"f_a{n}", [P, S]) for n in range(2)]
    op = [[m.pair(f"f_op{n}{t}", [P, S]) for t in range(2)] for n in range(2)]
    zt = [m(f"f_z{n}", [P, S]) for n in range(2)]
    z = m.pair("f_z", [P, S])
    order = [(b0 + n, t) for b0 in range(0, FB, 2) for t in range(3) for n in range(2)]
    U = len(order)
    hid = Hidden(nc, g, "f", U, m)
    turns = Turns(g.sems("f_turns"))
    sg = g.counted
    stats, powed, xs_ready, xT_t, xT_hi, xT_lo = sg("f_stats", 2), sg("f_pow", 2), sg("f_xs", 1), sg("f_xTt", 2), sg("f_xThi", 2), sg("f_xTlo", 2)
    lg_ready, lg_copied, lgT, centred, exped = sg("f_lg", 1), sg("f_lgc", 1), sg("f_lgT", 1), sg("f_cent", 1), sg("f_exp", 1)
    a_done, a_hi, a_lo = sg("f_a", 2), sg("f_ahi", 2), sg("f_alo", 2)
    spread, mask_t, mask_in, ops = sg("f_spread", 4), sg("f_maskt", 4), sg("f_maskin", 4), sg("f_ops", 8)
    zsum, zhi, zlo, acc_done = sg("f_zsum", 1), sg("f_zhi", 1), sg("f_zlo", 1), sg("f_acc", 1)
    NSTEP = 38
    dve_sem = g.sems("f_dve")
    gate = lambda u: bank[0] if order[u][0] % 2 == 0 else bank[2]
    up = lambda u: bank[1] if order[u][0] % 2 == 0 else bank[3]
    low_bank, acc = [bank[4], bank[5]], [bank[6], bank[7]]
    lg_bank, a_bank, lgT_bank = bank[2], [bank[3], bank[4]], bank[5]
    mask_bank = [bank[2], bank[5], bank[6], bank[7]]
    block = nc.Block()
    with block:
        @block.tensor
        def _(pe):
            pe.sem_inc(turns.sem, 1)

            def units(i, u):
                b, t = order[u]
                if u >= 2:
                    pe.wait_ge(hid.hidden.sem, hid.hidden.at(i, u - 1))
                for n, o in ((0, gate(u)), (1, up(u))):
                    cols = slice(b * P, (b + 1) * P)
                    if t == 0:
                        for k in range(KD):
                            last = product(nc, o[:, :], cut(wgu, a, k, n, cols), cut(xT, a, k), k == 0, k == KD - 1)
                    else:
                        if b == 0:
                            pe.wait_ge(ops.sem, ops.at(i, 4 * t if n else 4 * t - 2))
                        last = product(nc, o[:, :], cut(wb, a, n, cols), cut(op[t - 1][n], a, a), False, True)
                last.then_inc(hid.gate_up.sem, 1)

            def down(i, u):
                b, t = order[u]
                h = hid.unit(u)
                pe.wait_ge(hid.lo.sem, hid.lo.at(i, u + 1))
                if t == 0:
                    for c in range(C):
                        last = product(nc, acc[c // 2][:, c % 2 * D:(c % 2 + 1) * D], cut(h, a, slice(c * P, (c + 1) * P)),
                                       cut(wd, a, b), b == 0 and c % 2 == 0, False)
                else:
                    last = product(nc, low_bank[t - 1][:, :], cut(wad, a, b), cut(h, a, a), b == 0, b == FB - 1)
                last.then_inc(hid.down.sem, 1)

            with pe.Fori(0, B) as i:
                pe.wait_ge(turns.sem, turns.at(i))
                pe.wait_ge(xs_ready.sem, xs_ready.at(i, 1))
                for k in range(KD):
                    for c in range(C):
                        last = nc.tensor.transpose(bank[k][:, c * P:(c + 1) * P], xs[:, c, k * P:(k + 1) * P], ident[:, :])
                    last.then_inc(xT_t.sem, 1)
                pe.wait_ge(xT_lo.sem, xT_lo.at(i, KD))
                for k in range(KD):
                    last = product(nc, lg_bank[:, :], cut(wr, a, k), cut(xT, a, k), k == 0, k == KD - 1)
                last.then_inc(lg_ready.sem, 1)
                for n in range(2):
                    for k in range(KD):
                        last = product(nc, a_bank[n][:, :], cut(wa, a, k, n), cut(xT, a, k), k == 0, k == KD - 1)
                    last.then_inc(a_done.sem, 1)
                pe.wait_ge(lg_copied.sem, lg_copied.at(i, 1))
                for c in range(C):
                    last = nc.tensor.transpose(lgT_bank[:, c * P:(c + 1) * P], lg[:, c * P:(c + 1) * P], ident[:, :])
                last.then_inc(lgT.sem, 1)
                units(i, 0)
                for n in range(4):
                    pe.wait_ge(spread.sem, spread.at(i, n + 1))
                    for c in range(C):
                        last = nc.tensor.transpose(mask_bank[n][:, c * P:(c + 1) * P], selx[:, n, c * ER:(c + 1) * ER], ident[:, :])
                    last.then_inc(mask_t.sem, 1)
                pe.wait_ge(mask_in.sem, mask_in.at(i, 4))
                pe.wait_ge(a_lo.sem, a_lo.at(i, 2))
                for u in range(1, U):
                    units(i, u)
                    if u >= 2:
                        down(i, u - 2)
                down(i, U - 2)
                down(i, U - 1)
                pe.wait_ge(zlo.sem, zlo.at(i, 1))
                for c in range(C):
                    last = product(nc, acc[c // 2][:, c % 2 * D:(c % 2 + 1) * D], cut(z, a, slice(c * P, (c + 1) * P)),
                                   cut(wbd, a, a), False, True)
                last.then_inc(acc_done.sem, 1)
                pe.nop().then_inc(turns.sem, 1)

        @block.scalar
        def _(act):
            act.sem_inc(turns.sem, 1)
            with act.Fori(0, B) as i:
                act.wait_ge(turns.sem, turns.at(i))
                for k in range(KD):
                    act.wait_ge(xT_t.sem, xT_t.at(i, k + 1))
                    nc.scalar.activation(xT[0][:, k, :], bank[k][:, :], ACT.Copy).then_inc(xT_hi.sem, 1)
                act.wait_ge(lg_ready.sem, lg_ready.at(i, 1))
                nc.scalar.activation(lg[:, :], lg_bank[:, :], ACT.Copy).then_inc(lg_copied.sem, 1)
                for n in range(2):
                    act.wait_ge(a_done.sem, a_done.at(i, n + 1))
                    nc.scalar.activation(low[n][0][:, :], a_bank[n][:, :], ACT.Copy).then_inc(a_hi.sem, 1)
                act.wait_ge(centred.sem, centred.at(i, 1))
                nc.scalar.activation(small[1][:, :], small[0][:, :], ACT.Exp).then_inc(exped.sem, 1)
                for n in range(4):
                    act.wait_ge(mask_t.sem, mask_t.at(i, n + 1))
                    nc.scalar.activation(mask[:, n, :], mask_bank[n][:, :], ACT.Copy).then_inc(mask_in.sem, 1)
                for u in range(U):
                    hid.act_silu(act, i, u, gate(u)[:, :])
                    if u:
                        hid.act_hi(act, i, u - 1)
                hid.act_hi(act, i, U - 1)
                act.wait_ge(zsum.sem, zsum.at(i, 1))
                nc.scalar.activation(z[0][:, :], zt[0][:, :], ACT.Copy).then_inc(zhi.sem, 1)
                act.nop().then_inc(turns.sem, 1)

        @block.gpsimd
        def _(pool):
            pool.sem_inc(turns.sem, 1)
            with pool.Fori(0, B) as i:
                pool.wait_ge(turns.sem, turns.at(i))
                pool.wait_ge(stats.sem, stats.at(i, 1))
                nc.gpsimd.tensor_tensor(out=rstd[:, :], in0=vv[:, :], in1=g.minus_half[:, 0:C], op=ALU.pow).then_inc(powed.sem, 1)
                pool.wait_ge(stats.sem, stats.at(i, 2))
                nc.gpsimd.tensor_tensor(out=g.scale_y[:, ds(i * C, C)], in0=msq[:, :], in1=g.minus_half[:, 0:C], op=ALU.pow).then_inc(powed.sem, 1)
                pool.wait_ge(xs_ready.sem, xs_ready.at(i, 1))
                nc.gpsimd.tensor_copy(g.xnf[:, ds(i * C * D, C * D)], xs[:, :, :].rearrange("p c d -> p (c d)"))
                pool.wait_ge(a_lo.sem, a_lo.at(i, 2))
                for t in range(2):
                    pool.wait_ge(mask_in.sem, mask_in.at(i, t + 1))
                    for n in range(2):
                        for part in range(2):
                            nc.gpsimd.tensor_tensor(out=op[t][n][part][:, :], in0=f32(low[n][part][:, :]), in1=mask[:, t, :], op=ALU.mult).then_inc(ops.sem, 1)
                pool.nop().then_inc(turns.sem, 1)

        @block.vector
        def _(dve):
            dve.sem_inc(turns.sem, 1)
            with dve.Fori(0, B) as i:
                dve.wait_ge(turns.sem, turns.at(i))
                v = Steps(dve_sem, i, NSTEP)
                for c in range(C):
                    nc.vector.bn_stats(out=st[:, c, :], in_=g.res[:, ds((i * C + c) * D, D)]).then_inc(v.sem, v.one())
                dve.wait_ge(v.sem, v.done())
                moments(nc, v, st, mv, tiny)
                nc.vector.tensor_scalar(out=vv[:, :], in0=mv[:, :, 1], scalar1=1e-5, scalar2=None, op0=ALU.add).then_inc(stats.sem, 1)
                dve.wait_ge(powed.sem, powed.at(i, 1))
                for c in range(C):
                    last = nc.vector.tensor_scalar(out=xs[:, c, :], in0=g.res[:, ds((i * C + c) * D, D)], scalar1=mv[:, c, 0:1],
                                                   scalar2=rstd[:, c:c + 1], op0=ALU.subtract, op1=ALU.mult)
                    if c < C - 1:
                        last.then_inc(v.sem, v.one())
                last.then_inc(xs_ready.sem, 1)
                nc.vector.tensor_tensor(out=tiny[0][:, :], in0=mv[:, :, 1], in1=rstd[:, :], op=ALU.mult).then_inc(v.sem, v.one())
                dve.wait_ge(v.sem, v.done())
                nc.vector.tensor_tensor(out=tiny[1][:, :], in0=tiny[0][:, :], in1=rstd[:, :], op=ALU.mult).then_inc(v.sem, v.one())
                dve.wait_ge(v.sem, v.done())
                nc.vector.tensor_scalar(out=msq[:, :], in0=tiny[1][:, :], scalar1=1e-6, scalar2=None, op0=ALU.add).then_inc(stats.sem, 1)
                for k in range(KD):
                    dve.wait_ge(xT_hi.sem, xT_hi.at(i, k + 1))
                    nc.vector.tensor_tensor(out=xT[1][:, k, :], in0=bank[k][:, :], in1=f32(xT[0][:, k, :]), op=ALU.subtract).then_inc(xT_lo.sem, 1)
                for n in range(2):
                    dve.wait_ge(a_hi.sem, a_hi.at(i, n + 1))
                    nc.vector.tensor_tensor(out=low[n][1][:, :], in0=a_bank[n][:, :], in1=f32(low[n][0][:, :]), op=ALU.subtract).then_inc(a_lo.sem, 1)
                per_token = lambda t: t[:, :].rearrange("p (c e) -> p c e", e=E)
                lgv = lgT_bank[:, :].rearrange("p (c e) -> p c e", e=P)[:, :, 0:E]
                dve.wait_ge(lgT.sem, lgT.at(i, 1))
                nc.vector.tensor_reduce(out=tiny[0][:, :], in_=lgv, op=ALU.max, axis=AX.X).then_inc(v.sem, v.one())
                dve.wait_ge(v.sem, v.done())
                nc.vector.tensor_tensor(out=per_token(small[0]), in0=lgv, in1=expand(tiny[0][:, :], E), op=ALU.subtract).then_inc(centred.sem, 1)
                dve.wait_ge(exped.sem, exped.at(i, 1))
                nc.vector.tensor_reduce(out=tiny[1][:, :], in_=per_token(small[1]), op=ALU.add, axis=AX.X).then_inc(v.sem, v.one())
                dve.wait_ge(v.sem, v.done())
                nc.vector.reciprocal(out=tiny[2][:, :], in_=tiny[1][:, :]).then_inc(v.sem, v.one())
                dve.wait_ge(v.sem, v.done())
                nc.vector.tensor_tensor(out=per_token(small[2]), in0=per_token(small[1]), in1=expand(tiny[2][:, :], E), op=ALU.mult).then_inc(v.sem, v.one())
                dve.wait_ge(v.sem, v.done())

                def largest(src, one_hot, n):
                    nc.vector.tensor_reduce(out=tiny[n][:, :], in_=per_token(src), op=ALU.max, axis=AX.X).then_inc(v.sem, v.one())
                    dve.wait_ge(v.sem, v.done())
                    nc.vector.tensor_tensor(out=per_token(small[3]), in0=per_token(src), in1=expand(tiny[n][:, :], E), op=ALU.is_equal).then_inc(v.sem, v.one())
                    dve.wait_ge(v.sem, v.done())
                    nc.vector.tensor_tensor(out=small[4][:, :], in0=small[3][:, :], in1=g.expert_rank[:, :], op=ALU.mult).then_inc(v.sem, v.one())
                    dve.wait_ge(v.sem, v.done())
                    nc.vector.tensor_reduce(out=tiny[n + 1][:, :], in_=per_token(small[4]), op=ALU.max, axis=AX.X).then_inc(v.sem, v.one())
                    dve.wait_ge(v.sem, v.done())
                    nc.vector.tensor_tensor(out=per_token(one_hot), in0=per_token(small[4]), in1=expand(tiny[n + 1][:, :], E), op=ALU.is_equal).then_inc(v.sem, v.one())
                    dve.wait_ge(v.sem, v.done())

                largest(small[2], small[5], 3)
                nc.vector.scalar_tensor_tensor(out=small[0][:, :], in0=small[5][:, :], scalar=-4.0, in1=small[2][:, :], op0=ALU.mult, op1=ALU.add).then_inc(v.sem, v.one())
                dve.wait_ge(v.sem, v.done())
                largest(small[0], small[6], 5)
                nc.vector.tensor_scalar(out=sel[:, 0, :], in0=small[5][:, :], scalar1=2.0, scalar2=None, op0=ALU.mult).then_inc(v.sem, v.one())
                nc.vector.tensor_scalar(out=small[1][:, :], in0=small[6][:, :], scalar1=2.0, scalar2=None, op0=ALU.mult).then_inc(v.sem, v.one())
                dve.wait_ge(v.sem, v.done())
                nc.vector.tensor_tensor(out=sel[:, 1, :], in0=small[1][:, :], in1=sel[:, 0, :], op=ALU.subtract).then_inc(v.sem, v.one())
                nc.vector.tensor_tensor(out=sel[:, 2, :], in0=sel[:, 0, :], in1=small[2][:, :], op=ALU.mult).then_inc(v.sem, v.one())
                nc.vector.tensor_tensor(out=sel[:, 3, :], in0=small[1][:, :], in1=small[2][:, :], op=ALU.mult).then_inc(v.sem, v.one())
                dve.wait_ge(v.sem, v.done())
                for n in range(4):
                    nc.vector.tensor_copy(selx[:, n, :].rearrange("p (x r) -> p x r", r=RK), expand(sel[:, n, :], RK)).then_inc(spread.sem, 1)
                for u in range(U):
                    hid.dve_hidden(dve, i, u, up(u)[:, :])
                    if u:
                        hid.dve_lo(dve, i, u - 1)
                hid.dve_lo(dve, i, U - 1)
                dve.wait_ge(hid.down.sem, hid.down.at(i, U))
                for t in range(2):
                    nc.vector.tensor_tensor(out=zt[t][:, :], in0=low_bank[t][:, :], in1=mask[:, 2 + t, :], op=ALU.mult).then_inc(v.sem, v.one())
                dve.wait_ge(v.sem, v.done())
                nc.vector.tensor_tensor(out=zt[0][:, :], in0=zt[0][:, :], in1=zt[1][:, :], op=ALU.add).then_inc(zsum.sem, 1)
                dve.wait_ge(zhi.sem, zhi.at(i, 1))
                nc.vector.tensor_tensor(out=z[1][:, :], in0=zt[0][:, :], in1=f32(z[0][:, :]), op=ALU.subtract).then_inc(zlo.sem, 1)
                dve.wait_ge(acc_done.sem, acc_done.at(i, 1))
                for n in range(2):
                    at = g.res[:, ds(i * C * D + n * 2 * D, 2 * D)]
                    last = nc.vector.tensor_tensor(out=at, in0=acc[n][:, :], in1=at, op=ALU.add)
                    if n == 0:
                        last.then_inc(v.sem, v.one())
                last.then_inc(turns.sem, 1)
                v.close("ffn dve")


def mlstm_phase(nc, g, wq, wk, wv, w_ig, w_fg, w_og, w_out):
    bank, ident = g.bank, g.ident
    a = slice(None)
    m = Map(nc, g.W0)
    NKV = P + D
    wp = m.pair("wp", [P, KD, 2 * P + 2 * D])
    wg = m.pair("wg", [P, KD, 2, P])
    wo = m.pair("wo", [P, KD, D])
    Kc, Vc, Qc, Oc = slice(0, P), slice(P, NKV), slice(NKV, NKV + P), slice(NKV + P, NKV + P + D)
    rows = lambda w: w.rearrange("(k p) n -> p k n", p=P)
    zeros = [f32(wg[t][:, :, :, :]) for t in (0, 1)]

    VW = H * V1
    v1 = m("m_v1", [P, C, VW])
    gr = m("m_gr", [QUADS[2] + H, S])
    pairw = [m(f"m_pairw{n}", [P, H, P]) for n in range(2)]
    ga = m("m_ga", [P, 3, C, H])
    ga_flat = ga[:, :, :, :].rearrange("p a c h -> p (a c h)")

    def presets(pool):
        nc.gpsimd.memset(v1[:, :, :], 1.0).then_inc(preset, 1)
        nc.gpsimd.memset(gr[:, :], 0.0).then_inc(preset, 1)
        nc.gpsimd.memset(ga_flat, 0.0).then_inc(preset, 1)
        pool.wait_ge(preset, 3)

    preset = g.sems("m_preset")
    r = Map(nc, m.at)
    rp, rgt, ro = r("m_rp2", [P, KD, 2 * P + 2 * D]), r("m_rg2", [P, KD, 2, H]), r("m_ro2", [P, KD, D])
    loads = [(rp[:, :, Kc], rows(wk)), (rp[:, :, Vc], rows(wv)), (rp[:, :, Qc], rows(wq)), (rp[:, :, Oc], rows(w_og)),
             (rgt[:, :, 0, :], rows(w_ig)), (rgt[:, :, 1, :], rows(w_fg)), (ro[:, :, :], rows(w_out))]
    pieces = [Piece(wp[0][:, k, :], wp[1][:, k, :], raw=rp[:, k, :]) for k in range(KD)]
    pieces += [Piece(wg[0][:, k, :, 0:H], wg[1][:, k, :, 0:H], raw=rgt[:, k, :, :]) for k in range(KD)]
    pieces += [Piece(wo[0][:, :, :], wo[1][:, :, :], raw=ro[:, :, :])]
    prepare(nc, g.sems, "mlstm_w", bank, ident, loads, zeros, pieces, presets)

    ys = m("m_ys", [P, C, D])
    yT = m.pair("m_yT", [P, KD, S])
    qs, kT = m("m_qs", [P, S]), m("m_kT", [P, S])
    ktok, ktil = m("m_ktok", [P, C, P]), m("m_ktil", [P, C, P])
    sig = m("m_sig", [P, C, D])
    qbd = [m(f"m_qbd{n}", [P, H, P]) for n in range(2)]
    Gb = m("m_Gb", [P, H, S])
    PT = [m(f"m_PT{n}", [P, H, P]) for n in range(2)]
    tot = m("m_tot", [P, C, VW])
    hh, sq = m("m_hh", [P, C, D]), m("m_sq", [P, C, D])
    hT = m.pair("m_hT", [P, KD, S])
    row = [m(f"m_row{n}", [H, S]) for n in range(9)]
    tg = m("m_tg", [P, C, QUADS[2] + H])
    ea = m("m_ea", [P, 3, C, H])
    gend, dec, dexp = m("m_gend", [P, C]), m("m_dec", [P, C - 1]), m("m_dexp", [P, C - 1])
    state, part = m("m_state", [P, VW]), m("m_part", [P, VW])
    den = [m(f"m_den{n}", [P, C * H]) for n in range(7)]
    scratch = nc.dram_tensor("m_scratch", (B, H, S), fp32, kind="Internal").ap()

    sg = g.counted
    turns = Turns(g.sems("m_turns"))
    y_ready, yT_t, yT_hi, yT_lo = sg("m_y", 1), sg("m_yTt", 2), sg("m_yThi", 2), sg("m_yTlo", 2)
    gates, qk, kv, og = sg("m_gates", 2), sg("m_qk", 2), sg("m_kv", C), sg("m_og", 2)
    tanhed, qk_in, kv_in, og_in = sg("m_tanh", 2), sg("m_qkin", 2), sg("m_kvin", 2 * C), sg("m_ogin", 2)
    u_ready, y1_ready, ln_ready, rows_ready = sg("m_u", 1), sg("m_y1", 1), sg("m_ln", 2), sg("m_rows", 2)
    G_copied, stored, spread = sg("m_Gc", 1), sg("m_stored", 16), sg("m_spread", 16)
    tg_ready, gend_ready, tg_in = sg("m_tg_t", 1), sg("m_gend", 1), sg("m_tg_in", 2)
    ga_ready, ea_ready, dec_ready, dexp_ready = sg("m_ga", 1), sg("m_ea", 1), sg("m_dec", 1), sg("m_dexp", 1)
    q_spread, diff, weight, ktil_ready = sg("m_qspread", C), sg("m_diff", C), sg("m_weight", C), sg("m_ktil", 1)
    scores, PT_ready = sg("m_scores", C), sg("m_PT", C)
    intra, inter, local, state_ready, tot_ready = sg("m_intra", C), sg("m_inter", C - 1), sg("m_local", C - 1), sg("m_state", C - 1), sg("m_tot", C)
    ms_ready, rs0, h_ready = sg("m_ms", 1), sg("m_rs0", 2), sg("m_hready", 1)
    hT_t, hT_hi, hT_lo, x1_ready = sg("m_hTt", 2), sg("m_hThi", 2), sg("m_hTlo", 2), sg("m_x1", 1)
    NV, NP = 20, 0
    dve_sem, pool_sem = g.sems("m_dve"), g.sems("m_pool")
    gate_bank, q_bank, k_bank, kv_bank = [bank[2], bank[3]], bank[4], bank[5], [bank[6], bank[7]]
    og_bank, score_bank = [bank[0], bank[1]], [bank[0], bank[1]]
    tg_bank, gend_bank = bank[2], bank[3]
    intra_bank, inter_bank, local_bank = [bank[4], bank[5]], bank[6], bank[7]
    hT_bank, out_bank = [bank[2], bank[3]], [bank[0], bank[1]]
    per_head = lambda ap: ap.rearrange("p (h e) -> p h e", e=V1)
    block = nc.Block()
    with block:
        @block.sync
        def _(sp):
            with sp.Fori(0, B) as i:
                sp.wait_ge(rows_ready.sem, rows_ready.at(i, 1))
                dst = scratch[ds(i, 1), :, :].rearrange("o h s -> (o h) s")
                sp.dma_start(dst, row[7][:, :]).then_inc(stored.sem, 16)
                sp.wait_ge(stored.sem, stored.at(i, 16))
                src = scratch[ds(i, 1), :, :].rearrange("o h s -> o (h s)").to_broadcast([P, H * S])
                sp.dma_start(Gb[:, :, :].rearrange("p h s -> p (h s)"), src).then_inc(spread.sem, 16)

        @block.tensor
        def _(pe):
            pe.sem_inc(turns.sem, 1)
            with pe.Fori(0, B) as i:
                pe.wait_ge(turns.sem, turns.at(i))
                pe.wait_ge(y_ready.sem, y_ready.at(i, 1))
                for k in range(KD):
                    for c in range(C):
                        last = nc.tensor.transpose(bank[k][:, c * P:(c + 1) * P], ys[:, c, k * P:(k + 1) * P], ident[:, :])
                    last.then_inc(yT_t.sem, 1)
                pe.wait_ge(yT_lo.sem, yT_lo.at(i, KD))
                for n in range(2):
                    for k in range(KD):
                        last = product(nc, gate_bank[n][:, :], cut(wg, a, k, n), cut(yT, a, k), k == 0, k == KD - 1)
                    last.then_inc(gates.sem, 1)
                for o, cols in ((q_bank, Qc), (k_bank, Kc)):
                    for k in range(KD):
                        last = product(nc, o[:, :], cut(wp, a, k, cols), cut(yT, a, k), k == 0, k == KD - 1)
                    last.then_inc(qk.sem, 1)
                for c in range(C):
                    if c >= 2:
                        pe.wait_ge(kv_in.sem, kv_in.at(i, 2 * (c - 1)))
                    for k in range(KD):
                        last = product(nc, kv_bank[c % 2][:, 0:NKV], cut(yT, a, k, slice(c * P, (c + 1) * P)),
                                       cut(wp, a, k, slice(0, NKV)), k == 0, k == KD - 1)
                    last.then_inc(kv.sem, 1)
                for n in range(2):
                    for c in (2 * n, 2 * n + 1):
                        for k in range(KD):
                            last = product(nc, og_bank[n][:, c % 2 * D:(c % 2 + 1) * D], cut(yT, a, k, slice(c * P, (c + 1) * P)),
                                           cut(wp, a, k, Oc), k == 0 and c % 2 == 0, k == KD - 1)
                    last.then_inc(og.sem, 1)
                pe.wait_ge(rows_ready.sem, rows_ready.at(i, 2))
                pe.wait_ge(G_copied.sem, G_copied.at(i, 1))
                for c in range(C):
                    n = QUADS[2] + H
                    last = nc.tensor.transpose(tg_bank[:, c * P:c * P + n], gr[:, c * P:(c + 1) * P], ident[0:n, 0:n])
                last.then_inc(tg_ready.sem, 1)
                nc.tensor.matmul(gend_bank[:, 0:C], g.head_spread[:, :], row[7][:, P - 1::P], start=True, stop=True).then_inc(gend_ready.sem, 1)
                pe.wait_ge(qk_in.sem, qk_in.at(i, 2))
                pe.wait_ge(kv_in.sem, kv_in.at(i, 2 * C))
                pe.wait_ge(og_in.sem, og_in.at(i, 2))
                for c in range(C):
                    cols = slice(c * P, (c + 1) * P)
                    pe.wait_ge(q_spread.sem, q_spread.at(i, c + 1))
                    if c:
                        pe.wait_ge(PT_ready.sem, PT_ready.at(i, c))
                    for n in range(2):
                        last = nc.tensor.matmul(score_bank[n][:, :], kT[:, cols],
                                                qbd[c % 2][:, n * H // 2:(n + 1) * H // 2, :].rearrange("p h s -> p (h s)"),
                                                start=True, stop=True)
                    last.then_inc(scores.sem, 1)
                    if c:
                        pe.wait_ge(state_ready.sem, state_ready.at(i, c))
                        nc.tensor.matmul(inter_bank[:, 0:VW], qs[:, cols], state[:, :], start=True, stop=True).then_inc(inter.sem, 1)
                    if c < C - 1:
                        pe.wait_ge(ktil_ready.sem, ktil_ready.at(i, 1))
                        nc.tensor.matmul(local_bank[:, 0:VW], ktil[:, c, :], v1[:, c, :], start=True, stop=True).then_inc(local.sem, 1)
                    pe.wait_ge(PT_ready.sem, PT_ready.at(i, c + 1))
                    if c >= 2:
                        pe.wait_ge(tot_ready.sem, tot_ready.at(i, c - 1))
                    for h in range(H):
                        last = nc.tensor.matmul(intra_bank[c % 2][:, h * V1:(h + 1) * V1], PT[c % 2][:, h, :],
                                                v1[:, c, h * V1:(h + 1) * V1], start=True, stop=True)
                    last.then_inc(intra.sem, 1)
                pe.wait_ge(h_ready.sem, h_ready.at(i, 1))
                for k in range(KD):
                    for c in range(C):
                        last = nc.tensor.transpose(hT_bank[k][:, c * P:(c + 1) * P], hh[:, c, k * P:(k + 1) * P], ident[:, :])
                    last.then_inc(hT_t.sem, 1)
                pe.wait_ge(hT_lo.sem, hT_lo.at(i, KD))
                for c in range(C):
                    for k in range(KD):
                        last = product(nc, out_bank[c // 2][:, c % 2 * D:(c % 2 + 1) * D], cut(hT, a, k, slice(c * P, (c + 1) * P)),
                                       cut(wo, a, k), k == 0 and c % 2 == 0, k == KD - 1)
                last.then_inc(x1_ready.sem, 1)
                pe.nop().then_inc(turns.sem, 1)

        @block.scalar
        def _(act):
            act.sem_inc(turns.sem, 1)
            with act.Fori(0, B) as i:
                act.wait_ge(turns.sem, turns.at(i))
                for k in range(KD):
                    act.wait_ge(yT_t.sem, yT_t.at(i, k + 1))
                    nc.scalar.activation(yT[0][:, k, :], bank[k][:, :], ACT.Copy, scale=g.norm1_col[:, k:k + 1]).then_inc(yT_hi.sem, 1)
                for n in range(2):
                    act.wait_ge(gates.sem, gates.at(i, n + 1))
                    nc.scalar.activation(row[n][:, :], gate_bank[n][0:H, :], ACT.Tanh, bias=g.gate_bias15[:, n:n + 1], scale=1.0 / CAP).then_inc(tanhed.sem, 1)
                act.wait_ge(tanhed.sem, tanhed.at(i, 2))
                nc.scalar.activation(row[2][:, :], row[1][:, :], ACT.Exp, scale=-CAP).then_inc(u_ready.sem, 1)
                act.wait_ge(y1_ready.sem, y1_ready.at(i, 1))
                nc.scalar.activation(row[4][:, :], row[3][:, :], ACT.Ln).then_inc(ln_ready.sem, 1)
                act.wait_ge(ln_ready.sem, ln_ready.at(i, 1))
                nc.scalar.activation(row[5][:, :], row[4][:, :], ACT.Exp, scale=-1.0).then_inc(ln_ready.sem, 1)
                act.wait_ge(qk.sem, qk.at(i, 1))
                nc.scalar.activation(qs[:, :], q_bank[:, :], ACT.Copy, scale=float(DQ) ** -0.5).then_inc(qk_in.sem, 1)
                act.wait_ge(qk.sem, qk.at(i, 2))
                nc.scalar.activation(kT[:, :], k_bank[:, :], ACT.Copy).then_inc(qk_in.sem, 1)
                for c in range(C):
                    act.wait_ge(kv.sem, kv.at(i, c + 1))
                    nc.scalar.activation(ktok[:, c, :], kv_bank[c % 2][:, Kc], ACT.Copy).then_inc(kv_in.sem, 1)
                    nc.scalar.activation(per_head(v1[:, c, :])[:, :, 0:DV],
                                                  kv_bank[c % 2][:, Vc].rearrange("p (h e) -> p h e", e=DV), ACT.Copy).then_inc(kv_in.sem, 1)
                act.wait_ge(rows_ready.sem, rows_ready.at(i, 1))
                nc.scalar.activation(gr[QUADS[1]:QUADS[1] + H, :], row[7][:, :], ACT.Copy).then_inc(G_copied.sem, 1)
                for n in range(2):
                    act.wait_ge(og.sem, og.at(i, n + 1))
                    nc.scalar.activation(sig[:, 2 * n:2 * n + 2, :].rearrange("p c d -> p (c d)"), og_bank[n][:, :], ACT.Sigmoid).then_inc(og_in.sem, 1)
                act.wait_ge(tg_ready.sem, tg_ready.at(i, 1))
                nc.scalar.activation(tg[:, :, :], tg_bank[:, :].rearrange("p (c s) -> p c s", c=C)[:, :, 0:QUADS[2] + H], ACT.Copy).then_inc(tg_in.sem, 1)
                act.wait_ge(gend_ready.sem, gend_ready.at(i, 1))
                nc.scalar.activation(gend[:, :], gend_bank[:, 0:C], ACT.Copy).then_inc(tg_in.sem, 1)
                act.wait_ge(dec_ready.sem, dec_ready.at(i, 1))
                nc.scalar.activation(dexp[:, :], dec[:, :], ACT.Exp).then_inc(dexp_ready.sem, 1)
                act.wait_ge(ga_ready.sem, ga_ready.at(i, 1))
                nc.scalar.activation(ea[:, :, :, :].rearrange("p a c h -> p (a c h)"), ga_flat, ACT.Exp).then_inc(ea_ready.sem, 1)
                for c in range(C):
                    act.wait_ge(diff.sem, diff.at(i, c + 1))
                    w = pairw[c % 2][:, :, :].rearrange("p h s -> p (h s)")
                    nc.scalar.activation(w, w, ACT.Exp).then_inc(weight.sem, 1)
                act.wait_ge(ms_ready.sem, ms_ready.at(i, 1))
                nc.scalar.activation(den[3][:, :], den[2][:, :], ACT.Ln).then_inc(rs0.sem, 1)
                act.wait_ge(rs0.sem, rs0.at(i, 1))
                nc.scalar.activation(den[4][:, :], den[3][:, :], ACT.Exp, scale=-0.5).then_inc(rs0.sem, 1)
                for k in range(KD):
                    act.wait_ge(hT_t.sem, hT_t.at(i, k + 1))
                    nc.scalar.activation(hT[0][:, k, :], hT_bank[k][:, :], ACT.Copy, scale=g.mh_col[:, k:k + 1]).then_inc(hT_hi.sem, 1)
                act.nop().then_inc(turns.sem, 1)

        @block.gpsimd
        def _(pool):
            pool.sem_inc(turns.sem, 1)
            with pool.Fori(0, B) as i:
                pool.wait_ge(turns.sem, turns.at(i))
                steps = Steps(pool_sem, i, C)
                pool.wait_ge(qk_in.sem, qk_in.at(i, 1))

                def spread_q(c):
                    nc.gpsimd.tensor_tensor(
                        out=qbd[c % 2][:, :, :], in0=qs[:, c * P:(c + 1) * P].unsqueeze(1).to_broadcast([P, H, P]),
                        in1=expand(g.head_mask[:, :], P), op=ALU.mult).then_inc(q_spread.sem, 1)

                def differ(c):
                    nc.gpsimd.tensor_tensor(out=pairw[c % 2][:, :, :], in0=expand(tg[:, c, 0:H], P),
                                                  in1=Gb[:, :, c * P:(c + 1) * P], op=ALU.subtract).then_inc(steps.sem, steps.one())
                    pool.wait_ge(steps.sem, steps.done())
                    nc.gpsimd.tensor_tensor(out=pairw[c % 2][:, :, :], in0=pairw[c % 2][:, :, :],
                                                    in1=g.causal[:, :].unsqueeze(1).to_broadcast([P, H, P]), op=ALU.add).then_inc(diff.sem, 1)

                spread_q(0)
                spread_q(1)
                pool.wait_ge(tg_in.sem, tg_in.at(i, 1))
                pool.wait_ge(spread.sem, spread.at(i, 16))
                differ(0)
                pool.wait_ge(ea_ready.sem, ea_ready.at(i, 1))
                nc.gpsimd.tensor_tensor(
                    out=ktil[:, :, :].rearrange("p c (h d) -> p (c h) d", d=DQ), in0=ktok[:, :, :].rearrange("p c (h d) -> p (c h) d", d=DQ),
                    in1=expand(ea[:, 0, :, :].rearrange("p c h -> p (c h)"), DQ), op=ALU.mult).then_inc(ktil_ready.sem, 1)
                differ(1)
                for c in (2, 3):
                    pool.wait_ge(scores.sem, scores.at(i, c - 1))
                    spread_q(c)
                    pool.wait_ge(PT_ready.sem, PT_ready.at(i, c - 1))
                    differ(c)
                pool.nop().then_inc(turns.sem, 1)

        @block.vector
        def _(dve):
            dve.sem_inc(turns.sem, 1)
            with dve.Fori(0, B) as i:
                dve.wait_ge(turns.sem, turns.at(i))
                v = Steps(dve_sem, i, 31)
                for c in range(C):
                    last = nc.vector.tensor_scalar(out=ys[:, c, :], in0=g.xnf[:, ds((i * C + c) * D, D)],
                                                   scalar1=g.scale_y[:, ds(i * C + c, 1)], scalar2=None, op0=ALU.mult)
                    if c < C - 1:
                        last.then_inc(v.sem, v.one())
                last.then_inc(y_ready.sem, 1)
                for k in range(KD):
                    dve.wait_ge(yT_hi.sem, yT_hi.at(i, k + 1))
                    nc.vector.scalar_tensor_tensor(out=yT[1][:, k, :], in0=bank[k][:, :], scalar=g.norm1_col[:, k:k + 1],
                                                            in1=f32(yT[0][:, k, :]), op0=ALU.mult, op1=ALU.subtract).then_inc(yT_lo.sem, 1)
                dve.wait_ge(u_ready.sem, u_ready.at(i, 1))
                nc.vector.tensor_scalar(out=row[3][:, :], in0=row[2][:, :], scalar1=1.0, scalar2=None, op0=ALU.add).then_inc(y1_ready.sem, 1)
                dve.wait_ge(y1_ready.sem, y1_ready.at(i, 1))
                nc.vector.scalar_tensor_tensor(out=row[6][:, :], in0=row[3][:, :], scalar=1.0, in1=row[2][:, :], op0=ALU.subtract, op1=ALU.subtract).then_inc(v.sem, v.one())
                dve.wait_ge(ln_ready.sem, ln_ready.at(i, 2))
                dve.wait_ge(v.sem, v.done())
                nc.vector.tensor_tensor(out=row[6][:, :], in0=row[6][:, :], in1=row[5][:, :], op=ALU.mult).then_inc(v.sem, v.one())
                dve.wait_ge(v.sem, v.done())
                nc.vector.tensor_tensor(out=row[6][:, :], in0=row[4][:, :], in1=row[6][:, :], op=ALU.subtract).then_inc(v.sem, v.one())
                dve.wait_ge(v.sem, v.done())
                nc.vector.tensor_tensor_scan(out=row[8][:, :], data0=g.ones_row[:, :], data1=row[6][:, :], initial=0.0, op0=ALU.mult, op1=ALU.add).then_inc(v.sem, v.one())
                dve.wait_ge(v.sem, v.done())
                nc.vector.scalar_tensor_tensor(out=gr[0:H, :], in0=row[0][:, :], scalar=CAP, in1=row[8][:, :], op0=ALU.mult, op1=ALU.add).then_inc(v.sem, v.one())
                dve.wait_ge(v.sem, v.done())
                nc.vector.tensor_tensor_scan(out=row[7][:, :], data0=gr[0:H, :], data1=gr[0:H, :], initial=-3e38, op0=ALU.max, op1=ALU.max).then_inc(rows_ready.sem, 1)
                dve.wait_ge(rows_ready.sem, rows_ready.at(i, 1))
                nc.vector.tensor_tensor(out=gr[QUADS[2]:QUADS[2] + H, :], in0=row[8][:, :], in1=row[7][:, :], op=ALU.subtract).then_inc(rows_ready.sem, 1)
                dve.wait_ge(tg_in.sem, tg_in.at(i, 2))
                nc.vector.tensor_tensor(out=dec[:, :], in0=gend[:, 0:C - 1], in1=gend[:, 1:C], op=ALU.subtract).then_inc(dec_ready.sem, 1)
                dve.wait_ge(spread.sem, spread.at(i, 16))
                ends = Gb[:, :, P - 1::P].rearrange("p h c -> p c h")
                nc.vector.tensor_tensor(out=ga[:, 0, :, :], in0=tg[:, :, 0:H], in1=ends, op=ALU.subtract).then_inc(v.sem, v.one())
                nc.vector.tensor_tensor(out=ga[:, 1, 1:C, :], in0=ends[:, 0:C - 1, :], in1=tg[:, 1:C, QUADS[1]:QUADS[1] + H], op=ALU.subtract).then_inc(v.sem, v.one())
                nc.vector.tensor_copy(ga[:, 2, :, :], tg[:, :, QUADS[2]:QUADS[2] + H]).then_inc(ga_ready.sem, 1)
                dve.wait_ge(dexp_ready.sem, dexp_ready.at(i, 1))
                for c in range(C):
                    dve.wait_ge(scores.sem, scores.at(i, c + 1))
                    dve.wait_ge(weight.sem, weight.at(i, c + 1))
                    if c >= 2:
                        dve.wait_ge(intra.sem, intra.at(i, c - 1))
                    for n in range(2):
                        last = nc.vector.tensor_tensor(out=PT[c % 2][:, n * H // 2:(n + 1) * H // 2, :].rearrange("p h s -> p (h s)"),
                                                       in0=score_bank[n][:, :],
                                                       in1=pairw[c % 2][:, n * H // 2:(n + 1) * H // 2, :].rearrange("p h s -> p (h s)"), op=ALU.mult)
                        if n == 0:
                            last.then_inc(v.sem, v.one())
                    last.then_inc(PT_ready.sem, 1)
                    if c:
                        dve.wait_ge(inter.sem, inter.at(i, c))
                        nc.vector.tensor_tensor(out=per_head(tot[:, c, :]), in0=per_head(inter_bank[:, 0:VW]),
                                                  in1=expand(ea[:, 1, c, :], V1), op=ALU.mult).then_inc(v.sem, v.one())
                    if c < C - 1:
                        dve.wait_ge(local.sem, local.at(i, c + 1))
                        dst = state if c == 0 else part
                        last = nc.vector.tensor_tensor(out=per_head(dst[:, :]), in0=per_head(local_bank[:, 0:VW]),
                                                       in1=expand(g.head_mask[:, :], V1), op=ALU.mult)
                        if c == 0:
                            last.then_inc(state_ready.sem, 1)
                        else:
                            last.then_inc(v.sem, v.one())
                            dve.wait_ge(v.sem, v.done())
                            nc.vector.scalar_tensor_tensor(out=state[:, :], in0=state[:, :], scalar=dexp[:, c - 1:c],
                                                                          in1=part[:, :], op0=ALU.mult, op1=ALU.add).then_inc(state_ready.sem, 1)
                    dve.wait_ge(intra.sem, intra.at(i, c + 1))
                    if c == 0:
                        nc.vector.tensor_copy(tot[:, 0, :], intra_bank[0][:, 0:VW]).then_inc(tot_ready.sem, 1)
                    else:
                        dve.wait_ge(v.sem, v.done())
                        nc.vector.tensor_tensor(out=tot[:, c, :], in0=intra_bank[c % 2][:, 0:VW], in1=tot[:, c, :], op=ALU.add).then_inc(tot_ready.sem, 1)
                dve.wait_ge(tot_ready.sem, tot_ready.at(i, C))
                th = tot[:, :, :].rearrange("p c (h e) -> p (c h) e", e=V1)
                per = lambda t: t[:, :, :].rearrange("p c (h d) -> p (c h) d", d=DV)
                nc.vector.scalar_tensor_tensor(out=den[0][:, :], in0=th[:, :, DV], scalar=-1.0, in1=th[:, :, DV], op0=ALU.mult, op1=ALU.max).then_inc(v.sem, v.one())
                dve.wait_ge(v.sem, v.done())
                nc.vector.tensor_tensor(out=den[1][:, :], in0=den[0][:, :], in1=ea[:, 2, :, :].rearrange("p c h -> p (c h)"), op=ALU.max).then_inc(v.sem, v.one())
                dve.wait_ge(v.sem, v.done())
                nc.vector.reciprocal(out=den[0][:, :], in_=den[1][:, :]).then_inc(v.sem, v.one())
                dve.wait_ge(v.sem, v.done())
                nc.vector.tensor_tensor(out=per(hh), in0=th[:, :, 0:DV], in1=expand(den[0][:, :], DV), op=ALU.mult).then_inc(v.sem, v.one())
                dve.wait_ge(v.sem, v.done())
                nc.vector.tensor_tensor(out=per(sq), in0=per(hh), in1=per(hh), op=ALU.mult).then_inc(v.sem, v.one())
                dve.wait_ge(v.sem, v.done())
                nc.vector.tensor_reduce(out=den[1][:, :], in_=per(sq), op=ALU.add, axis=AX.X).then_inc(v.sem, v.one())
                dve.wait_ge(v.sem, v.done())
                nc.vector.tensor_scalar(out=den[2][:, :], in0=den[1][:, :], scalar1=1.0 / DV, scalar2=1e-6, op0=ALU.mult, op1=ALU.add).then_inc(ms_ready.sem, 1)
                dve.wait_ge(rs0.sem, rs0.at(i, 2))
                nc.vector.tensor_tensor(out=den[5][:, :], in0=den[4][:, :], in1=den[4][:, :], op=ALU.mult).then_inc(v.sem, v.one())
                dve.wait_ge(v.sem, v.done())
                nc.vector.tensor_tensor(out=den[6][:, :], in0=den[5][:, :], in1=den[2][:, :], op=ALU.mult).then_inc(v.sem, v.one())
                dve.wait_ge(v.sem, v.done())
                nc.vector.tensor_scalar(out=den[5][:, :], in0=den[6][:, :], scalar1=-0.5, scalar2=1.5, op0=ALU.mult, op1=ALU.add).then_inc(v.sem, v.one())
                dve.wait_ge(v.sem, v.done())
                nc.vector.tensor_tensor(out=den[6][:, :], in0=den[5][:, :], in1=den[4][:, :], op=ALU.mult).then_inc(v.sem, v.one())
                dve.wait_ge(v.sem, v.done())
                nc.vector.tensor_tensor(out=per(sq), in0=per(hh), in1=expand(den[6][:, :], DV), op=ALU.mult).then_inc(v.sem, v.one())
                dve.wait_ge(v.sem, v.done())
                nc.vector.tensor_tensor(out=hh[:, :, :], in0=sq[:, :, :], in1=sig[:, :, :], op=ALU.mult).then_inc(h_ready.sem, 1)
                for k in range(KD):
                    dve.wait_ge(hT_hi.sem, hT_hi.at(i, k + 1))
                    nc.vector.scalar_tensor_tensor(out=hT[1][:, k, :], in0=hT_bank[k][:, :], scalar=g.mh_col[:, k:k + 1],
                                                            in1=f32(hT[0][:, k, :]), op0=ALU.mult, op1=ALU.subtract).then_inc(hT_lo.sem, 1)
                dve.wait_ge(x1_ready.sem, x1_ready.at(i, 1))
                for n in range(2):
                    at = g.xnf[:, ds(i * C * D + n * 2 * D, 2 * D)]
                    last = nc.vector.tensor_tensor(out=at, in0=out_bank[n][:, :], in1=at, op=ALU.add)
                    if n == 0:
                        last.then_inc(v.sem, v.one())
                last.then_inc(turns.sem, 1)
                v.close("mlstm dve")


def mlp_phase(nc, g, w_gate, w_up, w_down):
    bank, ident = g.bank, g.ident
    a = slice(None)
    m = Map(nc, g.W0)
    wgu = m.pair("p_wgu", [P, KD, 2, FF])
    wd = m.pair("p_wd", [P, NF, D])
    r = Map(nc, m.at)
    rgu, rd = r("p_rgu", [P, KD, 2, FF]), r("p_rd", [P, NF, D])
    rows = lambda w: w.rearrange("(k p) n -> p k n", p=P)
    loads = [(rgu[:, :, 0, :], rows(w_gate)), (rgu[:, :, 1, :], rows(w_up)), (rd[:, :, :], rows(w_down))]
    pieces = [Piece(wgu[0][:, k, n, :], wgu[1][:, k, n, :], raw=rgu[:, k, n, :]) for k in range(KD) for n in range(2)]
    pieces += [Piece(wd[0][:, n:n + 4, :], wd[1][:, n:n + 4, :], raw=rd[:, n:n + 4, :]) for n in (0, 4)]
    prepare(nc, g.sems, "mlp_w", bank, ident, loads, [], pieces)

    junk, ys = m("p_junk", [P, D]), m("p_ys", [P, C, D])
    sq, ms, rs = m("p_sq", [P, C]), m("p_ms", [P, C]), m("p_rs", [P, C])
    yT = m.pair("p_yT", [P, KD, S])
    hid = Hidden(nc, g, "p", NF, m)
    turns = Turns(g.sems("p_turns"))
    sg = g.counted
    squared, ms_ready, powed, y_ready = sg("p_sq", C), sg("p_ms", 1), sg("p_pow", 1), sg("p_y", 1)
    yT_t, yT_hi, yT_lo, added, acc_done = sg("p_yTt", 2), sg("p_yThi", 2), sg("p_yTlo", 2), sg("p_added", 1), sg("p_acc", 1)
    dve_sem = g.sems("p_dve")
    acc = [bank[6], bank[7]]
    gate, up = (lambda u: bank[0 if u % 2 == 0 else 2]), (lambda u: bank[1 if u % 2 == 0 else 3])
    turn_bank = [bank[4], bank[5]]
    block = nc.Block()
    with block:
        @block.tensor
        def _(pe):
            pe.sem_inc(turns.sem, 1)

            def down(i, u):
                h = hid.unit(u)
                pe.wait_ge(hid.lo.sem, hid.lo.at(i, u + 1))
                for c in range(C):
                    last = product(nc, acc[c // 2][:, c % 2 * D:(c % 2 + 1) * D], cut(h, a, slice(c * P, (c + 1) * P)),
                                   cut(wd, a, u), u == 0 and c % 2 == 0, u == NF - 1)
                last.then_inc(hid.down.sem, 1)
                return last

            with pe.Fori(0, B) as i:
                pe.wait_ge(turns.sem, turns.at(i))
                pe.wait_ge(y_ready.sem, y_ready.at(i, 1))
                for k in range(KD):
                    for c in range(C):
                        last = nc.tensor.transpose(turn_bank[k][:, c * P:(c + 1) * P], ys[:, c, k * P:(k + 1) * P], ident[:, :])
                    last.then_inc(yT_t.sem, 1)
                pe.wait_ge(yT_lo.sem, yT_lo.at(i, KD))
                for u in range(NF):
                    if u >= 2:
                        pe.wait_ge(hid.hidden.sem, hid.hidden.at(i, u - 1))
                    for n, o in ((0, gate(u)), (1, up(u))):
                        for k in range(KD):
                            last = product(nc, o[:, :], cut(wgu, a, k, n, slice(u * P, (u + 1) * P)), cut(yT, a, k), k == 0, k == KD - 1)
                    last.then_inc(hid.gate_up.sem, 1)
                    if u >= 2:
                        down(i, u - 2)
                down(i, NF - 2)
                down(i, NF - 1)
                pe.nop().then_inc(turns.sem, 1)

        @block.scalar
        def _(act):
            act.sem_inc(turns.sem, 1)
            with act.Fori(0, B) as i:
                act.wait_ge(turns.sem, turns.at(i))
                for c in range(C):
                    if c:
                        act.wait_ge(squared.sem, squared.at(i, c))
                    nc.scalar.activation(junk[:, :], g.xnf[:, ds((i * C + c) * D, D)], ACT.Square, accum_out=sq[:, c:c + 1]).then_inc(squared.sem, 1)
                for k in range(KD):
                    act.wait_ge(yT_t.sem, yT_t.at(i, k + 1))
                    nc.scalar.activation(yT[0][:, k, :], turn_bank[k][:, :], ACT.Copy, scale=g.norm2_col[:, k:k + 1]).then_inc(yT_hi.sem, 1)
                for u in range(NF):
                    hid.act_silu(act, i, u, gate(u)[:, :])
                    if u:
                        hid.act_hi(act, i, u - 1)
                hid.act_hi(act, i, NF - 1)
                act.nop().then_inc(turns.sem, 1)

        @block.gpsimd
        def _(pool):
            pool.sem_inc(turns.sem, 1)
            with pool.Fori(0, B) as i:
                pool.wait_ge(turns.sem, turns.at(i))
                pool.wait_ge(ms_ready.sem, ms_ready.at(i, 1))
                nc.gpsimd.tensor_tensor(out=rs[:, :], in0=ms[:, :], in1=g.minus_half[:, 0:C], op=ALU.pow).then_inc(powed.sem, 1)
                at = g.res[:, ds(i * C * D, C * D)]
                nc.gpsimd.tensor_tensor(out=at, in0=at, in1=g.xnf[:, ds(i * C * D, C * D)], op=ALU.add).then_inc(added.sem, 1)
                pool.nop().then_inc(turns.sem, 1)

        @block.vector
        def _(dve):
            dve.sem_inc(turns.sem, 1)
            with dve.Fori(0, B) as i:
                dve.wait_ge(turns.sem, turns.at(i))
                v = Steps(dve_sem, i, C)
                dve.wait_ge(squared.sem, squared.at(i, C))
                nc.vector.tensor_scalar(out=ms[:, :], in0=sq[:, :], scalar1=1.0 / D, scalar2=1e-6, op0=ALU.mult, op1=ALU.add).then_inc(ms_ready.sem, 1)
                dve.wait_ge(powed.sem, powed.at(i, 1))
                for c in range(C):
                    last = nc.vector.tensor_scalar(out=ys[:, c, :], in0=g.xnf[:, ds((i * C + c) * D, D)], scalar1=rs[:, c:c + 1],
                                                   scalar2=None, op0=ALU.mult)
                    if c < C - 1:
                        last.then_inc(v.sem, v.one())
                last.then_inc(y_ready.sem, 1)
                for k in range(KD):
                    dve.wait_ge(yT_hi.sem, yT_hi.at(i, k + 1))
                    nc.vector.scalar_tensor_tensor(out=yT[1][:, k, :], in0=turn_bank[k][:, :], scalar=g.norm2_col[:, k:k + 1],
                                                            in1=f32(yT[0][:, k, :]), op0=ALU.mult, op1=ALU.subtract).then_inc(yT_lo.sem, 1)
                for u in range(NF):
                    hid.dve_hidden(dve, i, u, up(u)[:, :])
                    if u:
                        hid.dve_lo(dve, i, u - 1)
                hid.dve_lo(dve, i, NF - 1)
                dve.wait_ge(added.sem, added.at(i, 1))
                dve.wait_ge(hid.down.sem, hid.down.at(i, NF))
                for n in range(2):
                    at = g.res[:, ds(i * C * D + n * 2 * D, 2 * D)]
                    last = nc.vector.tensor_tensor(out=at, in0=acc[n][:, :], in1=at, op=ALU.add)
                    if n == 0:
                        last.then_inc(v.sem, v.one())
                last.then_inc(turns.sem, 1)
                v.close("mlp dve")


def layer1_phase(nc, g, wqkv, wo1, w1_gate, w1_up, w1_down, out):
    bank, ident = g.bank, g.ident
    a = slice(None)
    bf16 = mybir.dt.bfloat16
    L = B
    GP = 4
    NG = NF // GP
    m = Map(nc, g.W0)
    wqv = m.pair("l_wqv", [P, KD, 3 * D])
    wo = m.pair("l_wo", [P, KD, D])
    wgu = m.pair("l_wgu", [P, KD, 2, GP, FF // GP])
    wd = m.pair("l_wd", [P, NG, GP, D])
    r = Map(nc, m.at)
    rq, ro = r("l_rq", [P, 3 * D // P, D]), r("l_ro", [P, KD, D])
    rgu, rd = r("l_rgu", [P, KD, 2, FF]), r("l_rd", [P, NG, GP, D])
    rows = lambda w: w.rearrange("(k p) n -> p k n", p=P)
    loads = [(rq[:, :, :], rows(wqkv)), (ro[:, :, :], rows(wo1)), (rgu[:, :, 0, :], rows(w1_gate)), (rgu[:, :, 1, :], rows(w1_up)),
             (rd[:, :, :, :], w1_down.rearrange("(c p j) n -> p c j n", p=P, j=GP))]
    pieces = []
    for k in range(KD):
        cols = slice(k * P, (k + 1) * P)
        pieces.append(Piece(wqv[0][:, k, 0:4 * P], wqv[1][:, k, 0:4 * P], turned=[rq[:, b, cols] for b in range(4)]))
        pieces.append(Piece(wqv[0][:, k, 4 * P:6 * P], wqv[1][:, k, 4 * P:6 * P], turned=[rq[:, b, cols] for b in (4, 5)]))
        pieces.append(Piece(wo[0][:, k, :], wo[1][:, k, :], turned=[ro[:, b, cols] for b in range(KD)]))
    for k in range(KD):
        for n in range(2):
            pieces.append(Piece(wgu[0][:, k, n], wgu[1][:, k, n], raw=rgu[:, k, n, :].rearrange("p (q j) -> p j q", j=GP)))
    pieces += [Piece(wd[0][:, n], wd[1][:, n], raw=rd[:, n]) for n in range(NG)]

    sc = m("l_sc", [P, L, L, H1])

    preset = g.sems("l_preset")
    prepare(nc, g.sems, "l_w", bank, ident, loads, [], pieces)

    xs = m("l_xs", [P, L, D])
    o = xs
    st, mv = m("l_st", [P, L, 6]), m("l_mv", [P, L, 2])
    tiny = [m(f"l_tiny{n}", [P, L]) for n in range(4)]
    vv, rstd = m("l_vv", [P, L]), m("l_rstd", [P, L])
    xT = m.pair("l_xT", [P, KD, S])
    oT = m.pair("l_oT", [P, KD, S])
    q3, k3, v3 = m("l_q", [P, L, D]), m("l_k", [P, L, D]), m("l_v", [P, L, D])
    prod = [m(f"l_prod{n}", [P, L * D]) for n in range(2)]
    e3 = m("l_e", [P, L, L, H1])
    mx, sm, rc = m("l_mx", [P, L, H1]), m("l_sm", [P, L, H1]), m("l_rc", [P, L, H1])
    sb = [m(f"l_s{n}", [P, S]) for n in range(2)]
    h = [[m(f"l_h{c}{j}", [P, S]) for j in range(GP)] for c in range(NG)]
    ab = [m(f"l_ab{j}", [P, S]) for j in range(GP)]
    half = lambda name: m(name, [P, S // 2])
    ge = {}
    for x, y in ((0, 1), (0, 2), (0, 3), (1, 2), (1, 3), (2, 3)):
        ge[x, y] = half(f"l_ge{x}{y}")[:, :].bitcast(bf16)
    votes = [half(f"l_votes{j}")[:, :].bitcast(bf16) for j in range(GP)]
    ring = [m.pair(f"l_ring{j}", [P, S]) for j in range(GP)]
    sg = g.counted
    turns = Turns(g.sems("l_turns"))
    stats, powed, x_ready = sg("l_stats", 1), sg("l_pow", 1), sg("l_x", 1)
    xT_t, xT_hi, xT_lo = sg("l_xTt", 2), sg("l_xThi", 2), sg("l_xTlo", 2)
    qkv, qkv_in = sg("l_qkv", L), sg("l_qkvin", 3 * L)
    prods, reduced, centred, exped, probs = sg("l_prods", L), sg("l_red", L), sg("l_cent", 1), sg("l_exp", 1), sg("l_probs", 1)
    weighted, summed = sg("l_weighted", L), sg("l_summed", L)
    oT_t, oT_hi, oT_lo = sg("l_oTt", 2), sg("l_oThi", 2), sg("l_oTlo", 2)
    gate_up, silu, hidden, absed = sg("l_gu", NF), sg("l_silu", NF), sg("l_hid", NF), sg("l_abs", NF)
    compared, voted, kept, hi, lo, down = sg("l_ge", 6 * NG), sg("l_voted", NF), sg("l_kept", NF), sg("l_hi", NF), sg("l_lo", NF), sg("l_down", NF)
    acc_done, out_ready, stored = sg("l_acc", 1), sg("l_out", 1), sg("l_stored", 16)
    dve_sem, pool_sem = g.sems("l_dve"), g.sems("l_pool")
    acc, turn_bank = [bank[6], bank[7]], [bank[4], bank[5]]
    gate, up = (lambda u: bank[0 if u % 2 == 0 else 2]), (lambda u: bank[1 if u % 2 == 0 else 3])
    res4 = g.res.rearrange("p (l c d) -> p l c d", l=L, c=C)
    out4 = out.rearrange("l (c p) d -> p l c d", p=P)
    heads = lambda ap: ap.rearrange("p (h d) -> p h d", d=DH1)
    block = nc.Block()
    with block:
        @block.sync
        def _(sp):
            with sp.Fori(0, C) as i:
                sp.wait_ge(out_ready.sem, out_ready.at(i, 1))
                for l in range(L):
                    sp.dma_start(out4[:, l, ds(i, 1), :], res4[:, l, ds(i, 1), :]).then_inc(stored.sem, 16)
            sp.wait_ge(stored.sem, 16 * L * C)

        @block.tensor
        def _(pe):
            pe.sem_inc(turns.sem, 1)

            def downs(i, c):
                for j in range(GP):
                    u = c * GP + j
                    pe.wait_ge(lo.sem, lo.at(i, u + 1))
                    for l in range(L):
                        last = product(nc, acc[l // 2][:, l % 2 * D:(l % 2 + 1) * D], cut(ring[j], a, slice(l * P, (l + 1) * P)),
                                       cut(wd, a, c, j), u == 0 and l % 2 == 0, u == NF - 1)
                    last.then_inc(down.sem, 1)

            with pe.Fori(0, C) as i:
                pe.wait_ge(turns.sem, turns.at(i))
                pe.wait_ge(x_ready.sem, x_ready.at(i, 1))
                for k in range(KD):
                    for l in range(L):
                        last = nc.tensor.transpose(turn_bank[k][:, l * P:(l + 1) * P], xs[:, l, k * P:(k + 1) * P], ident[:, :])
                    last.then_inc(xT_t.sem, 1)
                pe.wait_ge(xT_lo.sem, xT_lo.at(i, KD))
                for l in range(L):
                    for k in range(KD):
                        product(nc, bank[l][:, :], cut(xT, a, k, slice(l * P, (l + 1) * P)), cut(wqv, a, k, slice(0, 2 * D)), k == 0, k == KD - 1)
                    for k in range(KD):
                        last = product(nc, turn_bank[l // 2][:, l % 2 * D:(l % 2 + 1) * D], cut(xT, a, k, slice(l * P, (l + 1) * P)),
                                       cut(wqv, a, k, slice(2 * D, 3 * D)), k == 0 and l % 2 == 0, k == KD - 1)
                    last.then_inc(qkv.sem, 1)
                for u in range(NF):
                    if u < 2:
                        pe.wait_ge(qkv_in.sem, qkv_in.at(i, 6 * (u + 1)))
                    else:
                        pe.wait_ge(hidden.sem, hidden.at(i, u - 1))
                    for n, b in ((0, gate(u)), (1, up(u))):
                        for k in range(KD):
                            c, j = u // GP, u % GP
                            last = product(nc, b[:, :], cut(wgu, a, k, n, j, slice(c * P, (c + 1) * P)), cut(xT, a, k), k == 0, k == KD - 1)
                    last.then_inc(gate_up.sem, 1)
                downs(i, 0)
                pe.wait_ge(summed.sem, summed.at(i, L))
                for k in range(KD):
                    for l in range(L):
                        last = nc.tensor.transpose(turn_bank[k][:, l * P:(l + 1) * P], o[:, l, k * P:(k + 1) * P], ident[:, :])
                    last.then_inc(oT_t.sem, 1)
                pe.wait_ge(oT_lo.sem, oT_lo.at(i, KD))
                for l in range(L):
                    for k in range(KD):
                        product(nc, acc[l // 2][:, l % 2 * D:(l % 2 + 1) * D], cut(oT, a, k, slice(l * P, (l + 1) * P)), cut(wo, a, k), False, False)
                downs(i, 1)
                pe.nop().then_inc(turns.sem, 1)

        @block.scalar
        def _(act):
            act.sem_inc(turns.sem, 1)

            def act_silu(i, u):
                act.wait_ge(gate_up.sem, gate_up.at(i, u + 1))
                if u >= 2:
                    act.wait_ge(hidden.sem, hidden.at(i, u - 1))
                nc.scalar.activation(sb[u % 2][:, :], gate(u)[:, :], ACT.Silu).then_inc(silu.sem, 1)

            def act_abs(i, u):
                act.wait_ge(hidden.sem, hidden.at(i, u + 1))
                if u >= GP:
                    act.wait_ge(compared.sem, compared.at(i, 6))
                nc.scalar.activation(ab[u % GP][:, :], h[u // GP][u % GP][:, :], ACT.Abs).then_inc(absed.sem, 1)

            def act_hi(i, u):
                act.wait_ge(kept.sem, kept.at(i, u + 1))
                if u >= GP:
                    act.wait_ge(down.sem, down.at(i, u + 1 - GP))
                nc.scalar.activation(ring[u % GP][0][:, :], h[u // GP][u % GP][:, :], ACT.Copy).then_inc(hi.sem, 1)

            with act.Fori(0, C) as i:
                act.wait_ge(turns.sem, turns.at(i))
                for k in range(KD):
                    act.wait_ge(xT_t.sem, xT_t.at(i, k + 1))
                    nc.scalar.activation(xT[0][:, k, :], turn_bank[k][:, :], ACT.Copy).then_inc(xT_hi.sem, 1)
                for l in range(L):
                    act.wait_ge(qkv.sem, qkv.at(i, l + 1))
                    nc.scalar.activation(q3[:, l, :], bank[l][:, 0:D], ACT.Copy, scale=float(DH1) ** -0.5).then_inc(qkv_in.sem, 1)
                    nc.scalar.activation(k3[:, l, :], bank[l][:, D:2 * D], ACT.Copy).then_inc(qkv_in.sem, 1)
                    if l % 2:
                        for x in (l - 1, l):
                            nc.scalar.activation(v3[:, x, :], turn_bank[l // 2][:, x % 2 * D:(x % 2 + 1) * D], ACT.Copy).then_inc(qkv_in.sem, 1)
                act_silu(i, 0)
                act_silu(i, 1)
                for u in range(2, 6):
                    act_abs(i, u - 2)
                    act_silu(i, u)
                act.wait_ge(centred.sem, centred.at(i, 1))
                nc.scalar.activation(e3[:, :, :, :].rearrange("p l m h -> p (l m h)"),
                                              e3[:, :, :, :].rearrange("p l m h -> p (l m h)"), ACT.Exp).then_inc(exped.sem, 1)
                act_silu(i, 6)
                act_silu(i, 7)
                for j in range(GP):
                    act_abs(i, GP + j)
                    act_hi(i, j)
                for k in range(KD):
                    act.wait_ge(oT_t.sem, oT_t.at(i, k + 1))
                    nc.scalar.activation(oT[0][:, k, :], turn_bank[k][:, :], ACT.Copy).then_inc(oT_hi.sem, 1)
                for j in range(GP):
                    act_hi(i, GP + j)
                act.nop().then_inc(turns.sem, 1)

        @block.gpsimd
        def _(pool):
            pool.sem_inc(turns.sem, 1)
            nc.gpsimd.memset(sc[:, :, :, :].rearrange("p l m h -> p (l m h)"), -1e30).then_inc(preset, 1)

            def votes_of(i, c, steps):
                first = 6 * c
                for n, (x, y, z, f1, f2) in enumerate((((0, 1), (0, 2), (0, 3), ALU.add, ALU.add), ((1, 2), (1, 3), (0, 1), ALU.add, ALU.subtract),
                                                       ((0, 2), (1, 2), (2, 3), ALU.add, ALU.subtract), ((0, 3), (1, 3), (2, 3), ALU.add, ALU.add))):
                    pool.wait_ge(compared.sem, compared.at(i, first + 6))
                    if c:
                        pool.wait_ge(kept.sem, kept.at(i, GP))
                    nc.gpsimd.tensor_tensor(out=votes[n], in0=ge[x], in1=ge[y], op=f1).then_inc(steps.sem, steps.one())
                    pool.wait_ge(steps.sem, steps.done())
                    nc.gpsimd.tensor_tensor(out=votes[n], in0=votes[n], in1=ge[z], op=f2).then_inc(voted.sem, 1)

            with pool.Fori(0, C) as i:
                pool.wait_ge(turns.sem, turns.at(i))
                steps = Steps(pool_sem, i, NF)
                pool.wait_ge(stats.sem, stats.at(i, 1))
                nc.gpsimd.tensor_tensor(out=rstd[:, :], in0=vv[:, :], in1=g.minus_half[:, 0:L], op=ALU.pow).then_inc(powed.sem, 1)
                for l in range(L):
                    pool.wait_ge(qkv_in.sem, qkv_in.at(i, 6 * (l // 2) + 2 * (l % 2) + 2))
                    if l >= 2:
                        pool.wait_ge(reduced.sem, reduced.at(i, l - 1))
                    nc.gpsimd.tensor_tensor(out=prod[l % 2][:, 0:(l + 1) * D].rearrange("p (m e) -> p m e", e=D),
                                                     in0=q3[:, l, :].unsqueeze(1).to_broadcast([P, l + 1, D]), in1=k3[:, 0:l + 1, :], op=ALU.mult).then_inc(prods.sem, 1)
                votes_of(i, 0, steps)
                pool.wait_ge(probs.sem, probs.at(i, 1))
                for l in range(L):
                    if l >= 2:
                        pool.wait_ge(summed.sem, summed.at(i, l - 1))
                    nc.gpsimd.tensor_tensor(
                        out=prod[l % 2][:, 0:(l + 1) * D].rearrange("p (x d) -> p x d", d=DH1),
                        in0=expand(e3[:, l, 0:l + 1, :].rearrange("p m h -> p (m h)"), DH1),
                        in1=v3[:, 0:l + 1, :].rearrange("p m (h d) -> p (m h) d", d=DH1), op=ALU.mult).then_inc(weighted.sem, 1)
                votes_of(i, 1, steps)
                pool.nop().then_inc(turns.sem, 1)

        @block.vector
        def _(dve):
            dve.sem_inc(turns.sem, 1)
            dve.wait_ge(preset, 1)
            with dve.Fori(0, C) as i:
                dve.wait_ge(turns.sem, turns.at(i))
                v = Steps(dve_sem, i, 23)
                for l in range(L):
                    nc.vector.bn_stats(out=st[:, l, :], in_=g.res[:, ds((l * C) * D + i * D, D)]).then_inc(v.sem, v.one())
                dve.wait_ge(v.sem, v.done())
                moments(nc, v, st, mv, tiny)
                nc.vector.tensor_scalar(out=vv[:, :], in0=mv[:, :, 1], scalar1=1e-5, scalar2=None, op0=ALU.add).then_inc(stats.sem, 1)
                dve.wait_ge(powed.sem, powed.at(i, 1))
                for l in range(L):
                    last = nc.vector.tensor_scalar(out=xs[:, l, :], in0=g.res[:, ds((l * C) * D + i * D, D)], scalar1=mv[:, l, 0:1],
                                                   scalar2=rstd[:, l:l + 1], op0=ALU.subtract, op1=ALU.mult)
                    if l < L - 1:
                        last.then_inc(v.sem, v.one())
                last.then_inc(x_ready.sem, 1)
                for k in range(KD):
                    dve.wait_ge(xT_hi.sem, xT_hi.at(i, k + 1))
                    nc.vector.tensor_tensor(out=xT[1][:, k, :], in0=turn_bank[k][:, :], in1=f32(xT[0][:, k, :]), op=ALU.subtract).then_inc(xT_lo.sem, 1)

                def times(u):
                    dve.wait_ge(silu.sem, silu.at(i, u + 1))
                    nc.vector.tensor_tensor(out=h[u // GP][u % GP][:, :], in0=sb[u % 2][:, :], in1=up(u)[:, :], op=ALU.mult).then_inc(hidden.sem, 1)

                def reduce_scores(l):
                    dve.wait_ge(prods.sem, prods.at(i, l + 1))
                    nc.vector.tensor_reduce(out=sc[:, l, 0:l + 1, :].rearrange("p m h -> p (m h)"),
                                                       in_=prod[l % 2][:, 0:(l + 1) * D].rearrange("p (x d) -> p x d", d=DH1), op=ALU.add, axis=AX.X).then_inc(reduced.sem, 1)

                def compare(c, x, y):
                    dve.wait_ge(absed.sem, absed.at(i, c * GP + GP))
                    if c:
                        dve.wait_ge(voted.sem, voted.at(i, GP))
                    nc.vector.tensor_tensor(out=ge[x, y], in0=ab[x][:, :], in1=ab[y][:, :], op=ALU.is_ge).then_inc(compared.sem, 1)

                def keep(c, j):
                    least, how = ((2.0, ALU.is_ge), (1.0, ALU.is_ge), (0.0, ALU.is_le), (1.0, ALU.is_le))[j]
                    dve.wait_ge(voted.sem, voted.at(i, c * GP + j + 1))
                    x = h[c][j][:, :]
                    nc.vector.scalar_tensor_tensor(out=x, in0=votes[j], scalar=least, in1=x, op0=how, op1=ALU.mult).then_inc(kept.sem, 1)

                def low(c, j):
                    dve.wait_ge(hi.sem, hi.at(i, c * GP + j + 1))
                    nc.vector.tensor_tensor(out=ring[j][1][:, :], in0=h[c][j][:, :], in1=f32(ring[j][0][:, :]), op=ALU.subtract).then_inc(lo.sem, 1)

                def by_head(t):
                    return t[:, :, :, :].rearrange("p l m h -> p l h m")

                for u in (0, 1, 2):
                    times(u)
                reduce_scores(0)
                reduce_scores(1)
                times(3)
                reduce_scores(2)
                reduce_scores(3)
                times(4)
                dve.wait_ge(reduced.sem, reduced.at(i, L))
                nc.vector.tensor_reduce(out=mx[:, :, :], in_=by_head(sc), op=ALU.max, axis=AX.X).then_inc(v.sem, v.one())
                dve.wait_ge(v.sem, v.done())
                last = None
                for l in range(L):
                    last = nc.vector.tensor_tensor(out=e3[:, l, :, :], in0=sc[:, l, :, :], in1=mx[:, l, :].unsqueeze(1).to_broadcast([P, L, H1]), op=ALU.subtract)
                    if l < L - 1:
                        last.then_inc(v.sem, v.one())
                last.then_inc(centred.sem, 1)
                times(5)
                for x, y in ((0, 1), (0, 2), (0, 3), (1, 2)):
                    compare(0, x, y)
                dve.wait_ge(exped.sem, exped.at(i, 1))
                nc.vector.tensor_reduce(out=sm[:, :, :], in_=by_head(e3), op=ALU.add, axis=AX.X).then_inc(v.sem, v.one())
                dve.wait_ge(v.sem, v.done())
                nc.vector.reciprocal(out=rc[:, :, :].rearrange("p l h -> p (l h)"), in_=sm[:, :, :].rearrange("p l h -> p (l h)")).then_inc(v.sem, v.one())
                compare(0, 1, 3)
                compare(0, 2, 3)
                dve.wait_ge(v.sem, v.done())
                for l in range(L):
                    last = nc.vector.tensor_tensor(out=e3[:, l, :, :], in0=e3[:, l, :, :], in1=rc[:, l, :].unsqueeze(1).to_broadcast([P, L, H1]), op=ALU.mult)
                    if l < L - 1:
                        last.then_inc(v.sem, v.one())
                last.then_inc(probs.sem, 1)
                times(6)
                times(7)
                for j in range(GP):
                    keep(0, j)
                for j in range(GP):
                    low(0, j)
                for x, y in ge:
                    compare(1, x, y)
                for l in range(L):
                    dve.wait_ge(weighted.sem, weighted.at(i, l + 1))
                    nc.vector.tensor_reduce(out=o[:, l, :], in_=prod[l % 2][:, 0:(l + 1) * D].rearrange("p (m e) -> p e m", e=D),
                                                      op=ALU.add, axis=AX.X).then_inc(summed.sem, 1)
                for k in range(KD):
                    dve.wait_ge(oT_hi.sem, oT_hi.at(i, k + 1))
                    nc.vector.tensor_tensor(out=oT[1][:, k, :], in0=turn_bank[k][:, :], in1=f32(oT[0][:, k, :]), op=ALU.subtract).then_inc(oT_lo.sem, 1)
                for j in range(GP):
                    keep(1, j)
                for j in range(GP):
                    low(1, j)
                dve.wait_ge(down.sem, down.at(i, NF))
                for n in range(2):
                    at = res4[:, 2 * n:2 * n + 2, ds(i, 1), :].rearrange("p l c d -> p l (c d)")
                    last = nc.vector.tensor_tensor(out=at, in0=acc[n][:, :].rearrange("p (l d) -> p l d", d=D), in1=at, op=ALU.add)
                    if n == 0:
                        last.then_inc(v.sem, v.one())
                last.then_inc(out_ready.sem, 1)
                dve.nop().then_inc(turns.sem, 1)
                v.close("layer1 dve")


NAMES = ["L0_attn_x", "L0_attn_norm1_w", "L0_attn_wq", "L0_attn_wk", "L0_attn_wv", "L0_attn_w_ig", "L0_attn_b_ig",
         "L0_attn_w_fg", "L0_attn_b_fg", "L0_attn_w_og", "L0_attn_mh_w", "L0_attn_w_out", "L0_attn_norm2_w",
         "L0_attn_w_gate", "L0_attn_w_up", "L0_attn_w_down", "L0_ffn_Wg", "L0_ffn_Wu", "L0_ffn_Wd", "L0_ffn_Wr",
         "L0_ffn_Ag", "L0_ffn_Bg", "L0_ffn_Au", "L0_ffn_Bu", "L0_ffn_Ad", "L0_ffn_Bd", "L1_attn_weight_qkv",
         "L1_attn_weight_out", "L1_ffn_w_gate", "L1_ffn_w_up", "L1_ffn_w_down"]


def kernel(**inputs):
    import numpy as _np
    import concourse.bacc as _bacc
    from concourse.bass_utils import run_bass_kernel_spmd as _run

    nc = _bacc.Bacc("TRN2", target_bir_lowering=False, num_devices=1)
    arrays, args = {}, []
    for name in NAMES:
        a = _np.ascontiguousarray(inputs[name])
        arrays[f"in_{name}"] = a
        args.append(nc.dram_tensor(f"in_{name}", a.shape, mybir.dt.from_np(a.dtype), kind="ExternalInput").ap())
    out = nc.dram_tensor("out_x", (B, S, D), fp32, kind="ExternalOutput").ap()
    program(nc, *args, out)
    return _run(nc, [arrays], core_ids=[0]).results[0]["out_x"]
```

```python
import concourse.bass as bass
from concourse import mybir
from contextlib import ExitStack

fp32 = mybir.dt.float32
fp32r = mybir.dt.float32r
ALU = mybir.AluOpType
ACT = mybir.ActivationFunctionType
AX = mybir.AxisListType
ds = bass.ds

P = 128
B, S, D = 4, 512, 256
C = S // P
KD = D // P
F = 704
FB = -(-F // P)
FP = FB * P
FT = F - (FB - 1) * P
E, RK = 8, 16
ER = E * RK
H = 8
DQ, DV = P // H, D // H
V1 = DV + 1
FF = 1024
NF = FF // P
H1, DH1 = 16, D // 16
CAP = 15.0
QUADS = (0, 32, 64)
KB = 1024


class Signal:

    def __init__(self, sem, per, credit=0):
        self.sem, self.per, self.credit = sem, per, credit

    def at(self, turn, k):
        return turn * self.per + (k + self.credit)


class Steps:

    def __init__(self, sem, turn, per):
        self.sem, self.turn, self.per, self.n = sem, turn, per, 0

    def one(self):
        self.n += 1
        return 1

    def done(self):
        return self.turn * self.per + self.n

    def close(self, what):
        assert self.n == self.per, f"{what}: {self.n} steps a turn, not {self.per}"


class Shared:
    pass


class Map:

    def __init__(self, nc, at):
        self.nc, self.at = nc, at

    def __call__(self, name, shape, dt=fp32):
        n = 4
        for x in shape[1:]:
            n *= x
        t = self.nc.alloc_sbuf_tensor_at(name, shape, dt, offset=self.at)
        self.at += -(-n // 32) * 32
        assert self.at <= self.nc.sbuf_top, name
        return t

    def pair(self, name, shape):
        return self(name + "_hi", shape, fp32r), self(name + "_lo", shape, fp32r)


def f32(ap):
    return ap.bitcast(fp32)


def product(nc, out, w, x, start, stop):
    nc.tensor.matmul(out, w[0], x[0], start=start, stop=False, skip_group_check=True)
    nc.tensor.matmul(out, w[0], x[1], start=False, stop=False, skip_group_check=True)
    return nc.tensor.matmul(out, w[1], x[0], start=False, stop=stop, skip_group_check=True)


def cut(pair, *index):
    return pair[0][index], pair[1][index]


LATE = 2


class Fetch:

    def __init__(self, sems, tag, groups):
        self.groups = groups
        self.sems = [sems(f"{tag}_loaded{n}") for n in range(len(groups))]

    def issue(self, eng, numbers):
        for n in numbers:
            for dst, src in self.groups[n]:
                eng.dma_start(dst, src).then_inc(self.sems[n], 16)

    def full(self, n):
        return 16 * len(self.groups[n])


class Piece:

    def __init__(self, hi, lo, raw=None, turned=None, rows=P, group=0):
        self.hi, self.lo, self.raw, self.turned, self.rows, self.group = hi, lo, raw, turned, rows, group


class Weights:

    def __init__(self, nc, sems, tag, banks, ident, fetch, presets, pieces):
        self.nc, self.banks, self.ident, self.fetch, self.presets, self.pieces = nc, banks, ident, fetch, presets, pieces
        self.turns = [n for n, p in enumerate(pieces) if p.turned]
        self.high, self.low = sems(f"{tag}_high"), sems(f"{tag}_low")
        self.turned = sems(f"{tag}_turned") if self.turns else None
        self.blank = sems(f"{tag}_blank") if presets else None
        self.all = len(pieces)

    def source(self, n):
        p = self.pieces[n]
        if p.raw is not None:
            src = p.raw
        else:
            k = self.turns.index(n)
            width = sum(x.shape[0] for x in p.turned)
            src = self.banks[k % len(self.banks)][0:p.rows, 0:width]
        if len(p.hi.shape) == 3 and len(src.shape) == 2:
            return src.rearrange("p (a b) -> p a b", a=p.hi.shape[1])
        return src

    def preset(self):
        for dst, value in self.presets:
            self.nc.gpsimd.memset(dst, value).then_inc(self.blank, 1)

    def turn(self, pe, late=0):
        seen = -1
        for k, n in enumerate(self.turns):
            if self.pieces[n].group != seen:
                seen = self.pieces[n].group
                pe.wait_ge(self.fetch.sems[seen], self.fetch.full(seen))
            if k >= len(self.banks):
                pe.wait_ge(self.low, self.turns[k - len(self.banks)] + 1)
            at = 0
            for x in self.pieces[n].turned:
                rows, cols = x.shape[0], x.shape[1]
                last = self.nc.tensor.transpose(self.banks[k % len(self.banks)][0:cols, at:at + rows], x, self.ident[0:rows, 0:rows])
                at += rows
            last.then_inc(self.turned, 1)
        pe.wait_ge(self.low, self.all - late)

    def split_high(self, act, first=0, end=None):
        if self.presets:
            act.wait_ge(self.blank, len(self.presets))
        for n in range(self.all)[first:end]:
            p = self.pieces[n]
            if p.turned:
                act.wait_ge(self.turned, self.turns.index(n) + 1)
            elif n == 0 or self.pieces[n - 1].turned or self.pieces[n - 1].group != p.group:
                act.wait_ge(self.fetch.sems[p.group], self.fetch.full(p.group))
            self.nc.scalar.activation(p.hi, self.source(n), ACT.Copy).then_inc(self.high, 1)

    def split_low(self, dve, first=0, end=None):
        for n in range(self.all)[first:end]:
            p = self.pieces[n]
            dve.wait_ge(self.high, n + 1)
            self.nc.vector.tensor_tensor(out=p.lo, in0=self.source(n), in1=f32(p.hi), op=ALU.subtract).then_inc(self.low, 1)


def program(nc, x_in, norm1_w, wq, wk, wv, w_ig, b_ig, w_fg, b_fg, w_og, mh_w, w_out, norm2_w, w_gate, w_up,
            w_down, Wg, Wu, Wd, Wr, Ag, Bg, Au, Bu, Ad, Bd, wqkv, wo1, w1_gate, w1_up, w1_down, out):
    ctx = ExitStack()
    with ctx:
        def sems(name):
            return ctx.enter_context(nc.semaphore(name))

        def counted(name, per, credit=0):
            return Signal(sems(name), per, credit)

        bank = [ctx.enter_context(nc.psum_tensor(f"bank{n}", [P, 512], fp32)) for n in range(8)]

        keep = Map(nc, -(-nc.sbuf_base // KB) * KB)
        ident = keep("ident", [P, P])
        minus_half = keep("minus_half", [P, 16])
        head_mask = keep("head_mask", [P, H])
        head_spread = keep("head_spread", [H, P])
        expert_rank = keep("expert_rank", [P, C * E])
        ones_row = keep("ones_row", [H, S])
        causal = keep("causal", [P, P])
        norm1_col = keep("norm1_col", [P, KD])
        norm2_col = keep("norm2_col", [P, KD])
        mh_col = keep("mh_col", [P, KD])
        gate_bias = keep("gate_bias", [H, 2])
        gate_bias15 = keep("gate_bias15", [H, 2])
        scale_y = keep("scale_y", [P, B * C])
        res = keep("res", [P, B * C, D])
        xn = keep("xn", [P, B * C, D])
        W0 = -(-keep.at // KB) * KB
        x_tiles = x_in.rearrange("b (c p) d -> p (b c) d", p=P)

        for_ffn = ffn_fetch(nc, sems, Wg, Wu, Wd, Wr, Ag, Bg, Au, Bu, Ad, Bd)
        const_ready, x_loaded = sems("const_ready"), sems("x_loaded")
        block = nc.Block()
        with block:
            @block.sync
            def _(sp):
                for b in range(B):
                    sp.dma_start(res[:, b * C:(b + 1) * C, :], x_tiles[:, b * C:(b + 1) * C, :]).then_inc(x_loaded, 16)
                small = [(norm1_col[:, :], norm1_w.rearrange("(k p) -> p k", p=P)),
                         (norm2_col[:, :], norm2_w.rearrange("(k p) -> p k", p=P)),
                         (mh_col[:, :], mh_w.rearrange("(k p) -> p k", p=P)),
                         (gate_bias[:, 0:1], b_ig.rearrange("(h o) -> h o", o=1)),
                         (gate_bias[:, 1:2], b_fg.rearrange("(h o) -> h o", o=1))]
                with nc.allow_non_contiguous_dma(reason="a few hundred words"):
                    for dst, src in small:
                        sp.dma_start(dst, src).then_inc(x_loaded, 16)
                for_ffn[-1].issue(sp, (3, 5))
                sp.wait_ge(x_loaded, 16 * (B + len(small)))

            @block.scalar
            def _(act):
                for_ffn[-1].issue(act, (0, 1, 2, 4))

            @block.gpsimd
            def _(pool):
                steps = Steps(const_ready, 0, 0)
                nc.gpsimd.memset(ident[:, :], 0.0).then_inc(steps.sem, steps.one())
                nc.gpsimd.memset(head_mask[:, :], 1.0).then_inc(steps.sem, steps.one())
                nc.gpsimd.memset(head_spread[:, :], 1.0).then_inc(steps.sem, steps.one())
                nc.gpsimd.memset(minus_half[:, :], -0.5).then_inc(steps.sem, steps.one())
                nc.gpsimd.memset(causal[:, :], 0.0).then_inc(steps.sem, steps.one())
                nc.gpsimd.memset(ones_row[:, :], 1.0).then_inc(steps.sem, steps.one())
                for e in range(E):
                    nc.gpsimd.memset(expert_rank[:, e::E], float(E - e)).then_inc(steps.sem, steps.one())
                pool.wait_ge(steps.sem, steps.done())
                nc.gpsimd.affine_select(out=ident[:, :], in_=ident[:, :], compare_op=ALU.not_equal, fill=1.0,
                                              base=0, pattern=[[-1, P]], channel_multiplier=1).then_inc(steps.sem, steps.one())
                nc.gpsimd.affine_select(out=causal[:, :], in_=causal[:, :], compare_op=ALU.is_ge, fill=-1e30,
                                              base=0, pattern=[[1, P]], channel_multiplier=-1).then_inc(steps.sem, steps.one())
                nc.gpsimd.affine_select(out=head_mask[:, :], in_=head_mask[:, :], compare_op=ALU.is_ge, fill=0.0,
                                              base=0, pattern=[[-DQ, H]], channel_multiplier=1).then_inc(steps.sem, steps.one())
                nc.gpsimd.affine_select(out=head_spread[:, :], in_=head_spread[:, :], compare_op=ALU.is_ge,
                                              fill=0.0, base=0, pattern=[[1, P]], channel_multiplier=-DQ).then_inc(steps.sem, steps.one())
                pool.wait_ge(steps.sem, steps.done())
                nc.gpsimd.affine_select(out=head_mask[:, :], in_=head_mask[:, :], compare_op=ALU.is_ge, fill=0.0,
                                              base=DQ - 1, pattern=[[DQ, H]], channel_multiplier=-1).then_inc(steps.sem, steps.one())
                nc.gpsimd.affine_select(out=head_spread[:, :], in_=head_spread[:, :], compare_op=ALU.is_ge,
                                              fill=0.0, base=DQ - 1, pattern=[[-1, P]], channel_multiplier=DQ).then_inc(steps.sem, steps.one())

            @block.vector
            def _(dve):
                dve.wait_ge(x_loaded, 16 * (B + 5))
                nc.vector.tensor_scalar(out=gate_bias15[:, :], in0=gate_bias[:, :], scalar1=1.0 / CAP, scalar2=None,
                                        op0=ALU.mult)

        g = Shared()
        g.ident, g.causal, g.head_mask, g.head_spread = ident, causal, head_mask, head_spread
        g.minus_half, g.expert_rank, g.ones_row = minus_half, expert_rank, ones_row
        g.norm1_col, g.norm2_col, g.mh_col, g.gate_bias15 = norm1_col, norm2_col, mh_col, gate_bias15
        g.scale_y, g.bank, g.W0, g.sems, g.counted = scale_y, bank, W0, sems, counted
        g.res, g.xnf = res[:, :, :].rearrange("p t d -> p (t d)"), xn[:, :, :].rearrange("p t d -> p (t d)")
        for_mlstm = mlstm_fetch(nc, sems, wq, wk, wv, w_ig, w_fg, w_og, w_out)
        for_mlp = mlp_fetch(nc, sems, w_gate, w_up, w_down)
        for_layer1 = layer1_fetch(nc, sems, wqkv, wo1, w1_gate, w1_up, w1_down)
        ffn_phase(nc, g, for_ffn, for_mlstm[-1])
        mlstm_phase(nc, g, for_mlstm, for_mlp[-1])
        mlp_phase(nc, g, for_mlp, for_layer1[-1])
        layer1_phase(nc, g, for_layer1, out)



def moments(nc, v, st, mv, t):
    nc.vector.tensor_tensor(out=t[0][:, :], in0=st[:, :, 1], in1=st[:, :, 4], op=ALU.add).then_inc(v.sem, v.one())
    nc.vector.tensor_tensor(out=t[1][:, :], in0=st[:, :, 1], in1=st[:, :, 4], op=ALU.subtract).then_inc(v.sem, v.one())
    nc.vector.tensor_tensor(out=t[2][:, :], in0=st[:, :, 2], in1=st[:, :, 5], op=ALU.add).then_inc(v.sem, v.one())
    nc.vector.wait_ge(v.sem, v.done())
    nc.vector.tensor_scalar(out=mv[:, :, 0], in0=t[0][:, :], scalar1=0.5, scalar2=None, op0=ALU.mult).then_inc(v.sem, v.one())
    nc.vector.scalar_tensor_tensor(out=t[3][:, :], in0=t[1][:, :], scalar=0.25, in1=t[1][:, :], op0=ALU.mult, op1=ALU.mult).then_inc(v.sem, v.one())
    nc.vector.wait_ge(v.sem, v.done())
    nc.vector.scalar_tensor_tensor(out=mv[:, :, 1], in0=t[2][:, :], scalar=1.0 / D, in1=t[3][:, :], op0=ALU.mult, op1=ALU.add).then_inc(v.sem, v.one())
    nc.vector.wait_ge(v.sem, v.done())


class Hidden:

    def __init__(self, nc, g, name, units, ring, m):
        assert units % ring == 0 and units % 2 == 0
        self.nc, self.units, self.slots = nc, units, ring
        self.gate_up = g.counted(name + "_gate_up", units)
        self.silu = g.counted(name + "_silu", units)
        self.hidden = g.counted(name + "_hidden", units, 2)
        self.hi = g.counted(name + "_hi", units, 2)
        self.lo = g.counted(name + "_lo", units, 2)
        self.down = g.counted(name + "_down", units, ring)
        self.s = [m(f"{name}_s{n}", [P, S]) for n in range(2)]
        self.h = [m(f"{name}_h{n}", [P, S]) for n in range(2)]
        self.ring = [m.pair(f"{name}_ring{n}", [P, S]) for n in range(ring)]

    def unit(self, u):
        return self.ring[u % self.slots]

    def act_silu(self, act, i, u, gate):
        act.wait_ge(self.gate_up.sem, self.gate_up.at(i, u + 1))
        act.wait_ge(self.hidden.sem, self.hidden.at(i, u - 1))
        self.nc.scalar.activation(self.s[u % 2][:, :], gate, ACT.Silu).then_inc(self.silu.sem, 1)

    def act_hi(self, act, i, u):
        act.wait_ge(self.hidden.sem, self.hidden.at(i, u + 1))
        act.wait_ge(self.down.sem, self.down.at(i, u + 1 - self.slots))
        self.nc.scalar.activation(self.unit(u)[0][:, :], self.h[u % 2][:, :], ACT.Copy).then_inc(self.hi.sem, 1)

    def dve_hidden(self, dve, i, u, up):
        dve.wait_ge(self.silu.sem, self.silu.at(i, u + 1))
        dve.wait_ge(self.hi.sem, self.hi.at(i, u - 1))
        dve.wait_ge(self.lo.sem, self.lo.at(i, u - 1))
        self.nc.vector.tensor_tensor(out=self.h[u % 2][:, :], in0=self.s[u % 2][:, :], in1=up, op=ALU.mult).then_inc(self.hidden.sem, 1)

    def dve_lo(self, dve, i, u):
        dve.wait_ge(self.hi.sem, self.hi.at(i, u + 1))
        self.nc.vector.tensor_tensor(out=self.unit(u)[1][:, :], in0=self.h[u % 2][:, :],
                                     in1=f32(self.unit(u)[0][:, :]), op=ALU.subtract).then_inc(self.lo.sem, 1)


def expand(ap, n):
    return ap.unsqueeze(len(ap.shape)).to_broadcast(list(ap.shape) + [n])


def top(nc, size):
    return Map(nc, (nc.sbuf_top - size) // 32 * 32)


def ffn_fetch(nc, sems, Wg, Wu, Wd, Wr, Ag, Bg, Au, Bu, Ad, Bd):
    r = top(nc, 4 * (2 * FB * (D + ER) + 3 * D + F + KD * (ER + F)))
    rg, ru = r("rg", [P, FB, D]), r("ru", [P, FB, D])
    rbg, rbu = r("rbg", [P, FB, ER]), r("rbu", [P, FB, ER])
    rag, rau, rad = r("rag", [P, D]), r("rau", [P, D]), r("rad", [P, F])
    rbd, rd, rr = r("rbd", [P, KD, ER]), r("rd", [P, KD, F]), r("rr", [E, D])
    whole = (FB - 1) * P
    groups = []
    for dst, src in ((rg, Wg), (ru, Wu)):
        groups.append([(dst[:, 0:FB - 1, :], src[0:whole, :].rearrange("(b p) d -> p b d", p=P)), (dst[0:FT, FB - 1, :], src[whole:F, :])])
    groups.append([(rag[:, :], Ag.rearrange("e r d -> (e r) d")), (rau[:, :], Au.rearrange("e r d -> (e r) d")),
                   (rad[:, :], Ad.rearrange("e r f -> (e r) f")), (rd[:, :, :], Wd.rearrange("(k p) f -> p k f", p=P)), (rr[:, :], Wr)])
    for dst, src in ((rbg, Bg), (rbu, Bu)):
        group = []
        for b in range(FB):
            n = min(P, F - b * P)
            group.append((dst[0:n, b, :].rearrange("p (e r) -> p e r", r=RK), src[:, b * P:b * P + n, :].rearrange("e p r -> p e r")))
        groups.append(group)
    groups.append([(rbd[:, k, :].rearrange("p (e r) -> p e r", r=RK), Bd[:, k * P:(k + 1) * P, :].rearrange("e p r -> p e r")) for k in range(KD)])
    return rg, ru, rbg, rbu, rag, rau, rad, rbd, rd, rr, Fetch(sems, "ffn", groups)


def mlstm_fetch(nc, sems, wq, wk, wv, w_ig, w_fg, w_og, w_out):
    r = top(nc, 4 * KD * (2 * P + 2 * D + 2 * H + D))
    rp, rgt, ro = r("m_rp2", [P, KD, 2 * P + 2 * D]), r("m_rg2", [P, KD, 2, H]), r("m_ro2", [P, KD, D])
    rows = lambda w: w.rearrange("(k p) n -> p k n", p=P)
    groups = [[(rp[:, :, 0:P], rows(wk)), (rp[:, :, P:P + D], rows(wv)), (rp[:, :, P + D:2 * P + D], rows(wq)),
               (rp[:, :, 2 * P + D:2 * P + 2 * D], rows(w_og)),
               (rgt[:, :, 0, :], rows(w_ig)), (rgt[:, :, 1, :], rows(w_fg)), (ro[:, :, :], rows(w_out))]]
    return rp, rgt, ro, Fetch(sems, "mlstm", groups)


def mlp_fetch(nc, sems, w_gate, w_up, w_down):
    r = top(nc, 4 * (KD * 2 * FF + NF * D))
    rgu, rd = r("p_rgu", [P, KD, 2, FF]), r("p_rd", [P, NF, D])
    rows = lambda w: w.rearrange("(k p) n -> p k n", p=P)
    groups = [[(rgu[:, :, 0, :], rows(w_gate)), (rgu[:, :, 1, :], rows(w_up)), (rd[:, :, :], rows(w_down))]]
    return rgu, rd, Fetch(sems, "mlp", groups)


def layer1_fetch(nc, sems, wqkv, wo1, w1_gate, w1_up, w1_down):
    GP = 4
    NG = NF // GP
    r = top(nc, 4 * (3 * D // P * D + KD * D + KD * 2 * FF + NF * D))
    rq, ro = r("l_rq", [P, 3 * D // P, D]), r("l_ro", [P, KD, D])
    rgu, rd = r("l_rgu", [P, KD, 2, FF]), r("l_rd", [P, NG, GP, D])
    rows = lambda w: w.rearrange("(k p) n -> p k n", p=P)
    groups = [[(rq[:, :, :], rows(wqkv)), (ro[:, :, :], rows(wo1)), (rgu[:, :, 0, :], rows(w1_gate)), (rgu[:, :, 1, :], rows(w1_up)),
               (rd[:, :, :, :], w1_down.rearrange("(c p j) n -> p c j n", p=P, j=GP))]]
    return rq, ro, rgu, rd, Fetch(sems, "l", groups)


def ffn_phase(nc, g, raws, after):
    bank, ident = g.bank, g.ident
    m = Map(nc, g.W0)
    wgu = m.pair("wgu", [P, KD, 2, FP])
    wb = m.pair("wb", [P, 2, FP])
    wa = m.pair("wa", [P, KD, 2, ER])
    wad = m.pair("wad", [P, FB, ER])
    wbd = m.pair("wbd", [P, D])
    wd = m.pair("wd", [P, FB, D])
    wr = m.pair("wr", [P, KD, P])
    rg, ru, rbg, rbu, rag, rau, rad, rbd, rd, rr, fetch = raws
    pieces = []

    def blocks(raw, b0, b1, cols):
        return [raw[0:min(P, F - b * P), b, cols] for b in range(b0, b1)]

    def both(pair, *index):
        return {"hi": pair[0][index], "lo": pair[1][index]}

    a = slice(None)
    for n, raw in ((0, rg), (1, ru)):
        for k in range(KD):
            cols = slice(k * P, (k + 1) * P)
            pieces.append(Piece(**both(wgu, a, k, n, slice(0, 4 * P)), turned=blocks(raw, 0, 4, cols), group=n))
            pieces.append(Piece(**both(wgu, a, k, n, slice(4 * P, F)), turned=blocks(raw, 4, FB, cols), group=n))
    for k in range(KD):
        pieces.append(Piece(**both(wa, a, k), turned=[x[:, k * P:(k + 1) * P] for x in (rag, rau)], group=2))
    pieces.append(Piece(**both(wad, a, slice(0, 4)), turned=[rad[:, b * P:(b + 1) * P] for b in range(4)], group=2))
    pieces.append(Piece(**both(wad, a, 4), turned=[rad[:, 4 * P:5 * P]], group=2))
    pieces.append(Piece(**both(wad, slice(0, FT), 5), turned=[rad[:, 5 * P:F]], rows=FT, group=2))
    for b in range(FB):
        n = min(P, F - b * P)
        pieces.append(Piece(**both(wd, slice(0, n), b), turned=[rd[:, k, b * P:b * P + n] for k in range(KD)], rows=n, group=2))
    for k in range(KD):
        pieces.append(Piece(**both(wr, a, k, slice(0, E)), turned=[rr[:, k * P:(k + 1) * P]], group=2))
    for n, raw in ((0, rbg), (1, rbu)):
        pieces.append(Piece(**both(wb, a, n, slice(0, 4 * P)), turned=blocks(raw, 0, 4, a), group=3 + n))
        pieces.append(Piece(**both(wb, a, n, slice(4 * P, F)), turned=blocks(raw, 4, FB, a), group=3 + n))
    pieces.append(Piece(**both(wbd, a, a), turned=[rbd[:, k, :] for k in range(KD)], group=5))
    presets = []
    for t in (0, 1):
        presets += [(x, 0.0) for x in (f32(wgu[t][:, :, :, F:FP]), f32(wb[t][:, :, F:FP]), f32(wad[t][:, FB - 1, :]), f32(wd[t][:, FB - 1, :]), f32(wr[t][:, :, :]))]
    splitting = Weights(nc, g.sems, "ffn_w", bank, ident, fetch, presets, pieces)

    xs = m("f_xs", [P, C, D])
    st, mv = m("f_st", [P, C, 6]), m("f_mv", [P, C, 2])
    vv, rstd, msq = m("f_vv", [P, C]), m("f_rstd", [P, C]), m("f_msq", [P, C])
    xT = m.pair("f_xT", [P, KD, S])
    lg = m("f_lg", [P, S])
    small = [m(f"f_small{n}", [P, C * E]) for n in range(7)]
    tiny = [m(f"f_tiny{n}", [P, C]) for n in range(7)]
    sel = m("f_sel", [P, 4, C * E])
    selx = m("f_selx", [P, 4, C * E * RK])
    mask = m("f_mask", [P, 4, S])
    low = [m.pair(f"f_a{n}", [P, S]) for n in range(2)]
    op = [[m.pair(f"f_op{n}{t}", [P, S]) for t in range(2)] for n in range(2)]
    zt = [m(f"f_z{n}", [P, S]) for n in range(2)]
    z = m.pair("f_z", [P, S])
    order = [(b0 + n, t) for b0 in range(0, FB, 2) for t in range(3) for n in range(2)]
    U = len(order)
    hid = Hidden(nc, g, "f", U, 6, m)
    sg = g.counted
    stats, powed, xs_ready, xT_t, xT_hi, xT_lo = sg("f_stats", 2), sg("f_pow", 2), sg("f_xs", 1), sg("f_xTt", 2), sg("f_xThi", 2), sg("f_xTlo", 2)
    lg_ready, lg_copied, lgT, centred, exped = sg("f_lg", 1), sg("f_lgc", 1), sg("f_lgT", 1), sg("f_cent", 1), sg("f_exp", 1)
    a_done, a_hi, a_lo = sg("f_a", 2), sg("f_ahi", 2), sg("f_alo", 2)
    spread, mask_t, mask_in, ops = sg("f_spread", 4), sg("f_maskt", 4), sg("f_maskin", 4), sg("f_ops", 8)
    zsum, zhi, zlo, acc_done = sg("f_zsum", 1), sg("f_zhi", 1), sg("f_zlo", 1), sg("f_acc", 1)
    copied, acc_free = sg("f_copied", 1), sg("f_accfree", 1, 1)
    NPRE, NBODY = 35, 3
    pre_sem, dve_sem = g.sems("f_pre"), g.sems("f_dve")
    gate = lambda u: bank[0] if order[u][0] % 2 == 0 else bank[2]
    up = lambda u: bank[1] if order[u][0] % 2 == 0 else bank[3]
    low_bank, acc = [bank[4], bank[5]], [bank[6], bank[7]]
    lg_bank, a_bank, lgT_bank = bank[2], [bank[3], bank[0]], bank[1]
    mask_bank = [bank[4], bank[5], bank[6], bank[7]]
    block = nc.Block()
    with block:
        @block.sync
        def _(sp):
            sp.wait_ge(splitting.low, splitting.all)
            after.issue(sp, range(len(after.groups)))

        @block.tensor
        def _(pe):
            pe.sem_inc(hid.down.sem, hid.down.credit)

            def units(i, u):
                b, t = order[u]
                pe.wait_ge(hid.hidden.sem, hid.hidden.at(i, u - 1))
                for n, o in ((0, gate(u)), (1, up(u))):
                    cols = slice(b * P, (b + 1) * P)
                    if t == 0:
                        for k in range(KD):
                            last = product(nc, o[:, :], cut(wgu, a, k, n, cols), cut(xT, a, k), k == 0, k == KD - 1)
                    else:
                        if b == 0:
                            pe.wait_ge(ops.sem, ops.at(i, 4 * t if n else 4 * t - 2))
                        last = product(nc, o[:, :], cut(wb, a, n, cols), cut(op[t - 1][n], a, a), False, True)
                last.then_inc(hid.gate_up.sem, 1)

            def down(i, u):
                b, t = order[u]
                h = hid.unit(u)
                pe.wait_ge(hid.lo.sem, hid.lo.at(i, u + 1))
                if t == 0:
                    for c in range(C):
                        last = product(nc, acc[c // 2][:, c % 2 * D:(c % 2 + 1) * D], cut(h, a, slice(c * P, (c + 1) * P)),
                                       cut(wd, a, b), b == 0 and c % 2 == 0, False)
                else:
                    last = product(nc, low_bank[t - 1][:, :], cut(wad, a, b), cut(h, a, a), b == 0, b == FB - 1)
                last.then_inc(hid.down.sem, 1)

            def turn_x(i):
                pe.wait_ge(xs_ready.sem, xs_ready.at(i, 1))
                for k in range(KD):
                    for c in range(C):
                        last = nc.tensor.transpose(bank[k][:, c * P:(c + 1) * P], xs[:, c, k * P:(k + 1) * P], ident[:, :])
                    last.then_inc(xT_t.sem, 1)

            def router_and_ranks(i):
                pe.wait_ge(xT_lo.sem, xT_lo.at(i, KD))
                pe.wait_ge(hid.hidden.sem, hid.hidden.at(i, 0))
                for k in range(KD):
                    last = product(nc, lg_bank[:, :], cut(wr, a, k), cut(xT, a, k), k == 0, k == KD - 1)
                last.then_inc(lg_ready.sem, 1)
                for n in range(2):
                    for k in range(KD):
                        last = product(nc, a_bank[n][:, :], cut(wa, a, k, n), cut(xT, a, k), k == 0, k == KD - 1)
                    last.then_inc(a_done.sem, 1)

            def turn_router(i):
                pe.wait_ge(lg_copied.sem, lg_copied.at(i, 1))
                for c in range(C):
                    last = nc.tensor.transpose(lgT_bank[:, c * P:(c + 1) * P], lg[:, c * P:(c + 1) * P], ident[:, :])
                last.then_inc(lgT.sem, 1)

            def turn_masks(i):
                pe.wait_ge(acc_free.sem, acc_free.at(i, 0))
                for n in range(4):
                    pe.wait_ge(spread.sem, spread.at(i, n + 1))
                    for c in range(C):
                        last = nc.tensor.transpose(mask_bank[n][:, c * P:(c + 1) * P], selx[:, n, c * ER:(c + 1) * ER], ident[:, :])
                    last.then_inc(mask_t.sem, 1)

            def expert_down(i):
                pe.wait_ge(zlo.sem, zlo.at(i, 1))
                for c in range(C):
                    last = product(nc, acc[c // 2][:, c % 2 * D:(c % 2 + 1) * D], cut(z, a, slice(c * P, (c + 1) * P)),
                                   cut(wbd, a, a), False, True)
                last.then_inc(acc_done.sem, 1)

            def body(i, following):
                pe.wait_ge(a_lo.sem, a_lo.at(i, 2))
                pe.wait_ge(centred.sem, centred.at(i, 1))
                units(i, 0)
                units(i, 1)
                turn_masks(i)
                pe.wait_ge(mask_in.sem, mask_in.at(i, 4))
                for u in range(2, U):
                    units(i, u)
                    down(i, u - 2)
                if following is not None:
                    pe.wait_ge(hid.hidden.sem, hid.hidden.at(i, U - 1))
                    turn_x(following)
                down(i, U - 2)
                down(i, U - 1)
                if following is not None:
                    router_and_ranks(following)
                    turn_router(following)
                expert_down(i)

            splitting.turn(pe)
            turn_x(0)
            router_and_ranks(0)
            turn_router(0)
            with pe.Fori(0, B - 1) as i:
                body(i, i + 1)
            body(B - 1, None)

        @block.scalar
        def _(act):
            act.sem_inc(hid.hi.sem, hid.hi.credit)
            def high_x(i):
                for k in range(KD):
                    act.wait_ge(xT_t.sem, xT_t.at(i, k + 1))
                    nc.scalar.activation(xT[0][:, k, :], bank[k][:, :], ACT.Copy).then_inc(xT_hi.sem, 1)

            def copy_router(i):
                act.wait_ge(lg_ready.sem, lg_ready.at(i, 1))
                nc.scalar.activation(lg[:, :], lg_bank[:, :], ACT.Copy).then_inc(lg_copied.sem, 1)

            def high_ranks(i, n):
                act.wait_ge(a_done.sem, a_done.at(i, n + 1))
                nc.scalar.activation(low[n][0][:, :], a_bank[n][:, :], ACT.Copy).then_inc(a_hi.sem, 1)

            def exponentials(i):
                act.wait_ge(centred.sem, centred.at(i, 1))
                nc.scalar.activation(small[1][:, :], small[0][:, :], ACT.Exp).then_inc(exped.sem, 1)

            def copy_masks(i):
                for n in range(4):
                    act.wait_ge(mask_t.sem, mask_t.at(i, n + 1))
                    nc.scalar.activation(mask[:, n, :], mask_bank[n][:, :], ACT.Copy).then_inc(mask_in.sem, 1)

            def high_z(i):
                act.wait_ge(zsum.sem, zsum.at(i, 1))
                nc.scalar.activation(z[0][:, :], zt[0][:, :], ACT.Copy).then_inc(zhi.sem, 1)

            def body(i, following):
                for u in range(U):
                    hid.act_silu(act, i, u, gate(u)[:, :])
                    if u:
                        hid.act_hi(act, i, u - 1)
                    if u == 1:
                        copy_masks(i)
                if following is not None:
                    high_x(following)
                hid.act_hi(act, i, U - 1)
                if following is not None:
                    copy_router(following)
                    high_ranks(following, 0)
                high_z(i)
                if following is not None:
                    high_ranks(following, 1)
                    exponentials(following)

            splitting.split_high(act)
            high_x(0)
            copy_router(0)
            high_ranks(0, 0)
            high_ranks(0, 1)
            exponentials(0)
            with act.Fori(0, B - 1) as i:
                body(i, i + 1)
            body(B - 1, None)

        @block.gpsimd
        def _(pool):
            splitting.preset()
            with pool.Fori(0, B) as i:
                pool.wait_ge(stats.sem, stats.at(i, 1))
                nc.gpsimd.tensor_tensor(out=rstd[:, :], in0=vv[:, :], in1=g.minus_half[:, 0:C], op=ALU.pow).then_inc(powed.sem, 1)
                pool.wait_ge(stats.sem, stats.at(i, 2))
                nc.gpsimd.tensor_tensor(out=g.scale_y[:, ds(i * C, C)], in0=msq[:, :], in1=g.minus_half[:, 0:C], op=ALU.pow).then_inc(powed.sem, 1)
                pool.wait_ge(xs_ready.sem, xs_ready.at(i, 1))
                nc.gpsimd.tensor_copy(g.xnf[:, ds(i * C * D, C * D)], xs[:, :, :].rearrange("p c d -> p (c d)")).then_inc(copied.sem, 1)
                pool.wait_ge(a_lo.sem, a_lo.at(i, 2))
                for t in range(2):
                    pool.wait_ge(mask_in.sem, mask_in.at(i, t + 1))
                    for n in range(2):
                        for part in range(2):
                            nc.gpsimd.tensor_tensor(out=op[t][n][part][:, :], in0=f32(low[n][part][:, :]), in1=mask[:, t, :], op=ALU.mult).then_inc(ops.sem, 1)

        @block.vector
        def _(dve):
            dve.sem_inc(acc_free.sem, acc_free.credit)
            dve.sem_inc(hid.hidden.sem, hid.hidden.credit)
            dve.sem_inc(hid.lo.sem, hid.lo.credit)
            per_token = lambda t: t[:, :].rearrange("p (c e) -> p c e", e=E)
            lgv = lgT_bank[:, :].rearrange("p (c e) -> p c e", e=P)[:, :, 0:E]

            def statistics(i, w):
                for c in range(C):
                    nc.vector.bn_stats(out=st[:, c, :], in_=g.res[:, ds((i * C + c) * D, D)]).then_inc(w.sem, w.one())
                dve.wait_ge(w.sem, w.done())
                moments(nc, w, st, mv, tiny)
                nc.vector.tensor_scalar(out=vv[:, :], in0=mv[:, :, 1], scalar1=1e-5, scalar2=None, op0=ALU.add).then_inc(stats.sem, 1)

            def norm(i, w, first=False):
                if not first:
                    dve.wait_ge(copied.sem, copied.at(i, 0))
                dve.wait_ge(powed.sem, powed.at(i, 1))
                for c in range(C):
                    last = nc.vector.tensor_scalar(out=xs[:, c, :], in0=g.res[:, ds((i * C + c) * D, D)], scalar1=mv[:, c, 0:1],
                                                   scalar2=rstd[:, c:c + 1], op0=ALU.subtract, op1=ALU.mult)
                    if c < C - 1:
                        last.then_inc(w.sem, w.one())
                last.then_inc(xs_ready.sem, 1)
                nc.vector.tensor_tensor(out=tiny[0][:, :], in0=mv[:, :, 1], in1=rstd[:, :], op=ALU.mult).then_inc(w.sem, w.one())
                dve.wait_ge(w.sem, w.done())
                nc.vector.tensor_tensor(out=tiny[1][:, :], in0=tiny[0][:, :], in1=rstd[:, :], op=ALU.mult).then_inc(w.sem, w.one())
                dve.wait_ge(w.sem, w.done())
                nc.vector.tensor_scalar(out=msq[:, :], in0=tiny[1][:, :], scalar1=1e-6, scalar2=None, op0=ALU.add).then_inc(stats.sem, 1)

            def low_x(i):
                for k in range(KD):
                    dve.wait_ge(xT_hi.sem, xT_hi.at(i, k + 1))
                    nc.vector.tensor_tensor(out=xT[1][:, k, :], in0=bank[k][:, :], in1=f32(xT[0][:, k, :]), op=ALU.subtract).then_inc(xT_lo.sem, 1)

            def low_ranks(i, n):
                dve.wait_ge(a_hi.sem, a_hi.at(i, n + 1))
                nc.vector.tensor_tensor(out=low[n][1][:, :], in0=a_bank[n][:, :], in1=f32(low[n][0][:, :]), op=ALU.subtract).then_inc(a_lo.sem, 1)

            def router_centred(i, w):
                dve.wait_ge(lgT.sem, lgT.at(i, 1))
                nc.vector.tensor_reduce(out=tiny[0][:, :], in_=lgv, op=ALU.max, axis=AX.X).then_inc(w.sem, w.one())
                dve.wait_ge(w.sem, w.done())
                nc.vector.tensor_tensor(out=per_token(small[0]), in0=lgv, in1=expand(tiny[0][:, :], E), op=ALU.subtract).then_inc(centred.sem, 1)

            def router(i, w):
                dve.wait_ge(exped.sem, exped.at(i, 1))
                nc.vector.tensor_reduce(out=tiny[1][:, :], in_=per_token(small[1]), op=ALU.add, axis=AX.X).then_inc(w.sem, w.one())
                dve.wait_ge(w.sem, w.done())
                nc.vector.reciprocal(out=tiny[2][:, :], in_=tiny[1][:, :]).then_inc(w.sem, w.one())
                dve.wait_ge(w.sem, w.done())
                nc.vector.tensor_tensor(out=per_token(small[2]), in0=per_token(small[1]), in1=expand(tiny[2][:, :], E), op=ALU.mult).then_inc(w.sem, w.one())
                dve.wait_ge(w.sem, w.done())

                def largest(src, one_hot, n):
                    nc.vector.tensor_reduce(out=tiny[n][:, :], in_=per_token(src), op=ALU.max, axis=AX.X).then_inc(w.sem, w.one())
                    dve.wait_ge(w.sem, w.done())
                    nc.vector.tensor_tensor(out=per_token(small[3]), in0=per_token(src), in1=expand(tiny[n][:, :], E), op=ALU.is_equal).then_inc(w.sem, w.one())
                    dve.wait_ge(w.sem, w.done())
                    nc.vector.tensor_tensor(out=small[4][:, :], in0=small[3][:, :], in1=g.expert_rank[:, :], op=ALU.mult).then_inc(w.sem, w.one())
                    dve.wait_ge(w.sem, w.done())
                    nc.vector.tensor_reduce(out=tiny[n + 1][:, :], in_=per_token(small[4]), op=ALU.max, axis=AX.X).then_inc(w.sem, w.one())
                    dve.wait_ge(w.sem, w.done())
                    nc.vector.tensor_tensor(out=per_token(one_hot), in0=per_token(small[4]), in1=expand(tiny[n + 1][:, :], E), op=ALU.is_equal).then_inc(w.sem, w.one())
                    dve.wait_ge(w.sem, w.done())

                largest(small[2], small[5], 3)
                nc.vector.scalar_tensor_tensor(out=small[0][:, :], in0=small[5][:, :], scalar=-4.0, in1=small[2][:, :], op0=ALU.mult, op1=ALU.add).then_inc(w.sem, w.one())
                dve.wait_ge(w.sem, w.done())
                largest(small[0], small[6], 5)
                nc.vector.tensor_scalar(out=sel[:, 0, :], in0=small[5][:, :], scalar1=2.0, scalar2=None, op0=ALU.mult).then_inc(w.sem, w.one())
                nc.vector.tensor_scalar(out=small[1][:, :], in0=small[6][:, :], scalar1=2.0, scalar2=None, op0=ALU.mult).then_inc(w.sem, w.one())
                dve.wait_ge(w.sem, w.done())
                nc.vector.tensor_tensor(out=sel[:, 1, :], in0=small[1][:, :], in1=sel[:, 0, :], op=ALU.subtract).then_inc(w.sem, w.one())
                nc.vector.tensor_tensor(out=sel[:, 2, :], in0=sel[:, 0, :], in1=small[2][:, :], op=ALU.mult).then_inc(w.sem, w.one())
                nc.vector.tensor_tensor(out=sel[:, 3, :], in0=small[1][:, :], in1=small[2][:, :], op=ALU.mult).then_inc(w.sem, w.one())
                dve.wait_ge(w.sem, w.done())
                for n in range(4):
                    nc.vector.tensor_copy(selx[:, n, :].rearrange("p (x r) -> p x r", r=RK), expand(sel[:, n, :], RK)).then_inc(spread.sem, 1)

            def body(i, following):
                v = Steps(dve_sem, i, NBODY)
                w = Steps(pre_sem, following, NPRE)
                for u in range(U):
                    hid.dve_hidden(dve, i, u, up(u)[:, :])
                    if u:
                        hid.dve_lo(dve, i, u - 1)
                    if u == 7 and following is not None:
                        statistics(following, w)
                    if u == 10 and following is not None:
                        norm(following, w)
                if following is not None:
                    low_x(following)
                hid.dve_lo(dve, i, U - 1)
                dve.wait_ge(hid.down.sem, hid.down.at(i, U))
                for t in range(2):
                    nc.vector.tensor_tensor(out=zt[t][:, :], in0=low_bank[t][:, :], in1=mask[:, 2 + t, :], op=ALU.mult).then_inc(v.sem, v.one())
                dve.wait_ge(v.sem, v.done())
                nc.vector.tensor_tensor(out=zt[0][:, :], in0=zt[0][:, :], in1=zt[1][:, :], op=ALU.add).then_inc(zsum.sem, 1)
                if following is not None:
                    low_ranks(following, 0)
                dve.wait_ge(zhi.sem, zhi.at(i, 1))
                nc.vector.tensor_tensor(out=z[1][:, :], in0=zt[0][:, :], in1=f32(z[0][:, :]), op=ALU.subtract).then_inc(zlo.sem, 1)
                if following is not None:
                    low_ranks(following, 1)
                    router_centred(following, w)
                dve.wait_ge(acc_done.sem, acc_done.at(i, 1))
                for n in range(2):
                    at = g.res[:, ds(i * C * D + n * 2 * D, 2 * D)]
                    last = nc.vector.tensor_tensor(out=at, in0=acc[n][:, :], in1=at, op=ALU.add)
                    if n == 0:
                        last.then_inc(v.sem, v.one())
                last.then_inc(acc_free.sem, 1)
                v.close("ffn body")
                if following is not None:
                    router(following, w)
                    w.close("ffn pre")

            w = Steps(pre_sem, 0, NPRE)
            statistics(0, w)
            norm(0, w, True)
            splitting.split_low(dve)
            low_x(0)
            low_ranks(0, 0)
            low_ranks(0, 1)
            router_centred(0, w)
            router(0, w)
            with dve.Fori(0, B - 1) as i:
                body(i, i + 1)
            body(B - 1, None)


def mlstm_phase(nc, g, raws, after):
    bank, ident = g.bank, g.ident
    a = slice(None)
    m = Map(nc, g.W0)
    NKV = P + D
    wp = m.pair("wp", [P, KD, 2 * P + 2 * D])
    wg = m.pair("wg", [P, KD, 2, P])
    wo = m.pair("wo", [P, KD, D])
    Kc, Vc, Qc, Oc = slice(0, P), slice(P, NKV), slice(NKV, NKV + P), slice(NKV + P, NKV + P + D)

    VW = H * V1
    v1 = m("m_v1", [P, C, VW])
    gr = m("m_gr", [QUADS[2] + H, S])
    pairw = [m(f"m_pairw{n}", [P, H, P]) for n in range(2)]
    ga = m("m_ga", [P, 3, C, H])
    ga_flat = ga[:, :, :, :].rearrange("p a c h -> p (a c h)")

    presets = [(f32(wg[t][:, :, :, :]), 0.0) for t in (0, 1)] + [(v1[:, :, :], 1.0), (gr[:, :], 0.0), (ga_flat, 0.0)]
    rp, rgt, ro, fetch = raws
    pieces = [Piece(wp[0][:, k, :], wp[1][:, k, :], raw=rp[:, k, :]) for k in range(KD)]
    pieces += [Piece(wg[0][:, k, :, 0:H], wg[1][:, k, :, 0:H], raw=rgt[:, k, :, :]) for k in range(KD)]
    pieces += [Piece(wo[0][:, :, :], wo[1][:, :, :], raw=ro[:, :, :])]
    splitting = Weights(nc, g.sems, "mlstm_w", bank, ident, fetch, presets, pieces)

    ys = m("m_ys", [P, C, D])
    yT = m.pair("m_yT", [P, KD, S])
    qs, kT = m("m_qs", [P, S]), m("m_kT", [P, S])
    ktok, ktil = m("m_ktok", [P, C, P]), m("m_ktil", [P, C, P])
    sig = m("m_sig", [P, C, D])
    qbd = [m(f"m_qbd{n}", [P, H, P]) for n in range(2)]
    Gb = m("m_Gb", [P, H, S])
    PT = [m(f"m_PT{n}", [P, H, P]) for n in range(2)]
    tot = m("m_tot", [P, C, VW])
    hh, sq = m("m_hh", [P, C, D]), m("m_sq", [P, C, D])
    hT = m.pair("m_hT", [P, KD, S])
    row = [m(f"m_row{n}", [H, S]) for n in range(9)]
    tg = m("m_tg", [P, C, QUADS[2] + H])
    ea = m("m_ea", [P, 3, C, H])
    gend, dec, dexp = m("m_gend", [P, C]), m("m_dec", [P, C - 1]), m("m_dexp", [P, C - 1])
    state, part = m("m_state", [P, VW]), m("m_part", [P, VW])
    den = [m(f"m_den{n}", [P, C * H]) for n in range(7)]
    scratch = nc.dram_tensor("m_scratch", (B, H, S), fp32, kind="Internal").ap()

    sg = g.counted
    y_ready, yT_t, yT_hi, yT_lo = sg("m_y", 1), sg("m_yTt", 2), sg("m_yThi", 2), sg("m_yTlo", 2)
    gates, qk, kv, og = sg("m_gates", 2), sg("m_qk", 2), sg("m_kv", C), sg("m_og", 2)
    tanhed, qk_in, kv_in, og_in = sg("m_tanh", 2), sg("m_qkin", 2), sg("m_kvin", 2 * C), sg("m_ogin", 2)
    u_ready, y1_ready, ln_ready, rows_ready = sg("m_u", 1), sg("m_y1", 1), sg("m_ln", 2), sg("m_rows", 2)
    G_copied, stored, spread = sg("m_Gc", 1), sg("m_stored", 16), sg("m_spread", 16)
    tg_ready, gend_ready, tg_in = sg("m_tg_t", 1), sg("m_gend", 1), sg("m_tg_in", 2)
    ga_ready, ea_ready, dec_ready, dexp_ready = sg("m_ga", 1), sg("m_ea", 1), sg("m_dec", 1), sg("m_dexp", 1)
    q_late = sg("m_qlate", C - 2)
    q_spread, diff, weight, ktil_ready = sg("m_qspread", 2), sg("m_diff", C), sg("m_weight", C), sg("m_ktil", 1)
    scores, PT_ready = sg("m_scores", C), sg("m_PT", C)
    intra, inter, local, state_ready, tot_ready = sg("m_intra", C), sg("m_inter", C - 1), sg("m_local", C - 1), sg("m_state", C - 1), sg("m_tot", C)
    ms_ready, rs0, h_ready = sg("m_ms", 1), sg("m_rs0", 2), sg("m_hready", 1)
    hT_t, hT_hi, hT_lo, x1_ready = sg("m_hTt", 2), sg("m_hThi", 2), sg("m_hTlo", 2), sg("m_x1", 1)
    NPRE, NBODY = 10, 22
    pre_sem, dve_sem, pool_sem = g.sems("m_pre"), g.sems("m_dve"), g.sems("m_pool")
    gate_bank, q_bank, k_bank, kv_bank = [bank[2], bank[3]], bank[4], bank[5], [bank[6], bank[7]]
    og_bank, score_bank = [bank[0], bank[1]], [bank[0], bank[1]]
    tg_bank, gend_bank = bank[2], bank[3]
    intra_bank, inter_bank, local_bank = [bank[4], bank[5]], bank[6], bank[7]
    hT_bank, out_bank = [bank[2], bank[3]], [bank[4], bank[5]]
    per_head = lambda ap: ap.rearrange("p (h e) -> p h e", e=V1)
    block = nc.Block()
    with block:
        @block.sync
        def _(sp):
            sp.wait_ge(splitting.low, splitting.all)
            after.issue(sp, range(len(after.groups)))
            with sp.Fori(0, B) as i:
                sp.wait_ge(rows_ready.sem, rows_ready.at(i, 1))
                dst = scratch[ds(i, 1), :, :].rearrange("o h s -> (o h) s")
                sp.dma_start(dst, row[7][:, :]).then_inc(stored.sem, 16)
                sp.wait_ge(stored.sem, stored.at(i, 16))
                src = scratch[ds(i, 1), :, :].rearrange("o h s -> o (h s)").to_broadcast([P, H * S])
                sp.dma_start(Gb[:, :, :].rearrange("p h s -> p (h s)"), src).then_inc(spread.sem, 16)

        @block.tensor
        def _(pe):
            def turn_y(i):
                pe.wait_ge(y_ready.sem, y_ready.at(i, 1))
                for k in range(KD):
                    for c in range(C):
                        last = nc.tensor.transpose(bank[k][:, c * P:(c + 1) * P], ys[:, c, k * P:(k + 1) * P], ident[:, :])
                    last.then_inc(yT_t.sem, 1)

            def project(i):
                pe.wait_ge(yT_lo.sem, yT_lo.at(i, KD))
                for n in range(2):
                    for k in range(KD):
                        last = product(nc, gate_bank[n][:, :], cut(wg, a, k, n), cut(yT, a, k), k == 0, k == KD - 1)
                    last.then_inc(gates.sem, 1)
                for o, cols in ((q_bank, Qc), (k_bank, Kc)):
                    for k in range(KD):
                        last = product(nc, o[:, :], cut(wp, a, k, cols), cut(yT, a, k), k == 0, k == KD - 1)
                    last.then_inc(qk.sem, 1)
                for c in range(C):
                    if c >= 2:
                        pe.wait_ge(kv_in.sem, kv_in.at(i, 2 * (c - 1)))
                    for k in range(KD):
                        last = product(nc, kv_bank[c % 2][:, 0:NKV], cut(yT, a, k, slice(c * P, (c + 1) * P)),
                                       cut(wp, a, k, slice(0, NKV)), k == 0, k == KD - 1)
                    last.then_inc(kv.sem, 1)

            def output_gate(i):
                for n in range(2):
                    for c in (2 * n, 2 * n + 1):
                        for k in range(KD):
                            last = product(nc, og_bank[n][:, c % 2 * D:(c % 2 + 1) * D], cut(yT, a, k, slice(c * P, (c + 1) * P)),
                                           cut(wp, a, k, Oc), k == 0 and c % 2 == 0, k == KD - 1)
                    last.then_inc(og.sem, 1)

            def turn_gates(i):
                pe.wait_ge(rows_ready.sem, rows_ready.at(i, 2))
                pe.wait_ge(G_copied.sem, G_copied.at(i, 1))
                for c in range(C):
                    n = QUADS[2] + H
                    last = nc.tensor.transpose(tg_bank[:, c * P:c * P + n], gr[:, c * P:(c + 1) * P], ident[0:n, 0:n])
                last.then_inc(tg_ready.sem, 1)
                nc.tensor.matmul(gend_bank[:, 0:C], g.head_spread[:, :], row[7][:, P - 1::P], start=True, stop=True).then_inc(gend_ready.sem, 1)

            def attend(i):
                pe.wait_ge(qk_in.sem, qk_in.at(i, 2))
                pe.wait_ge(kv_in.sem, kv_in.at(i, 2 * C))
                pe.wait_ge(og_in.sem, og_in.at(i, 2))

                def score(c):
                    if c < 2:
                        pe.wait_ge(q_spread.sem, q_spread.at(i, c + 1))
                    else:
                        pe.wait_ge(q_late.sem, q_late.at(i, c - 1))
                    for n in range(2):
                        last = nc.tensor.matmul(score_bank[n][:, :], kT[:, c * P:(c + 1) * P],
                                                qbd[c % 2][:, n * H // 2:(n + 1) * H // 2, :].rearrange("p h s -> p (h s)"),
                                                start=True, stop=True)
                    last.then_inc(scores.sem, 1)

                score(0)
                for c in range(C):
                    cols = slice(c * P, (c + 1) * P)
                    if c:
                        pe.wait_ge(state_ready.sem, state_ready.at(i, c))
                        nc.tensor.matmul(inter_bank[:, 0:VW], qs[:, cols], state[:, :], start=True, stop=True).then_inc(inter.sem, 1)
                    if c < C - 1:
                        pe.wait_ge(ktil_ready.sem, ktil_ready.at(i, 1))
                        nc.tensor.matmul(local_bank[:, 0:VW], ktil[:, c, :], v1[:, c, :], start=True, stop=True).then_inc(local.sem, 1)
                    pe.wait_ge(PT_ready.sem, PT_ready.at(i, c + 1))
                    if c < C - 1:
                        score(c + 1)
                    if c >= 2:
                        pe.wait_ge(tot_ready.sem, tot_ready.at(i, c - 1))
                    for h in range(H):
                        last = nc.tensor.matmul(intra_bank[c % 2][:, h * V1:(h + 1) * V1], PT[c % 2][:, h, :],
                                                v1[:, c, h * V1:(h + 1) * V1], start=True, stop=True)
                    last.then_inc(intra.sem, 1)

            def turn_h(i):
                pe.wait_ge(h_ready.sem, h_ready.at(i, 1))
                for k in range(KD):
                    for c in range(C):
                        last = nc.tensor.transpose(hT_bank[k][:, c * P:(c + 1) * P], hh[:, c, k * P:(k + 1) * P], ident[:, :])
                    last.then_inc(hT_t.sem, 1)

            def project_out(i):
                pe.wait_ge(hT_lo.sem, hT_lo.at(i, KD))
                for c in range(C):
                    for k in range(KD):
                        last = product(nc, out_bank[c // 2][:, c % 2 * D:(c % 2 + 1) * D], cut(hT, a, k, slice(c * P, (c + 1) * P)),
                                       cut(wo, a, k), k == 0 and c % 2 == 0, k == KD - 1)
                last.then_inc(x1_ready.sem, 1)

            def body(i, following):
                attend(i)
                if following is not None:
                    turn_y(following)
                    pe.wait_ge(tot_ready.sem, tot_ready.at(i, C))
                    project(following)
                    pe.wait_ge(tanhed.sem, tanhed.at(following, 2))
                turn_h(i)
                if following is not None:
                    output_gate(following)
                    pe.wait_ge(qk_in.sem, qk_in.at(following, 2))
                else:
                    pe.wait_ge(tot_ready.sem, tot_ready.at(i, C))
                project_out(i)
                if following is not None:
                    turn_gates(following)

            splitting.turn(pe)
            turn_y(0)
            project(0)
            output_gate(0)
            turn_gates(0)
            with pe.Fori(0, B - 1) as i:
                body(i, i + 1)
            body(B - 1, None)

        @block.scalar
        def _(act):
            def high_y(i):
                for k in range(KD):
                    act.wait_ge(yT_t.sem, yT_t.at(i, k + 1))
                    nc.scalar.activation(yT[0][:, k, :], bank[k][:, :], ACT.Copy, scale=g.norm1_col[:, k:k + 1]).then_inc(yT_hi.sem, 1)

            def gates_start(i):
                for n in range(2):
                    act.wait_ge(gates.sem, gates.at(i, n + 1))
                    nc.scalar.activation(row[n][:, :], gate_bank[n][0:H, :], ACT.Tanh, bias=g.gate_bias15[:, n:n + 1], scale=1.0 / CAP).then_inc(tanhed.sem, 1)
                act.wait_ge(tanhed.sem, tanhed.at(i, 2))
                nc.scalar.activation(row[2][:, :], row[1][:, :], ACT.Exp, scale=-CAP).then_inc(u_ready.sem, 1)

            def log_sigmoid(i):
                act.wait_ge(y1_ready.sem, y1_ready.at(i, 1))
                nc.scalar.activation(row[4][:, :], row[3][:, :], ACT.Ln).then_inc(ln_ready.sem, 1)
                act.wait_ge(ln_ready.sem, ln_ready.at(i, 1))
                nc.scalar.activation(row[5][:, :], row[4][:, :], ACT.Exp, scale=-1.0).then_inc(ln_ready.sem, 1)

            def copy_qk(i):
                act.wait_ge(qk.sem, qk.at(i, 1))
                nc.scalar.activation(qs[:, :], q_bank[:, :], ACT.Copy, scale=float(DQ) ** -0.5).then_inc(qk_in.sem, 1)
                act.wait_ge(qk.sem, qk.at(i, 2))
                nc.scalar.activation(kT[:, :], k_bank[:, :], ACT.Copy).then_inc(qk_in.sem, 1)

            def copy_kv(i):
                for c in range(C):
                    act.wait_ge(kv.sem, kv.at(i, c + 1))
                    nc.scalar.activation(ktok[:, c, :], kv_bank[c % 2][:, Kc], ACT.Copy).then_inc(kv_in.sem, 1)
                    nc.scalar.activation(per_head(v1[:, c, :])[:, :, 0:DV],
                                                  kv_bank[c % 2][:, Vc].rearrange("p (h e) -> p h e", e=DV), ACT.Copy).then_inc(kv_in.sem, 1)

            def copy_G(i):
                act.wait_ge(rows_ready.sem, rows_ready.at(i, 1))
                nc.scalar.activation(gr[QUADS[1]:QUADS[1] + H, :], row[7][:, :], ACT.Copy).then_inc(G_copied.sem, 1)

            def output_gate(i):
                for n in range(2):
                    act.wait_ge(og.sem, og.at(i, n + 1))
                    nc.scalar.activation(sig[:, 2 * n:2 * n + 2, :].rearrange("p c d -> p (c d)"), og_bank[n][:, :], ACT.Sigmoid).then_inc(og_in.sem, 1)

            def scales(i):
                act.wait_ge(tg_ready.sem, tg_ready.at(i, 1))
                nc.scalar.activation(tg[:, :, :], tg_bank[:, :].rearrange("p (c s) -> p c s", c=C)[:, :, 0:QUADS[2] + H], ACT.Copy).then_inc(tg_in.sem, 1)
                act.wait_ge(gend_ready.sem, gend_ready.at(i, 1))
                nc.scalar.activation(gend[:, :], gend_bank[:, 0:C], ACT.Copy).then_inc(tg_in.sem, 1)
                act.wait_ge(dec_ready.sem, dec_ready.at(i, 1))
                nc.scalar.activation(dexp[:, :], dec[:, :], ACT.Exp).then_inc(dexp_ready.sem, 1)
                act.wait_ge(ga_ready.sem, ga_ready.at(i, 1))
                nc.scalar.activation(ea[:, :, :, :].rearrange("p a c h -> p (a c h)"), ga_flat, ACT.Exp).then_inc(ea_ready.sem, 1)

            def weights(i):
                for c in range(C):
                    act.wait_ge(diff.sem, diff.at(i, c + 1))
                    w = pairw[c % 2][:, :, :].rearrange("p h s -> p (h s)")
                    nc.scalar.activation(w, w, ACT.Exp).then_inc(weight.sem, 1)
                    if c < C - 2:
                        act.wait_ge(scores.sem, scores.at(i, c + 1))
                        for h in range(H):
                            last = nc.scalar.activation(qbd[c % 2][:, h, :], qs[:, (c + 2) * P:(c + 3) * P], ACT.Copy,
                                                        scale=g.head_mask[:, h:h + 1])
                        last.then_inc(q_late.sem, 1)

            def inverse_root(i):
                act.wait_ge(ms_ready.sem, ms_ready.at(i, 1))
                nc.scalar.activation(den[3][:, :], den[2][:, :], ACT.Ln).then_inc(rs0.sem, 1)
                act.wait_ge(rs0.sem, rs0.at(i, 1))
                nc.scalar.activation(den[4][:, :], den[3][:, :], ACT.Exp, scale=-0.5).then_inc(rs0.sem, 1)

            def high_h(i):
                for k in range(KD):
                    act.wait_ge(hT_t.sem, hT_t.at(i, k + 1))
                    nc.scalar.activation(hT[0][:, k, :], hT_bank[k][:, :], ACT.Copy, scale=g.mh_col[:, k:k + 1]).then_inc(hT_hi.sem, 1)

            def body(i, following):
                weights(i)
                if following is None:
                    inverse_root(i)
                    high_h(i)
                    return
                high_y(following)
                gates_start(following)
                log_sigmoid(following)
                copy_qk(following)
                inverse_root(i)
                copy_kv(following)
                high_h(i)
                copy_G(following)
                output_gate(following)
                scales(following)

            splitting.split_high(act)
            high_y(0)
            gates_start(0)
            log_sigmoid(0)
            copy_qk(0)
            copy_kv(0)
            copy_G(0)
            output_gate(0)
            scales(0)
            with act.Fori(0, B - 1) as i:
                body(i, i + 1)
            body(B - 1, None)

        @block.gpsimd
        def _(pool):
            splitting.preset()
            with pool.Fori(0, B) as i:
                steps = Steps(pool_sem, i, C)
                pool.wait_ge(qk_in.sem, qk_in.at(i, 1))

                def spread_q(c):
                    nc.gpsimd.tensor_tensor(
                        out=qbd[c % 2][:, :, :], in0=qs[:, c * P:(c + 1) * P].unsqueeze(1).to_broadcast([P, H, P]),
                        in1=expand(g.head_mask[:, :], P), op=ALU.mult).then_inc(q_spread.sem, 1)

                def differ(c):
                    nc.gpsimd.tensor_tensor(out=pairw[c % 2][:, :, :], in0=expand(tg[:, c, 0:H], P),
                                                  in1=Gb[:, :, c * P:(c + 1) * P], op=ALU.subtract).then_inc(steps.sem, steps.one())
                    pool.wait_ge(steps.sem, steps.done())
                    nc.gpsimd.tensor_tensor(out=pairw[c % 2][:, :, :], in0=pairw[c % 2][:, :, :],
                                                    in1=g.causal[:, :].unsqueeze(1).to_broadcast([P, H, P]), op=ALU.add).then_inc(diff.sem, 1)

                spread_q(0)
                spread_q(1)
                pool.wait_ge(tg_in.sem, tg_in.at(i, 1))
                pool.wait_ge(spread.sem, spread.at(i, 16))
                differ(0)
                pool.wait_ge(ea_ready.sem, ea_ready.at(i, 1))
                nc.gpsimd.tensor_tensor(
                    out=ktil[:, :, :].rearrange("p c (h d) -> p (c h) d", d=DQ), in0=ktok[:, :, :].rearrange("p c (h d) -> p (c h) d", d=DQ),
                    in1=expand(ea[:, 0, :, :].rearrange("p c h -> p (c h)"), DQ), op=ALU.mult).then_inc(ktil_ready.sem, 1)
                differ(1)
                for c in (2, 3):
                    pool.wait_ge(PT_ready.sem, PT_ready.at(i, c - 1))
                    differ(c)

        @block.vector
        def _(dve):
            per = lambda t: t[:, :, :].rearrange("p c (h d) -> p (c h) d", d=DV)
            th = tot[:, :, :].rearrange("p c (h e) -> p (c h) e", e=V1)

            def scale_x(i, w):
                for c in range(C):
                    last = nc.vector.tensor_scalar(out=ys[:, c, :], in0=g.xnf[:, ds((i * C + c) * D, D)],
                                                   scalar1=g.scale_y[:, ds(i * C + c, 1)], scalar2=None, op0=ALU.mult)
                    if c < C - 1:
                        last.then_inc(w.sem, w.one())
                last.then_inc(y_ready.sem, 1)

            def low_y(i):
                for k in range(KD):
                    dve.wait_ge(yT_hi.sem, yT_hi.at(i, k + 1))
                    nc.vector.scalar_tensor_tensor(out=yT[1][:, k, :], in0=bank[k][:, :], scalar=g.norm1_col[:, k:k + 1],
                                                            in1=f32(yT[0][:, k, :]), op0=ALU.mult, op1=ALU.subtract).then_inc(yT_lo.sem, 1)

            def gates_start(i, w):
                dve.wait_ge(u_ready.sem, u_ready.at(i, 1))
                nc.vector.tensor_scalar(out=row[3][:, :], in0=row[2][:, :], scalar1=1.0, scalar2=None, op0=ALU.add).then_inc(y1_ready.sem, 1)
                dve.wait_ge(y1_ready.sem, y1_ready.at(i, 1))
                nc.vector.scalar_tensor_tensor(out=row[6][:, :], in0=row[3][:, :], scalar=1.0, in1=row[2][:, :], op0=ALU.subtract, op1=ALU.subtract).then_inc(w.sem, w.one())

            def gate_rows(i, w):
                dve.wait_ge(ln_ready.sem, ln_ready.at(i, 2))
                dve.wait_ge(w.sem, w.done())
                nc.vector.tensor_tensor(out=row[6][:, :], in0=row[6][:, :], in1=row[5][:, :], op=ALU.mult).then_inc(w.sem, w.one())
                dve.wait_ge(w.sem, w.done())
                nc.vector.tensor_tensor(out=row[6][:, :], in0=row[4][:, :], in1=row[6][:, :], op=ALU.subtract).then_inc(w.sem, w.one())
                dve.wait_ge(w.sem, w.done())
                nc.vector.tensor_tensor_scan(out=row[8][:, :], data0=g.ones_row[:, :], data1=row[6][:, :], initial=0.0, op0=ALU.mult, op1=ALU.add).then_inc(w.sem, w.one())
                dve.wait_ge(w.sem, w.done())
                nc.vector.scalar_tensor_tensor(out=gr[0:H, :], in0=row[0][:, :], scalar=CAP, in1=row[8][:, :], op0=ALU.mult, op1=ALU.add).then_inc(w.sem, w.one())
                dve.wait_ge(w.sem, w.done())
                nc.vector.tensor_tensor_scan(out=row[7][:, :], data0=gr[0:H, :], data1=gr[0:H, :], initial=-3e38, op0=ALU.max, op1=ALU.max).then_inc(rows_ready.sem, 1)
                dve.wait_ge(rows_ready.sem, rows_ready.at(i, 1))
                nc.vector.tensor_tensor(out=gr[QUADS[2]:QUADS[2] + H, :], in0=row[8][:, :], in1=row[7][:, :], op=ALU.subtract).then_inc(rows_ready.sem, 1)

            def scales(i, w):
                dve.wait_ge(tg_in.sem, tg_in.at(i, 2))
                nc.vector.tensor_tensor(out=dec[:, :], in0=gend[:, 0:C - 1], in1=gend[:, 1:C], op=ALU.subtract).then_inc(dec_ready.sem, 1)
                dve.wait_ge(spread.sem, spread.at(i, 16))
                ends = Gb[:, :, P - 1::P].rearrange("p h c -> p c h")
                nc.vector.tensor_tensor(out=ga[:, 0, :, :], in0=tg[:, :, 0:H], in1=ends, op=ALU.subtract).then_inc(w.sem, w.one())
                nc.vector.tensor_tensor(out=ga[:, 1, 1:C, :], in0=ends[:, 0:C - 1, :], in1=tg[:, 1:C, QUADS[1]:QUADS[1] + H], op=ALU.subtract).then_inc(w.sem, w.one())
                nc.vector.tensor_copy(ga[:, 2, :, :], tg[:, :, QUADS[2]:QUADS[2] + H]).then_inc(ga_ready.sem, 1)

            def attend(i, v):
                def add_up(c):
                    dve.wait_ge(intra.sem, intra.at(i, c + 1))
                    if c == 0:
                        nc.vector.tensor_copy(tot[:, 0, :], intra_bank[0][:, 0:VW]).then_inc(tot_ready.sem, 1)
                    else:
                        dve.wait_ge(v.sem, v.done())
                        nc.vector.tensor_tensor(out=tot[:, c, :], in0=intra_bank[c % 2][:, 0:VW], in1=tot[:, c, :], op=ALU.add).then_inc(tot_ready.sem, 1)

                dve.wait_ge(dexp_ready.sem, dexp_ready.at(i, 1))
                for c in range(C):
                    dve.wait_ge(scores.sem, scores.at(i, c + 1))
                    dve.wait_ge(weight.sem, weight.at(i, c + 1))
                    if c >= 2:
                        dve.wait_ge(intra.sem, intra.at(i, c - 1))
                    for n in range(2):
                        last = nc.vector.tensor_tensor(out=PT[c % 2][:, n * H // 2:(n + 1) * H // 2, :].rearrange("p h s -> p (h s)"),
                                                       in0=score_bank[n][:, :],
                                                       in1=pairw[c % 2][:, n * H // 2:(n + 1) * H // 2, :].rearrange("p h s -> p (h s)"), op=ALU.mult)
                        if n == 0:
                            last.then_inc(v.sem, v.one())
                    last.then_inc(PT_ready.sem, 1)
                    if c:
                        add_up(c - 1)
                        dve.wait_ge(inter.sem, inter.at(i, c))
                        nc.vector.tensor_tensor(out=per_head(tot[:, c, :]), in0=per_head(inter_bank[:, 0:VW]),
                                                  in1=expand(ea[:, 1, c, :], V1), op=ALU.mult).then_inc(v.sem, v.one())
                    if c < C - 1:
                        dve.wait_ge(local.sem, local.at(i, c + 1))
                        dst = state if c == 0 else part
                        last = nc.vector.tensor_tensor(out=per_head(dst[:, :]), in0=per_head(local_bank[:, 0:VW]),
                                                       in1=expand(g.head_mask[:, :], V1), op=ALU.mult)
                        if c == 0:
                            last.then_inc(state_ready.sem, 1)
                        else:
                            last.then_inc(v.sem, v.one())
                            dve.wait_ge(v.sem, v.done())
                            nc.vector.scalar_tensor_tensor(out=state[:, :], in0=state[:, :], scalar=dexp[:, c - 1:c],
                                                                          in1=part[:, :], op0=ALU.mult, op1=ALU.add).then_inc(state_ready.sem, 1)
                add_up(C - 1)

            def divide(i, v):
                dve.wait_ge(tot_ready.sem, tot_ready.at(i, C))
                nc.vector.scalar_tensor_tensor(out=den[0][:, :], in0=th[:, :, DV], scalar=-1.0, in1=th[:, :, DV], op0=ALU.mult, op1=ALU.max).then_inc(v.sem, v.one())
                dve.wait_ge(v.sem, v.done())
                nc.vector.tensor_tensor(out=den[1][:, :], in0=den[0][:, :], in1=ea[:, 2, :, :].rearrange("p c h -> p (c h)"), op=ALU.max).then_inc(v.sem, v.one())
                dve.wait_ge(v.sem, v.done())
                nc.vector.reciprocal(out=den[0][:, :], in_=den[1][:, :]).then_inc(v.sem, v.one())
                dve.wait_ge(v.sem, v.done())
                nc.vector.tensor_tensor(out=per(hh), in0=th[:, :, 0:DV], in1=expand(den[0][:, :], DV), op=ALU.mult).then_inc(v.sem, v.one())
                dve.wait_ge(v.sem, v.done())

            def mean_square(i, v):
                nc.vector.tensor_tensor(out=per(sq), in0=per(hh), in1=per(hh), op=ALU.mult).then_inc(v.sem, v.one())
                dve.wait_ge(v.sem, v.done())
                nc.vector.tensor_reduce(out=den[1][:, :], in_=per(sq), op=ALU.add, axis=AX.X).then_inc(v.sem, v.one())
                dve.wait_ge(v.sem, v.done())
                nc.vector.tensor_scalar(out=den[2][:, :], in0=den[1][:, :], scalar1=1.0 / DV, scalar2=1e-6, op0=ALU.mult, op1=ALU.add).then_inc(ms_ready.sem, 1)

            def norm(i, v):
                dve.wait_ge(rs0.sem, rs0.at(i, 2))
                nc.vector.tensor_tensor(out=den[5][:, :], in0=den[4][:, :], in1=den[4][:, :], op=ALU.mult).then_inc(v.sem, v.one())
                dve.wait_ge(v.sem, v.done())
                nc.vector.tensor_tensor(out=den[6][:, :], in0=den[5][:, :], in1=den[2][:, :], op=ALU.mult).then_inc(v.sem, v.one())
                dve.wait_ge(v.sem, v.done())
                nc.vector.tensor_scalar(out=den[5][:, :], in0=den[6][:, :], scalar1=-0.5, scalar2=1.5, op0=ALU.mult, op1=ALU.add).then_inc(v.sem, v.one())
                dve.wait_ge(v.sem, v.done())
                nc.vector.tensor_tensor(out=den[6][:, :], in0=den[5][:, :], in1=den[4][:, :], op=ALU.mult).then_inc(v.sem, v.one())
                dve.wait_ge(v.sem, v.done())
                nc.vector.tensor_tensor(out=per(sq), in0=per(hh), in1=expand(den[6][:, :], DV), op=ALU.mult).then_inc(v.sem, v.one())
                dve.wait_ge(v.sem, v.done())
                nc.vector.tensor_tensor(out=hh[:, :, :], in0=sq[:, :, :], in1=sig[:, :, :], op=ALU.mult).then_inc(h_ready.sem, 1)

            def low_h(i):
                for k in range(KD):
                    dve.wait_ge(hT_hi.sem, hT_hi.at(i, k + 1))
                    nc.vector.scalar_tensor_tensor(out=hT[1][:, k, :], in0=hT_bank[k][:, :], scalar=g.mh_col[:, k:k + 1],
                                                            in1=f32(hT[0][:, k, :]), op0=ALU.mult, op1=ALU.subtract).then_inc(hT_lo.sem, 1)

            def add(i, v):
                dve.wait_ge(x1_ready.sem, x1_ready.at(i, 1))
                for n in range(2):
                    at = g.xnf[:, ds(i * C * D + n * 2 * D, 2 * D)]
                    last = nc.vector.tensor_tensor(out=at, in0=out_bank[n][:, :], in1=at, op=ALU.add)
                    last.then_inc(v.sem, v.one())

            def body(i, following):
                v = Steps(dve_sem, i, NBODY)
                if following is None:
                    attend(i, v)
                    divide(i, v)
                    mean_square(i, v)
                    norm(i, v)
                    low_h(i)
                    add(i, v)
                    v.close("mlstm body")
                    return
                w = Steps(pre_sem, following, NPRE)
                scale_x(following, w)
                attend(i, v)
                low_y(following)
                divide(i, v)
                gates_start(following, w)
                mean_square(i, v)
                gate_rows(following, w)
                norm(i, v)
                low_h(i)
                add(i, v)
                scales(following, w)
                v.close("mlstm body")
                w.close("mlstm pre")

            w = Steps(pre_sem, 0, NPRE)
            scale_x(0, w)
            splitting.split_low(dve)
            low_y(0)
            gates_start(0, w)
            gate_rows(0, w)
            scales(0, w)
            with dve.Fori(0, B - 1) as i:
                body(i, i + 1)
            body(B - 1, None)


def mlp_phase(nc, g, raws, after):
    bank, ident = g.bank, g.ident
    a = slice(None)
    m = Map(nc, g.W0)
    wgu = m.pair("p_wgu", [P, KD, 2, FF])
    wd = m.pair("p_wd", [P, NF, D])
    rgu, rd, fetch = raws
    pieces = [Piece(wgu[0][:, k, n, :], wgu[1][:, k, n, :], raw=rgu[:, k, n, :]) for k in range(KD) for n in range(2)]
    pieces += [Piece(wd[0][:, n:n + 4, :], wd[1][:, n:n + 4, :], raw=rd[:, n:n + 4, :]) for n in (0, 4)]
    splitting = Weights(nc, g.sems, "mlp_w", bank, ident, fetch, [], pieces)

    junk, ys = m("p_junk", [P, D]), m("p_ys", [P, C, D])
    sq, ms, rs = m("p_sq", [P, C]), m("p_ms", [P, C]), m("p_rs", [P, C])
    yT = m.pair("p_yT", [P, KD, S])
    hid = Hidden(nc, g, "p", NF, 4, m)
    sg = g.counted
    squared, ms_ready, powed, y_ready = sg("p_sq", C), sg("p_ms", 1), sg("p_pow", 1), sg("p_y", 1)
    yT_t, yT_hi, yT_lo, added, acc_free = sg("p_yTt", KD), sg("p_yThi", KD), sg("p_yTlo", KD), sg("p_added", 1), sg("p_acc", 1, 1)
    norm_sem, sum_sem = g.sems("p_norm"), g.sems("p_sum")
    acc = [bank[6], bank[7]]
    gate, up = (lambda u: bank[0 if u % 2 == 0 else 2]), (lambda u: bank[1 if u % 2 == 0 else 3])
    turn_bank = [bank[4], bank[5]]
    block = nc.Block()
    with block:
        @block.sync
        def _(sp):
            sp.wait_ge(splitting.low, splitting.all)
            after.issue(sp, range(len(after.groups)))

        @block.tensor
        def _(pe):
            pe.sem_inc(hid.down.sem, hid.down.credit)

            def turn_y(i):
                pe.wait_ge(y_ready.sem, y_ready.at(i, 1))
                for k in range(KD):
                    for c in range(C):
                        last = nc.tensor.transpose(turn_bank[k][:, c * P:(c + 1) * P], ys[:, c, k * P:(k + 1) * P], ident[:, :])
                    last.then_inc(yT_t.sem, 1)

            def down(i, u):
                h = hid.unit(u)
                pe.wait_ge(hid.lo.sem, hid.lo.at(i, u + 1))
                if u == 0:
                    pe.wait_ge(splitting.low, splitting.all)
                    pe.wait_ge(acc_free.sem, acc_free.at(i, 0))
                for c in range(C):
                    last = product(nc, acc[c // 2][:, c % 2 * D:(c % 2 + 1) * D], cut(h, a, slice(c * P, (c + 1) * P)),
                                   cut(wd, a, u), u == 0 and c % 2 == 0, u == NF - 1)
                last.then_inc(hid.down.sem, 1)

            def body(i, following):
                pe.wait_ge(yT_lo.sem, yT_lo.at(i, KD))
                for u in range(NF):
                    pe.wait_ge(hid.hidden.sem, hid.hidden.at(i, u - 1))
                    for n, o in ((0, gate(u)), (1, up(u))):
                        for k in range(KD):
                            last = product(nc, o[:, :], cut(wgu, a, k, n, slice(u * P, (u + 1) * P)), cut(yT, a, k), k == 0, k == KD - 1)
                    last.then_inc(hid.gate_up.sem, 1)
                    if u >= 2:
                        down(i, u - 2)
                    if u == NF - 2 and following is not None:
                        turn_y(following)
                down(i, NF - 2)
                down(i, NF - 1)

            splitting.turn(pe, LATE)
            turn_y(0)
            with pe.Fori(0, B - 1) as i:
                body(i, i + 1)
            body(B - 1, None)

        @block.scalar
        def _(act):
            act.sem_inc(hid.hi.sem, hid.hi.credit)

            def squares(i, first=False):
                for c in range(C):
                    if c or not first:
                        act.wait_ge(squared.sem, squared.at(i, c))
                    nc.scalar.activation(junk[:, :], g.xnf[:, ds((i * C + c) * D, D)], ACT.Square,
                                         accum_out=sq[:, c:c + 1]).then_inc(squared.sem, 1)

            def high_y(i, first=False):
                if not first:
                    act.wait_ge(hid.gate_up.sem, hid.gate_up.at(i, 0))
                for k in range(KD):
                    act.wait_ge(yT_t.sem, yT_t.at(i, k + 1))
                    nc.scalar.activation(yT[0][:, k, :], turn_bank[k][:, :], ACT.Copy, scale=g.norm2_col[:, k:k + 1]).then_inc(yT_hi.sem, 1)

            def body(i, following):
                for u in range(NF):
                    hid.act_silu(act, i, u, gate(u)[:, :])
                    if u:
                        hid.act_hi(act, i, u - 1)
                    if u == 2 and following is not None:
                        squares(following)
                if following is not None:
                    high_y(following)
                hid.act_hi(act, i, NF - 1)

            squares(0, True)
            splitting.split_high(act, 0, -LATE)
            high_y(0, True)
            splitting.split_high(act, -LATE)
            with act.Fori(0, B - 1) as i:
                body(i, i + 1)
            body(B - 1, None)

        @block.gpsimd
        def _(pool):
            with pool.Fori(0, B) as i:
                pool.wait_ge(ms_ready.sem, ms_ready.at(i, 1))
                nc.gpsimd.tensor_tensor(out=rs[:, :], in0=ms[:, :], in1=g.minus_half[:, 0:C], op=ALU.pow).then_inc(powed.sem, 1)
                at = g.res[:, ds(i * C * D, C * D)]
                nc.gpsimd.tensor_tensor(out=at, in0=at, in1=g.xnf[:, ds(i * C * D, C * D)], op=ALU.add).then_inc(added.sem, 1)

        @block.vector
        def _(dve):
            dve.sem_inc(hid.hidden.sem, hid.hidden.credit)
            dve.sem_inc(hid.lo.sem, hid.lo.credit)
            dve.sem_inc(acc_free.sem, acc_free.credit)

            def mean_square(i):
                dve.wait_ge(squared.sem, squared.at(i, C))
                nc.vector.tensor_scalar(out=ms[:, :], in0=sq[:, :], scalar1=1.0 / D, scalar2=1e-6, op0=ALU.mult, op1=ALU.add).then_inc(ms_ready.sem, 1)

            def norm(i):
                dve.wait_ge(powed.sem, powed.at(i, 1))
                for c in range(C):
                    last = nc.vector.tensor_scalar(out=ys[:, c, :], in0=g.xnf[:, ds((i * C + c) * D, D)], scalar1=rs[:, c:c + 1],
                                                   scalar2=None, op0=ALU.mult)
                    last.then_inc(norm_sem if c < C - 1 else y_ready.sem, 1)

            def low_y(i, first=False):
                if not first:
                    dve.wait_ge(hid.gate_up.sem, hid.gate_up.at(i, 0))
                for k in range(KD):
                    dve.wait_ge(yT_hi.sem, yT_hi.at(i, k + 1))
                    nc.vector.scalar_tensor_tensor(out=yT[1][:, k, :], in0=turn_bank[k][:, :], scalar=g.norm2_col[:, k:k + 1],
                                                   in1=f32(yT[0][:, k, :]), op0=ALU.mult, op1=ALU.subtract).then_inc(yT_lo.sem, 1)

            def body(i, following):
                for u in range(NF):
                    hid.dve_hidden(dve, i, u, up(u)[:, :])
                    if u:
                        hid.dve_lo(dve, i, u - 1)
                    if u == 3 and following is not None:
                        mean_square(following)
                    if u == 4 and following is not None:
                        norm(following)
                if following is not None:
                    low_y(following)
                hid.dve_lo(dve, i, NF - 1)
                dve.wait_ge(added.sem, added.at(i, 1))
                dve.wait_ge(hid.down.sem, hid.down.at(i, NF))
                for n in range(2):
                    at = g.res[:, ds(i * C * D + n * 2 * D, 2 * D)]
                    last = nc.vector.tensor_tensor(out=at, in0=acc[n][:, :], in1=at, op=ALU.add)
                    last.then_inc(sum_sem if n == 0 else acc_free.sem, 1)

            mean_square(0)
            norm(0)
            splitting.split_low(dve, 0, -LATE)
            low_y(0, True)
            splitting.split_low(dve, -LATE)
            with dve.Fori(0, B - 1) as i:
                body(i, i + 1)
            body(B - 1, None)


def layer1_phase(nc, g, raws, out):
    bank, ident = g.bank, g.ident
    a = slice(None)
    bf16 = mybir.dt.bfloat16
    L = B
    GP = 4
    NG = NF // GP
    m = Map(nc, g.W0)
    wqv = m.pair("l_wqv", [P, KD, 3 * D])
    wo = m.pair("l_wo", [P, KD, D])
    wgu = m.pair("l_wgu", [P, KD, 2, GP, FF // GP])
    wd = m.pair("l_wd", [P, NG, GP, D])
    rq, ro, rgu, rd, fetch = raws
    pieces = []
    for k in range(KD):
        cols = slice(k * P, (k + 1) * P)
        pieces.append(Piece(wqv[0][:, k, 0:4 * P], wqv[1][:, k, 0:4 * P], turned=[rq[:, b, cols] for b in range(4)]))
        pieces.append(Piece(wqv[0][:, k, 4 * P:6 * P], wqv[1][:, k, 4 * P:6 * P], turned=[rq[:, b, cols] for b in (4, 5)]))
        pieces.append(Piece(wo[0][:, k, :], wo[1][:, k, :], turned=[ro[:, b, cols] for b in range(KD)]))
    for k in range(KD):
        for n in range(2):
            pieces.append(Piece(wgu[0][:, k, n], wgu[1][:, k, n], raw=rgu[:, k, n, :].rearrange("p (q j) -> p j q", j=GP)))
    pieces += [Piece(wd[0][:, n], wd[1][:, n], raw=rd[:, n]) for n in range(NG)]

    sc = m("l_sc", [P, L, L, H1])

    preset = g.sems("l_preset")
    splitting = Weights(nc, g.sems, "l_w", bank, ident, fetch, [], pieces)

    xs = m("l_xs", [P, L, D])
    o = m("l_o", [P, L, D])
    st, mv = m("l_st", [P, L, 6]), m("l_mv", [P, L, 2])
    tiny = [m(f"l_tiny{n}", [P, L]) for n in range(4)]
    vv, rstd = m("l_vv", [P, L]), m("l_rstd", [P, L])
    xT = m.pair("l_xT", [P, KD, S])
    oT = m.pair("l_oT", [P, KD, S])
    q3, k3, v3 = m("l_q", [P, L, D]), m("l_k", [P, L, D]), m("l_v", [P, L, D])
    prod = [m(f"l_prod{n}", [P, L * D]) for n in range(2)]
    e3 = m("l_e", [P, L, L, H1])
    mx, sm, rc = m("l_mx", [P, L, H1]), m("l_sm", [P, L, H1]), m("l_rc", [P, L, H1])
    sb = [m(f"l_s{n}", [P, S]) for n in range(2)]
    h = [[m(f"l_h{c}{j}", [P, S]) for j in range(GP)] for c in range(NG)]
    ab = [m(f"l_ab{j}", [P, S]) for j in range(GP)]
    half = lambda name: m(name, [P, S // 2])
    ge = {}
    for x, y in ((0, 1), (0, 2), (0, 3), (1, 2), (1, 3), (2, 3)):
        ge[x, y] = half(f"l_ge{x}{y}")[:, :].bitcast(bf16)
    votes = [half(f"l_votes{j}")[:, :].bitcast(bf16) for j in range(GP)]
    ring = [m.pair(f"l_ring{j}", [P, S]) for j in range(GP)]
    sg = g.counted
    stats, powed, x_ready = sg("l_stats", 1), sg("l_pow", 1), sg("l_x", 1)
    xT_t, xT_hi, xT_lo = sg("l_xTt", 2), sg("l_xThi", 2), sg("l_xTlo", 2)
    qkv, qk_in, v_in = sg("l_qkv", L), sg("l_qkin", 2 * L), sg("l_vin", L)
    prods, reduced, centred, exped, probs = sg("l_prods", L), sg("l_red", L), sg("l_cent", 1), sg("l_exp", 1), sg("l_probs", 1)
    weighted, summed = sg("l_weighted", L), sg("l_summed", L, 2)
    oT_t, oT_hi, oT_lo = sg("l_oTt", 2), sg("l_oThi", 2), sg("l_oTlo", 2)
    gate_up, silu, hidden, absed = sg("l_gu", NF), sg("l_silu", NF), sg("l_hid", NF, 2), sg("l_abs", NF)
    compared, voted, kept = sg("l_ge", 6 * NG, 1), sg("l_voted", NF, 1), sg("l_kept", NF, 1)
    hi, lo, down = sg("l_hi", NF), sg("l_lo", NF), sg("l_down", NF, GP)
    out_ready, stored = sg("l_out", 1, 1), sg("l_stored", 16)
    NPRE, NBODY = 13, 10
    pre_sem, dve_sem, pool_sem = g.sems("l_pre"), g.sems("l_dve"), g.sems("l_pool")
    acc, turn_bank = [bank[6], bank[7]], [bank[4], bank[5]]
    gate, up = (lambda u: bank[0 if u % 2 == 0 else 2]), (lambda u: bank[1 if u % 2 == 0 else 3])
    res4 = g.res.rearrange("p (l c d) -> p l c d", l=L, c=C)
    out4 = out.rearrange("l (c p) d -> p l c d", p=P)
    block = nc.Block()
    with block:
        @block.sync
        def _(sp):
            with sp.Fori(0, C) as i:
                sp.wait_ge(out_ready.sem, out_ready.at(i, 1))
                for l in range(L):
                    sp.dma_start(out4[:, l, ds(i, 1), :], res4[:, l, ds(i, 1), :]).then_inc(stored.sem, 16)
            sp.wait_ge(stored.sem, 16 * L * C)

        @block.tensor
        def _(pe):
            pe.sem_inc(down.sem, down.credit)

            def downs(i, c):
                for j in range(GP):
                    u = c * GP + j
                    pe.wait_ge(lo.sem, lo.at(i, u + 1))
                    for l in range(L):
                        last = product(nc, acc[l // 2][:, l % 2 * D:(l % 2 + 1) * D], cut(ring[j], a, slice(l * P, (l + 1) * P)),
                                       cut(wd, a, c, j), u == 0 and l % 2 == 0, u == NF - 1)
                    last.then_inc(down.sem, 1)

            def turn_x(i):
                pe.wait_ge(x_ready.sem, x_ready.at(i, 1))
                for k in range(KD):
                    for l in range(L):
                        last = nc.tensor.transpose(turn_bank[k][:, l * P:(l + 1) * P], xs[:, l, k * P:(k + 1) * P], ident[:, :])
                    last.then_inc(xT_t.sem, 1)

            def project(i):
                pe.wait_ge(xT_lo.sem, xT_lo.at(i, KD))
                for l in range(L):
                    for k in range(KD):
                        product(nc, bank[l][:, :], cut(xT, a, k, slice(l * P, (l + 1) * P)), cut(wqv, a, k, slice(0, 2 * D)), k == 0, k == KD - 1)
                    for k in range(KD):
                        last = product(nc, turn_bank[l // 2][:, l % 2 * D:(l % 2 + 1) * D], cut(xT, a, k, slice(l * P, (l + 1) * P)),
                                       cut(wqv, a, k, slice(2 * D, 3 * D)), k == 0 and l % 2 == 0, k == KD - 1)
                    last.then_inc(qkv.sem, 1)

            def units(i, u):
                if u < 2:
                    pe.wait_ge(qk_in.sem, qk_in.at(i, 4 * (u + 1)))
                else:
                    pe.wait_ge(hidden.sem, hidden.at(i, u - 1))
                for n, b in ((0, gate(u)), (1, up(u))):
                    for k in range(KD):
                        c, j = u // GP, u % GP
                        last = product(nc, b[:, :], cut(wgu, a, k, n, j, slice(c * P, (c + 1) * P)), cut(xT, a, k), k == 0, k == KD - 1)
                last.then_inc(gate_up.sem, 1)

            def attention_out(i):
                pe.wait_ge(summed.sem, summed.at(i, L))
                for k in range(KD):
                    for l in range(L):
                        last = nc.tensor.transpose(turn_bank[k][:, l * P:(l + 1) * P], o[:, l, k * P:(k + 1) * P], ident[:, :])
                    last.then_inc(oT_t.sem, 1)
                pe.wait_ge(oT_lo.sem, oT_lo.at(i, KD))
                for l in range(L):
                    for k in range(KD):
                        product(nc, acc[l // 2][:, l % 2 * D:(l % 2 + 1) * D], cut(oT, a, k, slice(l * P, (l + 1) * P)), cut(wo, a, k), False, False)

            def body(i, following):
                for u in range(2, NF):
                    units(i, u)
                if following is not None:
                    pe.wait_ge(v_in.sem, v_in.at(i, L))
                    turn_x(following)
                    pe.wait_ge(hidden.sem, hidden.at(i, NF))
                    project(following)
                pe.wait_ge(splitting.low, splitting.all)
                pe.wait_ge(out_ready.sem, out_ready.at(i, 0))
                downs(i, 0)
                if following is not None:
                    units(following, 0)
                    pe.wait_ge(v_in.sem, v_in.at(following, L))
                attention_out(i)
                if following is not None:
                    units(following, 1)
                downs(i, 1)

            splitting.turn(pe, LATE)
            turn_x(0)
            project(0)
            units(0, 0)
            units(0, 1)
            with pe.Fori(0, C - 1) as i:
                body(i, i + 1)
            body(C - 1, None)

        @block.scalar
        def _(act):

            def act_silu(i, u):
                act.wait_ge(gate_up.sem, gate_up.at(i, u + 1))
                act.wait_ge(hidden.sem, hidden.at(i, u - 1))
                nc.scalar.activation(sb[u % 2][:, :], gate(u)[:, :], ACT.Silu).then_inc(silu.sem, 1)

            def act_abs(i, u):
                act.wait_ge(hidden.sem, hidden.at(i, u + 1))
                act.wait_ge(compared.sem, compared.at(i, 6 * (u // GP)))
                nc.scalar.activation(ab[u % GP][:, :], h[u // GP][u % GP][:, :], ACT.Abs).then_inc(absed.sem, 1)

            def act_hi(i, u):
                act.wait_ge(kept.sem, kept.at(i, u + 1))
                act.wait_ge(down.sem, down.at(i, u + 1 - GP))
                nc.scalar.activation(ring[u % GP][0][:, :], h[u // GP][u % GP][:, :], ACT.Copy).then_inc(hi.sem, 1)

            def high_x(i):
                for k in range(KD):
                    act.wait_ge(xT_t.sem, xT_t.at(i, k + 1))
                    nc.scalar.activation(xT[0][:, k, :], turn_bank[k][:, :], ACT.Copy).then_inc(xT_hi.sem, 1)

            def copy_qk(i, first=False):
                if not first:
                    act.wait_ge(prods.sem, prods.at(i, 0))
                for l in range(L):
                    act.wait_ge(qkv.sem, qkv.at(i, l + 1))
                    nc.scalar.activation(q3[:, l, :], bank[l][:, 0:D], ACT.Copy, scale=float(DH1) ** -0.5).then_inc(qk_in.sem, 1)
                    nc.scalar.activation(k3[:, l, :], bank[l][:, D:2 * D], ACT.Copy).then_inc(qk_in.sem, 1)

            def copy_v(i, first=False):
                if not first:
                    act.wait_ge(weighted.sem, weighted.at(i, 0))
                for l in range(L):
                    nc.scalar.activation(v3[:, l, :], turn_bank[l // 2][:, l % 2 * D:(l % 2 + 1) * D], ACT.Copy).then_inc(v_in.sem, 1)

            def exponentials(i):
                act.wait_ge(centred.sem, centred.at(i, 1))
                nc.scalar.activation(e3[:, :, :, :].rearrange("p l m h -> p (l m h)"),
                                              e3[:, :, :, :].rearrange("p l m h -> p (l m h)"), ACT.Exp).then_inc(exped.sem, 1)

            def high_o(i):
                for k in range(KD):
                    act.wait_ge(oT_t.sem, oT_t.at(i, k + 1))
                    nc.scalar.activation(oT[0][:, k, :], turn_bank[k][:, :], ACT.Copy).then_inc(oT_hi.sem, 1)

            def body(i, following):
                act_silu(i, 0)
                act_silu(i, 1)
                for u in range(2, 6):
                    act_abs(i, u - 2)
                    act_silu(i, u)
                exponentials(i)
                act_silu(i, 6)
                act_silu(i, 7)
                if following is not None:
                    high_x(following)
                for j in range(GP):
                    act_abs(i, GP + j)
                for j in range(GP):
                    act_hi(i, j)
                if following is not None:
                    copy_qk(following)
                if following is not None:
                    copy_v(following)
                high_o(i)
                for j in range(GP):
                    act_hi(i, GP + j)

            splitting.split_high(act, 0, -LATE)
            high_x(0)
            splitting.split_high(act, -LATE)
            copy_qk(0, True)
            copy_v(0, True)
            with act.Fori(0, C - 1) as i:
                body(i, i + 1)
            body(C - 1, None)

        @block.gpsimd
        def _(pool):
            pool.sem_inc(voted.sem, voted.credit)
            nc.gpsimd.memset(sc[:, :, :, :].rearrange("p l m h -> p (l m h)"), -1e30).then_inc(preset, 1)

            def votes_of(i, c, steps):
                first = 6 * c
                for n, (x, y, z, f1, f2) in enumerate((((0, 1), (0, 2), (0, 3), ALU.add, ALU.add), ((1, 2), (1, 3), (0, 1), ALU.add, ALU.subtract),
                                                       ((0, 2), (1, 2), (2, 3), ALU.add, ALU.subtract), ((0, 3), (1, 3), (2, 3), ALU.add, ALU.add))):
                    pool.wait_ge(compared.sem, compared.at(i, first + 6))
                    pool.wait_ge(kept.sem, kept.at(i, c * GP))
                    nc.gpsimd.tensor_tensor(out=votes[n], in0=ge[x], in1=ge[y], op=f1).then_inc(steps.sem, steps.one())
                    pool.wait_ge(steps.sem, steps.done())
                    nc.gpsimd.tensor_tensor(out=votes[n], in0=votes[n], in1=ge[z], op=f2).then_inc(voted.sem, 1)

            def inverse_deviation(i):
                pool.wait_ge(stats.sem, stats.at(i, 1))
                nc.gpsimd.tensor_tensor(out=rstd[:, :], in0=vv[:, :], in1=g.minus_half[:, 0:L], op=ALU.pow).then_inc(powed.sem, 1)

            def body(i, following):
                steps = Steps(pool_sem, i, NF)
                for l in range(L):
                    pool.wait_ge(qk_in.sem, qk_in.at(i, 2 * (l + 1)))
                    if l >= 2:
                        pool.wait_ge(reduced.sem, reduced.at(i, l - 1))
                    else:
                        pool.wait_ge(summed.sem, summed.at(i, l - 1))
                    nc.gpsimd.tensor_tensor(out=prod[l % 2][:, 0:(l + 1) * D].rearrange("p (m e) -> p m e", e=D),
                                                     in0=q3[:, l, :].unsqueeze(1).to_broadcast([P, l + 1, D]), in1=k3[:, 0:l + 1, :], op=ALU.mult).then_inc(prods.sem, 1)
                if following is not None:
                    inverse_deviation(following)
                votes_of(i, 0, steps)
                pool.wait_ge(v_in.sem, v_in.at(i, L))
                pool.wait_ge(probs.sem, probs.at(i, 1))
                for l in range(L):
                    if l >= 2:
                        pool.wait_ge(summed.sem, summed.at(i, l - 1))
                    nc.gpsimd.tensor_tensor(
                        out=prod[l % 2][:, 0:(l + 1) * D].rearrange("p (x d) -> p x d", d=DH1),
                        in0=expand(e3[:, l, 0:l + 1, :].rearrange("p m h -> p (m h)"), DH1),
                        in1=v3[:, 0:l + 1, :].rearrange("p m (h d) -> p (m h) d", d=DH1), op=ALU.mult).then_inc(weighted.sem, 1)
                votes_of(i, 1, steps)

            inverse_deviation(0)
            with pool.Fori(0, C - 1) as i:
                body(i, i + 1)
            body(C - 1, None)

        @block.vector
        def _(dve):
            for x in (hidden, compared, kept, summed, out_ready):
                dve.sem_inc(x.sem, x.credit)
            dve.wait_ge(preset, 1)
            def statistics(i, w):
                for l in range(L):
                    nc.vector.bn_stats(out=st[:, l, :], in_=g.res[:, ds((l * C) * D + i * D, D)]).then_inc(w.sem, w.one())
                dve.wait_ge(w.sem, w.done())
                moments(nc, w, st, mv, tiny)
                nc.vector.tensor_scalar(out=vv[:, :], in0=mv[:, :, 1], scalar1=1e-5, scalar2=None, op0=ALU.add).then_inc(stats.sem, 1)

            def norm(i, w):
                dve.wait_ge(powed.sem, powed.at(i, 1))
                for l in range(L):
                    last = nc.vector.tensor_scalar(out=xs[:, l, :], in0=g.res[:, ds((l * C) * D + i * D, D)], scalar1=mv[:, l, 0:1],
                                                   scalar2=rstd[:, l:l + 1], op0=ALU.subtract, op1=ALU.mult)
                    if l < L - 1:
                        last.then_inc(w.sem, w.one())
                last.then_inc(x_ready.sem, 1)

            def low_x(i):
                for k in range(KD):
                    dve.wait_ge(xT_hi.sem, xT_hi.at(i, k + 1))
                    nc.vector.tensor_tensor(out=xT[1][:, k, :], in0=turn_bank[k][:, :], in1=f32(xT[0][:, k, :]), op=ALU.subtract).then_inc(xT_lo.sem, 1)


            def body(i, following):
                v = Steps(dve_sem, i, NBODY)
                w = Steps(pre_sem, following, NPRE)

                def times(u):
                    dve.wait_ge(silu.sem, silu.at(i, u + 1))
                    nc.vector.tensor_tensor(out=h[u // GP][u % GP][:, :], in0=sb[u % 2][:, :], in1=up(u)[:, :], op=ALU.mult).then_inc(hidden.sem, 1)

                def reduce_scores(l):
                    dve.wait_ge(prods.sem, prods.at(i, l + 1))
                    nc.vector.tensor_reduce(out=sc[:, l, 0:l + 1, :].rearrange("p m h -> p (m h)"),
                                                       in_=prod[l % 2][:, 0:(l + 1) * D].rearrange("p (x d) -> p x d", d=DH1), op=ALU.add, axis=AX.X).then_inc(reduced.sem, 1)

                def compare(c, x, y):
                    dve.wait_ge(absed.sem, absed.at(i, c * GP + GP))
                    dve.wait_ge(voted.sem, voted.at(i, c * GP))
                    nc.vector.tensor_tensor(out=ge[x, y], in0=ab[x][:, :], in1=ab[y][:, :], op=ALU.is_ge).then_inc(compared.sem, 1)

                def keep(c, j):
                    least, how = ((2.0, ALU.is_ge), (1.0, ALU.is_ge), (0.0, ALU.is_le), (1.0, ALU.is_le))[j]
                    dve.wait_ge(voted.sem, voted.at(i, c * GP + j + 1))
                    x = h[c][j][:, :]
                    nc.vector.scalar_tensor_tensor(out=x, in0=votes[j], scalar=least, in1=x, op0=how, op1=ALU.mult).then_inc(kept.sem, 1)

                def low(c, j):
                    dve.wait_ge(hi.sem, hi.at(i, c * GP + j + 1))
                    nc.vector.tensor_tensor(out=ring[j][1][:, :], in0=h[c][j][:, :], in1=f32(ring[j][0][:, :]), op=ALU.subtract).then_inc(lo.sem, 1)

                def by_head(t):
                    return t[:, :, :, :].rearrange("p l m h -> p l h m")

                for u in (0, 1, 2):
                    times(u)
                reduce_scores(0)
                reduce_scores(1)
                times(3)
                if following is not None:
                    statistics(following, w)
                reduce_scores(2)
                reduce_scores(3)
                times(4)
                dve.wait_ge(reduced.sem, reduced.at(i, L))
                nc.vector.tensor_reduce(out=mx[:, :, :], in_=by_head(sc), op=ALU.max, axis=AX.X).then_inc(v.sem, v.one())
                dve.wait_ge(v.sem, v.done())
                last = None
                for l in range(L):
                    last = nc.vector.tensor_tensor(out=e3[:, l, :, :], in0=sc[:, l, :, :], in1=mx[:, l, :].unsqueeze(1).to_broadcast([P, L, H1]), op=ALU.subtract)
                    if l < L - 1:
                        last.then_inc(v.sem, v.one())
                last.then_inc(centred.sem, 1)
                times(5)
                for x, y in ((0, 1), (0, 2), (0, 3), (1, 2)):
                    compare(0, x, y)
                dve.wait_ge(exped.sem, exped.at(i, 1))
                nc.vector.tensor_reduce(out=sm[:, :, :], in_=by_head(e3), op=ALU.add, axis=AX.X).then_inc(v.sem, v.one())
                dve.wait_ge(v.sem, v.done())
                nc.vector.reciprocal(out=rc[:, :, :].rearrange("p l h -> p (l h)"), in_=sm[:, :, :].rearrange("p l h -> p (l h)")).then_inc(v.sem, v.one())
                compare(0, 1, 3)
                compare(0, 2, 3)
                dve.wait_ge(v.sem, v.done())
                for l in range(L):
                    last = nc.vector.tensor_tensor(out=e3[:, l, :, :], in0=e3[:, l, :, :], in1=rc[:, l, :].unsqueeze(1).to_broadcast([P, L, H1]), op=ALU.mult)
                    if l < L - 1:
                        last.then_inc(v.sem, v.one())
                last.then_inc(probs.sem, 1)
                times(6)
                if following is not None:
                    norm(following, w)
                times(7)
                if following is not None:
                    low_x(following)
                for j in range(GP):
                    keep(0, j)
                for x, y in ge:
                    compare(1, x, y)
                for j in range(GP):
                    low(0, j)
                for l in range(L):
                    dve.wait_ge(weighted.sem, weighted.at(i, l + 1))
                    nc.vector.tensor_reduce(out=o[:, l, :], in_=prod[l % 2][:, 0:(l + 1) * D].rearrange("p (m e) -> p e m", e=D),
                                                      op=ALU.add, axis=AX.X).then_inc(summed.sem, 1)
                for k in range(KD):
                    dve.wait_ge(oT_hi.sem, oT_hi.at(i, k + 1))
                    nc.vector.tensor_tensor(out=oT[1][:, k, :], in0=turn_bank[k][:, :], in1=f32(oT[0][:, k, :]), op=ALU.subtract).then_inc(oT_lo.sem, 1)
                for j in range(GP):
                    keep(1, j)
                for j in range(GP):
                    low(1, j)
                dve.wait_ge(down.sem, down.at(i, NF))
                for n in range(2):
                    at = res4[:, 2 * n:2 * n + 2, ds(i, 1), :].rearrange("p l c d -> p l (c d)")
                    last = nc.vector.tensor_tensor(out=at, in0=acc[n][:, :].rearrange("p (l d) -> p l d", d=D), in1=at, op=ALU.add)
                    if n == 0:
                        last.then_inc(v.sem, v.one())
                last.then_inc(out_ready.sem, 1)
                v.close("layer1 body")
                if following is not None:
                    w.close("layer1 pre")

            w = Steps(pre_sem, 0, NPRE)
            statistics(0, w)
            norm(0, w)
            splitting.split_low(dve, 0, -LATE)
            low_x(0)
            splitting.split_low(dve, -LATE)
            with dve.Fori(0, C - 1) as i:
                body(i, i + 1)
            body(C - 1, None)


NAMES = ["L0_attn_x", "L0_attn_norm1_w", "L0_attn_wq", "L0_attn_wk", "L0_attn_wv", "L0_attn_w_ig", "L0_attn_b_ig",
         "L0_attn_w_fg", "L0_attn_b_fg", "L0_attn_w_og", "L0_attn_mh_w", "L0_attn_w_out", "L0_attn_norm2_w",
         "L0_attn_w_gate", "L0_attn_w_up", "L0_attn_w_down", "L0_ffn_Wg", "L0_ffn_Wu", "L0_ffn_Wd", "L0_ffn_Wr",
         "L0_ffn_Ag", "L0_ffn_Bg", "L0_ffn_Au", "L0_ffn_Bu", "L0_ffn_Ad", "L0_ffn_Bd", "L1_attn_weight_qkv",
         "L1_attn_weight_out", "L1_ffn_w_gate", "L1_ffn_w_up", "L1_ffn_w_down"]


def kernel(**inputs):
    import numpy as _np
    import concourse.bacc as _bacc
    from concourse.bass_utils import run_bass_kernel_spmd as _run

    nc = _bacc.Bacc("TRN2", target_bir_lowering=False, num_devices=1)
    arrays, args = {}, []
    for name in NAMES:
        a = _np.ascontiguousarray(inputs[name])
        arrays[f"in_{name}"] = a
        args.append(nc.dram_tensor(f"in_{name}", a.shape, mybir.dt.from_np(a.dtype), kind="ExternalInput").ap())
    out = nc.dram_tensor("out_x", (B, S, D), fp32, kind="ExternalOutput").ap()
    program(nc, *args, out)
    return _run(nc, [arrays], core_ids=[0]).results[0]["out_x"]
```
